# Optimizing a Trainium2 kernel written in Bass

```python
import numpy as np
import jax
import jax.numpy as jnp

def _softmax(x, axis=-1):
    return jax.nn.softmax(x, axis=axis)

def _gelu(x):
    return jax.nn.gelu(x, approximate=True)

def _silu(x):
    return jax.nn.silu(x)

def _sigmoid(x):
    return jax.nn.sigmoid(x)

def _layernorm(x, axis=-1, eps=1e-05):
    m = jnp.mean(x, axis=axis, keepdims=True)
    v = jnp.var(x, axis=axis, keepdims=True)
    return (x - m) / jnp.sqrt(v + eps)

def _scatter_add(tgt, idx, src, axis=0):
    return tgt.at[idx].add(src)

def _segment_sum(src, seg, n):
    return jax.ops.segment_sum(src, seg, n)
kernel_name = 'mk_prb_d2_jaxref_r4_3fca08'

def setup_inputs(seed: int=0):
    np.random.seed(seed)
    _w = jnp.asarray

    def _L0_attn_setup():
        import jax, jax.numpy as jnp
        import numpy as np
        EMBED = 512
        HEADS = 16
        HEAD_DIM = EMBED // HEADS
        CHUNK = 128
        BASE = 10000.0
        EPS = 1e-06

        def _alibi_log_decay(h):
            slopes = 2.0 ** (-8.0 * (jnp.arange(h, dtype=jnp.float32) + 1.0) / h)
            return -slopes

        def _lrpe_rotate(x):
            b, n, h, d = x.shape
            half = d // 2
            theta = BASE ** (-2.0 * jnp.arange(half, dtype=jnp.float32) / d)
            ang = jnp.arange(n, dtype=jnp.float32)[:, None] * theta[None, :]
            cos = jnp.cos(ang)[None, :, None, :]
            sin = jnp.sin(ang)[None, :, None, :]
            x1, x2 = (x[..., :half], x[..., half:])
            return jnp.concatenate([x1 * cos - x2 * sin, x1 * sin + x2 * cos], axis=-1)

        def _lightning_attn(q, k, v, log_lam):
            b, n, h, d = q.shape
            C = CHUNK
            nc = n // C
            qc = q.reshape(b, nc, C, h, d).transpose(1, 0, 2, 3, 4)
            kc = k.reshape(b, nc, C, h, d).transpose(1, 0, 2, 3, 4)
            vc = v.reshape(b, nc, C, h, d).transpose(1, 0, 2, 3, 4)
            i = jnp.arange(C, dtype=jnp.float32)
            diff = i[:, None] - i[None, :]
            D = jnp.where(diff[None] >= 0, jnp.exp(log_lam[:, None, None] * diff[None]), 0.0)
            decay_q = jnp.exp(log_lam[None, :] * (i[:, None] + 1.0))
            decay_k = jnp.exp(log_lam[None, :] * (C - 1.0 - i[:, None]))
            lam_C = jnp.exp(log_lam * C)

            def step(S, qkv):
                qi, ki, vi = qkv
                scores = jnp.einsum('bthd,bshd->bhts', qi, ki) * D[None]
                o_intra = jnp.einsum('bhts,bshd->bthd', scores, vi)
                o_inter = jnp.einsum('bthd,bhde->bthe', qi * decay_q[None, :, :, None], S)
                S_new = lam_C[None, :, None, None] * S + jnp.einsum('bshd,bshe->bhde', ki * decay_k[None, :, :, None], vi)
                return (S_new, o_intra + o_inter)
            S0 = jnp.zeros((b, h, d, d), q.dtype)
            _, o = jax.lax.scan(step, S0, (qc, kc, vc))
            return o.transpose(1, 0, 2, 3, 4).reshape(b, n, h, d)

        def _gated_group_rmsnorm(o, gate, weight):
            b, n, d = o.shape
            x = o * jax.nn.sigmoid(gate)
            xg = x.reshape(b, n, HEADS, HEAD_DIM)
            ms = jnp.mean(xg * xg, axis=-1, keepdims=True)
            xg = xg * jax.lax.rsqrt(ms + EPS)
            return xg.reshape(b, n, d) * weight
        key = jax.random.key(seed)
        ks = jax.random.split(key, 8)
        b, n, d = (2, 512, EMBED)
        std = 0.02
        return {'x': jax.random.normal(ks[0], (b, n, d), jnp.float32), 'Wq': jax.random.normal(ks[1], (d, d), jnp.float32) * std, 'Wk': jax.random.normal(ks[2], (d, d), jnp.float32) * std, 'Wv': jax.random.normal(ks[3], (d, d), jnp.float32) * std, 'Wo': jax.random.normal(ks[4], (d, d), jnp.float32) * std, 'Wg1': jax.random.normal(ks[5], (d, HEAD_DIM), jnp.float32) * std, 'Wg2': jax.random.normal(ks[6], (HEAD_DIM, d), jnp.float32) * std, 'norm_weight': jnp.ones((d,), jnp.float32)}
    _L0_attn_in = _L0_attn_setup()

    def _L0_ffn_setup():
        import jax, jax.numpy as jnp
        import numpy as np
        _FP4_LUT = jnp.array([0.0, 0.5, 1.0, 1.5, 2.0, 3.0, 4.0, 6.0, -0.0, -0.5, -1.0, -1.5, -2.0, -3.0, -4.0, -6.0], dtype=jnp.float32)
        GROUP_SIZE = 128
        EPS = 1e-06

        def _dequant_fp4(packed_i32, scales_f16, group_size):
            out_f, in_p = packed_i32.shape
            w = packed_i32.astype(jnp.uint32)
            shifts = jnp.arange(8, dtype=jnp.uint32) * 4
            nib = w[:, :, None] >> shifts & jnp.uint32(15)
            vals = _FP4_LUT[nib.astype(jnp.int32)].reshape(out_f, in_p * 8)
            s = scales_f16.astype(jnp.float32).T
            s_full = jnp.repeat(s, group_size, axis=1)
            return vals * s_full
        key = jax.random.key(seed)
        k1, k2, k3, k4, k5 = jax.random.split(key, 5)
        B, S, H, I = (4, 512, 512, 1408)
        x = jax.random.normal(k1, (B, S, H), dtype=jnp.float32)
        gate_up_packed = jax.random.randint(k2, (2 * I, H // 8), 0, 2147483647, dtype=jnp.int32)
        gate_up_scales = jax.random.uniform(k3, (H // GROUP_SIZE, 2 * I), dtype=jnp.float32).astype(jnp.float16)
        down_packed = jax.random.randint(k4, (H, I // 8), 0, 2147483647, dtype=jnp.int32)
        down_scales = jax.random.uniform(k5, (I // GROUP_SIZE, H), dtype=jnp.float32).astype(jnp.float16)
        return {'x': x, 'gate_up_packed': gate_up_packed, 'gate_up_scales': gate_up_scales, 'down_packed': down_packed, 'down_scales': down_scales}
    _L0_ffn_in = _L0_ffn_setup()

    def _L1_attn_setup():
        import jax, jax.numpy as jnp
        import numpy as np
        B_, S, H = (2, 512, 512)
        E = 2 * H
        P = 64
        NH = E // P
        N = 64
        G = 1
        K = 4
        CS = 64
        CONV_DIM = E + 2 * G * N
        PROJ = E + CONV_DIM + NH
        EPS = 1e-06

        def segment_sum(a):
            l = a.shape[-1]
            a_exp = jnp.broadcast_to(a[..., None], (*a.shape, l))
            a_exp = jnp.where(jnp.tril(jnp.ones((l, l), bool), -1), a_exp, 0.0)
            s = jnp.cumsum(a_exp, axis=-2)
            return jnp.where(jnp.tril(jnp.ones((l, l), bool), 0), s, -jnp.inf)
        key = jax.random.key(seed)
        ks = jax.random.split(key, 8)
        s = 0.02
        return {'x': jax.random.normal(ks[0], (B_, S, H), jnp.float32), 'in_proj_w': jax.random.normal(ks[1], (PROJ, H), jnp.float32) * s, 'conv_w': jax.random.normal(ks[2], (CONV_DIM, K), jnp.float32) * s, 'conv_b': jnp.zeros((CONV_DIM,), jnp.float32), 'dt_bias': jax.random.uniform(ks[3], (NH,), jnp.float32, 0.0, 1.0), 'A_log': jnp.log(jax.random.uniform(ks[4], (NH,), jnp.float32, 1.0, 16.0)), 'D': jnp.ones((NH,), jnp.float32), 'norm_w': jnp.ones((E,), jnp.float32), 'out_proj_w': jax.random.normal(ks[5], (H, E), jnp.float32) * s}
    _L1_attn_in = _L1_attn_setup()

    def _L1_ffn_setup():
        import jax, jax.numpy as jnp
        import numpy as np
        B, T, C = (2, 256, 512)
        E, TOPK = (8, 2)
        F_MOE = 352
        F_SHARED = 1408
        key = jax.random.key(seed)
        ks = jax.random.split(key, 9)
        s = 0.02
        return {'x': jax.random.normal(ks[0], (B, T, C), dtype=jnp.float32), 'gate_w': jax.random.normal(ks[1], (E, C), dtype=jnp.float32) * s, 'expert_fc1': jax.random.normal(ks[2], (E, F_MOE, C), dtype=jnp.float32) * s, 'expert_fc2': jax.random.normal(ks[3], (E, F_MOE, C), dtype=jnp.float32) * s, 'expert_proj': jax.random.normal(ks[4], (E, C, F_MOE), dtype=jnp.float32) * s, 'shared_fc1': jax.random.normal(ks[5], (F_SHARED, C), dtype=jnp.float32) * s, 'shared_fc2': jax.random.normal(ks[6], (F_SHARED, C), dtype=jnp.float32) * s, 'shared_proj': jax.random.normal(ks[7], (C, F_SHARED), dtype=jnp.float32) * s, 'shared_gate_w': jax.random.normal(ks[8], (1, C), dtype=jnp.float32) * s}
    _L1_ffn_in = _L1_ffn_setup()
    _d = {'L0_attn_x': _L0_attn_in['x'], 'L0_attn_Wq': _L0_attn_in['Wq'], 'L0_attn_Wk': _L0_attn_in['Wk'], 'L0_attn_Wv': _L0_attn_in['Wv'], 'L0_attn_Wo': _L0_attn_in['Wo'], 'L0_attn_Wg1': _L0_attn_in['Wg1'], 'L0_attn_Wg2': _L0_attn_in['Wg2'], 'L0_attn_norm_weight': _L0_attn_in['norm_weight'], 'L0_ffn_gate_up_packed': _L0_ffn_in['gate_up_packed'], 'L0_ffn_gate_up_scales': _L0_ffn_in['gate_up_scales'], 'L0_ffn_down_packed': _L0_ffn_in['down_packed'], 'L0_ffn_down_scales': _L0_ffn_in['down_scales'], 'L1_attn_in_proj_w': _L1_attn_in['in_proj_w'], 'L1_attn_conv_w': _L1_attn_in['conv_w'], 'L1_attn_conv_b': _L1_attn_in['conv_b'], 'L1_attn_dt_bias': _L1_attn_in['dt_bias'], 'L1_attn_A_log': _L1_attn_in['A_log'], 'L1_attn_D': _L1_attn_in['D'], 'L1_attn_norm_w': _L1_attn_in['norm_w'], 'L1_attn_out_proj_w': _L1_attn_in['out_proj_w'], 'L1_ffn_gate_w': _L1_ffn_in['gate_w'], 'L1_ffn_expert_fc1': _L1_ffn_in['expert_fc1'], 'L1_ffn_expert_fc2': _L1_ffn_in['expert_fc2'], 'L1_ffn_expert_proj': _L1_ffn_in['expert_proj'], 'L1_ffn_shared_fc1': _L1_ffn_in['shared_fc1'], 'L1_ffn_shared_fc2': _L1_ffn_in['shared_fc2'], 'L1_ffn_shared_proj': _L1_ffn_in['shared_proj'], 'L1_ffn_shared_gate_w': _L1_ffn_in['shared_gate_w']}
    _x0 = _d['L0_attn_x']
    _d['L0_attn_x'] = jax.random.normal(jax.random.fold_in(jax.random.key(seed), 1), (4, 512, 512), dtype=_x0.dtype)
    del _x0
    return _d

def reference(L0_attn_x, L0_attn_Wq, L0_attn_Wk, L0_attn_Wv, L0_attn_Wo, L0_attn_Wg1, L0_attn_Wg2, L0_attn_norm_weight, L0_ffn_gate_up_packed, L0_ffn_gate_up_scales, L0_ffn_down_packed, L0_ffn_down_scales, L1_attn_in_proj_w, L1_attn_conv_w, L1_attn_conv_b, L1_attn_dt_bias, L1_attn_A_log, L1_attn_D, L1_attn_norm_w, L1_attn_out_proj_w, L1_ffn_gate_w, L1_ffn_expert_fc1, L1_ffn_expert_fc2, L1_ffn_expert_proj, L1_ffn_shared_fc1, L1_ffn_shared_fc2, L1_ffn_shared_proj, L1_ffn_shared_gate_w):

    def _L0_attn_ref(x, Wq, Wk, Wv, Wo, Wg1, Wg2, norm_weight):
        import jax, jax.numpy as jnp
        import numpy as np
        EMBED = 512
        HEADS = 16
        HEAD_DIM = EMBED // HEADS
        CHUNK = 128
        BASE = 10000.0
        EPS = 1e-06

        def _alibi_log_decay(h):
            slopes = 2.0 ** (-8.0 * (jnp.arange(h, dtype=jnp.float32) + 1.0) / h)
            return -slopes

        def _lrpe_rotate(x):
            b, n, h, d = x.shape
            half = d // 2
            theta = BASE ** (-2.0 * jnp.arange(half, dtype=jnp.float32) / d)
            ang = jnp.arange(n, dtype=jnp.float32)[:, None] * theta[None, :]
            cos = jnp.cos(ang)[None, :, None, :]
            sin = jnp.sin(ang)[None, :, None, :]
            x1, x2 = (x[..., :half], x[..., half:])
            return jnp.concatenate([x1 * cos - x2 * sin, x1 * sin + x2 * cos], axis=-1)

        def _lightning_attn(q, k, v, log_lam):
            b, n, h, d = q.shape
            C = CHUNK
            nc = n // C
            qc = q.reshape(b, nc, C, h, d).transpose(1, 0, 2, 3, 4)
            kc = k.reshape(b, nc, C, h, d).transpose(1, 0, 2, 3, 4)
            vc = v.reshape(b, nc, C, h, d).transpose(1, 0, 2, 3, 4)
            i = jnp.arange(C, dtype=jnp.float32)
            diff = i[:, None] - i[None, :]
            D = jnp.where(diff[None] >= 0, jnp.exp(log_lam[:, None, None] * diff[None]), 0.0)
            decay_q = jnp.exp(log_lam[None, :] * (i[:, None] + 1.0))
            decay_k = jnp.exp(log_lam[None, :] * (C - 1.0 - i[:, None]))
            lam_C = jnp.exp(log_lam * C)

            def step(S, qkv):
                qi, ki, vi = qkv
                scores = jnp.einsum('bthd,bshd->bhts', qi, ki) * D[None]
                o_intra = jnp.einsum('bhts,bshd->bthd', scores, vi)
                o_inter = jnp.einsum('bthd,bhde->bthe', qi * decay_q[None, :, :, None], S)
                S_new = lam_C[None, :, None, None] * S + jnp.einsum('bshd,bshe->bhde', ki * decay_k[None, :, :, None], vi)
                return (S_new, o_intra + o_inter)
            S0 = jnp.zeros((b, h, d, d), q.dtype)
            _, o = jax.lax.scan(step, S0, (qc, kc, vc))
            return o.transpose(1, 0, 2, 3, 4).reshape(b, n, h, d)

        def _gated_group_rmsnorm(o, gate, weight):
            b, n, d = o.shape
            x = o * jax.nn.sigmoid(gate)
            xg = x.reshape(b, n, HEADS, HEAD_DIM)
            ms = jnp.mean(xg * xg, axis=-1, keepdims=True)
            xg = xg * jax.lax.rsqrt(ms + EPS)
            return xg.reshape(b, n, d) * weight
        b, n, d = x.shape
        q = (x @ Wq).reshape(b, n, HEADS, HEAD_DIM)
        k = (x @ Wk).reshape(b, n, HEADS, HEAD_DIM)
        v = (x @ Wv).reshape(b, n, HEADS, HEAD_DIM)
        q = jax.nn.silu(q)
        k = jax.nn.silu(k)
        q = _lrpe_rotate(q)
        k = _lrpe_rotate(k)
        log_lam = _alibi_log_decay(HEADS)
        o = _lightning_attn(q, k, v, log_lam).reshape(b, n, d)
        gate = x @ Wg1 @ Wg2
        o = _gated_group_rmsnorm(o, gate, norm_weight)
        return o @ Wo

    def _L0_ffn_ref(x, gate_up_packed, gate_up_scales, down_packed, down_scales):
        import jax, jax.numpy as jnp
        import numpy as np
        _FP4_LUT = jnp.array([0.0, 0.5, 1.0, 1.5, 2.0, 3.0, 4.0, 6.0, -0.0, -0.5, -1.0, -1.5, -2.0, -3.0, -4.0, -6.0], dtype=jnp.float32)
        GROUP_SIZE = 128
        EPS = 1e-06

        def _dequant_fp4(packed_i32, scales_f16, group_size):
            out_f, in_p = packed_i32.shape
            w = packed_i32.astype(jnp.uint32)
            shifts = jnp.arange(8, dtype=jnp.uint32) * 4
            nib = w[:, :, None] >> shifts & jnp.uint32(15)
            vals = _FP4_LUT[nib.astype(jnp.int32)].reshape(out_f, in_p * 8)
            s = scales_f16.astype(jnp.float32).T
            s_full = jnp.repeat(s, group_size, axis=1)
            return vals * s_full
        I = gate_up_packed.shape[0] // 2
        w_gu = _dequant_fp4(gate_up_packed, gate_up_scales, GROUP_SIZE)
        w_down = _dequant_fp4(down_packed, down_scales, GROUP_SIZE)
        gate_up = jnp.einsum('bsh,oh->bso', x, w_gu)
        gate, up = (gate_up[..., :I], gate_up[..., I:])
        h = jax.nn.silu(gate) * up
        y = jnp.einsum('bsi,hi->bsh', h, w_down)
        rms = jnp.sqrt(jnp.mean(y * y, axis=-1, keepdims=True) + EPS)
        return y / rms

    def _L1_attn_ref(x, in_proj_w, conv_w, conv_b, dt_bias, A_log, D, norm_w, out_proj_w):
        import jax, jax.numpy as jnp
        import numpy as np
        B_, S, H = (2, 512, 512)
        E = 2 * H
        P = 64
        NH = E // P
        N = 64
        G = 1
        K = 4
        CS = 64
        CONV_DIM = E + 2 * G * N
        PROJ = E + CONV_DIM + NH
        EPS = 1e-06

        def segment_sum(a):
            l = a.shape[-1]
            a_exp = jnp.broadcast_to(a[..., None], (*a.shape, l))
            a_exp = jnp.where(jnp.tril(jnp.ones((l, l), bool), -1), a_exp, 0.0)
            s = jnp.cumsum(a_exp, axis=-2)
            return jnp.where(jnp.tril(jnp.ones((l, l), bool), 0), s, -jnp.inf)
        b, s, _ = x.shape
        proj = x @ in_proj_w.T
        gate, hBC, dt = jnp.split(proj, [E, E + CONV_DIM], axis=-1)
        xp = jnp.pad(hBC, ((0, 0), (K - 1, 0), (0, 0)))
        conv = sum((xp[:, k:k + s, :] * conv_w[:, k] for k in range(K))) + conv_b
        hBC = jax.nn.silu(conv)
        h, Bm, Cm = jnp.split(hBC, [E, E + G * N], axis=-1)
        dt = jax.nn.softplus(dt + dt_bias)
        A = -jnp.exp(A_log)
        h = h.reshape(b, s, NH, P)
        Bm = jnp.tile(Bm.reshape(b, s, G, N), (1, 1, NH // G, 1))
        Cm = jnp.tile(Cm.reshape(b, s, G, N), (1, 1, NH // G, 1))
        pad = -s % CS
        D_res = D[:, None] * jnp.pad(h, ((0, 0), (0, pad), (0, 0), (0, 0)))
        h = h * dt[..., None]
        A_d = A * dt

        def chunk(t):
            t = jnp.pad(t, ((0, 0), (0, pad)) + ((0, 0),) * (t.ndim - 2))
            return t.reshape(b, -1, CS, *t.shape[2:])
        hc, Ac, Bc, Cc = (chunk(h), chunk(A_d), chunk(Bm), chunk(Cm))
        Ac = jnp.transpose(Ac, (0, 3, 1, 2))
        A_cs = jnp.cumsum(Ac, axis=-1)
        L = jnp.exp(segment_sum(Ac))
        Gm = jnp.einsum('bclhn,bcshn->bclsh', Cc, Bc)
        M = Gm * jnp.transpose(L, (0, 2, 3, 4, 1))
        Y_diag = jnp.einsum('bclsh,bcshp->bclhp', M, hc)
        decay = jnp.exp(A_cs[..., -1:] - A_cs)
        Bdec = Bc * jnp.transpose(decay, (0, 2, 3, 1))[..., None]
        states = jnp.einsum('bclhn,bclhp->bchpn', Bdec, hc)
        states = jnp.concatenate([jnp.zeros_like(states[:, :1]), states], axis=1)
        A_last = jnp.pad(A_cs[..., -1], ((0, 0), (0, 0), (1, 0)))
        dchunk = jnp.transpose(jnp.exp(segment_sum(A_last)), (0, 3, 2, 1))
        new_states = jnp.einsum('bzjh,bzhpn->bjhpn', dchunk, states)
        states = new_states[:, :-1]
        sdo = jnp.exp(A_cs)
        Y_off = jnp.einsum('bclhn,bchpn->bclhp', Cc, states) * jnp.transpose(sdo, (0, 2, 3, 1))[..., None]
        y = (Y_diag + Y_off).reshape(b, -1, NH, P) + D_res
        y = y[:, :s].reshape(b, s, E)
        yf = y * jax.nn.silu(gate)
        var = jnp.mean(yf * yf, axis=-1, keepdims=True)
        yn = norm_w * (yf * jax.lax.rsqrt(var + EPS))
        return yn @ out_proj_w.T

    def _L1_ffn_ref(x, gate_w, expert_fc1, expert_fc2, expert_proj, shared_fc1, shared_fc2, shared_proj, shared_gate_w):
        import jax, jax.numpy as jnp
        import numpy as np
        B, T, C = (2, 256, 512)
        E, TOPK = (8, 2)
        F_MOE = 352
        F_SHARED = 1408
        b, t, c = x.shape
        xf = x.reshape(-1, c)
        n = xf.shape[0]
        router = xf @ gate_w.T
        probs = jax.nn.softmax(router.astype(jnp.float32), axis=1).astype(x.dtype)
        top_p, top_i = jax.lax.top_k(probs, TOPK)
        combine = jnp.zeros((n, E), dtype=x.dtype).at[jnp.arange(n)[:, None], top_i].set(top_p)
        h1 = jnp.einsum('nc,efc->enf', xf, expert_fc1)
        h2 = jnp.einsum('nc,efc->enf', xf, expert_fc2)
        h = jax.nn.silu(h1) * h2
        out_e = jnp.einsum('enf,ecf->enc', h, expert_proj)
        y = jnp.einsum('ne,enc->nc', combine, out_e)
        s1 = xf @ shared_fc1.T
        s2 = xf @ shared_fc2.T
        shared = jax.nn.silu(s1) * s2 @ shared_proj.T
        y = y + jax.nn.sigmoid(xf @ shared_gate_w.T) * shared
        return y.reshape(b, t, c)
    x = L0_attn_x
    xn = _layernorm(x, axis=-1)
    x = x + _L0_attn_ref(xn, L0_attn_Wq, L0_attn_Wk, L0_attn_Wv, L0_attn_Wo, L0_attn_Wg1, L0_attn_Wg2, L0_attn_norm_weight) + _L0_ffn_ref(xn, L0_ffn_gate_up_packed, L0_ffn_gate_up_scales, L0_ffn_down_packed, L0_ffn_down_scales)
    xn = _layernorm(x, axis=-1)
    x = x + _L1_attn_ref(xn, L1_attn_in_proj_w, L1_attn_conv_w, L1_attn_conv_b, L1_attn_dt_bias, L1_attn_A_log, L1_attn_D, L1_attn_norm_w, L1_attn_out_proj_w) + _L1_ffn_ref(xn, L1_ffn_gate_w, L1_ffn_expert_fc1, L1_ffn_expert_fc2, L1_ffn_expert_proj, L1_ffn_shared_fc1, L1_ffn_shared_fc2, L1_ffn_shared_proj, L1_ffn_shared_gate_w)
    return x

_drawn_inputs = setup_inputs


def setup_inputs(seed=0):
    import zlib

    import numpy as np

    out = dict(_drawn_inputs(seed))
    spreads = {'L0_attn_norm_weight': (1.0, 0.2),
     'L1_attn_conv_b': (0.0, 0.394),
     'L1_attn_D': (1.0, 0.6),
     'L1_attn_norm_w': (1.0, 0.6)}
    factors = {'L0_attn_Wg1': 7.444,
     'L0_attn_Wg2': 7.369,
     'L1_attn_dt_bias': 200.0,
     'L1_attn_A_log': 8.0,
     'L1_ffn_gate_w': 8.0,
     'L1_ffn_expert_fc1': 7.769,
     'L1_ffn_expert_fc2': 7.623,
     'L1_ffn_expert_proj': 7.631,
     'L1_ffn_shared_gate_w': 64.0,
     'L1_attn_conv_w': 22.414,
     'L1_ffn_shared_fc1': 8.0,
     'L1_ffn_shared_fc2': 8.0,
     'L1_ffn_shared_proj': 8.0,
     'L1_attn_in_proj_w': 2.73,
     'L1_attn_out_proj_w': 2.716}
    for name, (base, spread) in spreads.items():
        noise = np.random.default_rng([zlib.crc32(name.encode()), seed]).standard_normal(out[name].shape)
        drawn = base * np.exp(spread * noise) if base else spread * noise
        out[name] = jnp.asarray(drawn.astype(out[name].dtype))
    for name, factor in factors.items():
        out[name] = (out[name] * factor).astype(out[name].dtype)
    return out
```

```python
from contextlib import ExitStack

import concourse.bass as bass
from concourse import mybir

F32 = mybir.dt.float32
F32R = mybir.dt.float32r
F16 = mybir.dt.float16
BF16 = mybir.dt.bfloat16
I32 = mybir.dt.int32
ALU = mybir.AluOpType
ACT = mybir.ActivationFunctionType
AX_X = mybir.AxisListType.X

P = 128
BANK = 512
BATCHES = 4
BT = 512
TPB = BT // P
TILES = BATCHES * TPB
D = 512
KT = D // P
JT = 3
LAST_JT = 2
GF = JT * P



def clear_semaphores(nc, semaphores):
    nc.clear_and_free_semaphores(semaphores)
    nc.all_engine_barrier()


FP4_GROUPS = 4
SHARED_GROUPS = FP4_GROUPS


HEADS = 16
HD = 32
HPT = P // HD


def linear_attention_phase(nc, x_dram, wts, tables, x_parts, out_dram):
    name = "a0"
    semaphores = []
    with ExitStack() as ctx:
        ctx.callback(clear_semaphores, nc, semaphores)

        def sb(label, shape, dt=F32):
            return ctx.enter_context(nc.sbuf_tensor(f"{name}_{label}", shape, dt))

        def bank(label):
            return ctx.enter_context(nc.psum_tensor(f"{name}_{label}", [P, BANK], F32))

        def sem(label):
            semaphores.append(nc.alloc_semaphore(f"{name}_{label}"))
            return semaphores[-1]

        w_raw = sb("w_raw", [P, 2, KT, D])
        w_hi = sb("w_hi", [P, 4, KT, D], F32R)
        w_lo = sb("w_lo", [P, 4, KT, D], F32R)
        g1_raw = sb("g1_raw", [P, KT, HD])
        g1_hi = sb("g1_hi", [P, KT, HD], F32R)
        g1_lo = sb("g1_lo", [P, KT, HD], F32R)
        g2 = sb("g2", [HD, D])
        norm_w = sb("norm_w", [P, KT])
        ident = sb("ident", [P, P])
        rope_cos = sb("rope_cos", [P, TPB, HD])
        rope_sin = sb("rope_sin", [P, TPB, HD])
        decay = sb("decay", [P, HPT, HPT, P])
        decay_q = sb("decay_q", [P, HEADS])
        decay_k = sb("decay_k", [P, HEADS])
        same_head = sb("same_head", [P, P])
        chunk_decay = sb("chunk_decay", [P, KT, P])
        power = sb("power", [P, HEADS])

        x = sb("x", [P, TPB, D])
        stats = sb("stats", [P, 6])
        mean_var = sb("mean_var", [P, 2, 2])
        ln_tmp = sb("ln_tmp", [P, 1])
        stats_copy = sb("stats_copy", [P, 1])
        eps_ln = sb("eps_ln", [P, 1])
        eps_head = sb("eps_head", [P, HEADS])
        ln_rs = sb("ln_rs", [P, 2])
        xn = sb("xn", [P, 2, D])
        xt_hi = [sb(f"xt_hi{n}", [P, KT, P], F32R) for n in range(2)]
        xt_lo = [sb(f"xt_lo{n}", [P, KT, P], F32R) for n in range(2)]
        qk = sb("qk", [P, 2 * HEADS, HD])
        qk_cos = sb("qk_cos", [P, 2 * HEADS, HD])
        qk_sin = sb("qk_sin", [P, 2 * HEADS, HD])
        qk_rot = [sb(f"qk_rot{n}", [P, 2 * HEADS, HD]) for n in range(2)]
        k_dec = [sb(f"k_dec{n}", [P, HEADS, HD]) for n in range(2)]
        v = [sb(f"v{n}", [P, D]) for n in range(2)]
        gate_low = sb("gate_low", [HD, P])
        gate = sb("gate", [P, 2, D])
        qt = sb("qt", [P, KT, P])
        kt_ = sb("kt", [P, KT, P])
        scores = sb("scores", [P, HPT, HPT, P])
        inter = sb("inter", [P, D])
        o_sum = sb("o_sum", [P, D])
        x2 = sb("x2", [P, D])
        sq = sb("sq", [P, D])
        ss = sb("ss", [P, HEADS])
        ms = sb("ms", [P, HEADS])
        rs = sb("rs", [P, HEADS])
        o_norm = sb("o_norm", [P, D])
        ot_hi = sb("ot_hi", [P, KT, P], F32R)
        ot_lo = sb("ot_lo", [P, KT, P], F32R)
        state = sb("state", [P, KT, P])
        state_new = sb("state_new", [P, KT, P])
        state_old = sb("state_old", [P, KT, P])

        proj_ps = [bank(f"proj{n}") for n in range(2)]
        score_ps = [bank(f"score{n}") for n in range(HPT)]
        misc_ps = [bank(f"misc{n}") for n in range(2)]
        o_ps, y_ps = score_ps[0], score_ps[1]

        def sems(group, labels):
            return {label: sem(f"{group}_{label}") for label in labels.split()}

        loaded = sems("loaded", "const q_k_v_low")
        w = sems("w", "hi split normed")
        ln = sems("ln", "stats_step stats rstd normed")
        xt = sems("xt", "ps hi lo")
        ps = sems("ps", "q k v low gate qt kt scores inter state o ot y")
        act_out = sems("act_out", "q k v low gate qt kt sq ot_hi")
        rot = sems("rot", "cos sin done k_decayed")
        st = sems("st", "masked old ready")
        masked = sem("masked")
        out = sems("out", "inter_scaled summed gated squares rstd normed ot_lo y_added")
        power_set = sem("power_set")
        x_in = [sem(f"x_in{n}") for n in range(TPB)]
        y_stored = [sem(f"y_stored{n}") for n in range(TPB)]
        xt_stored = [sem(f"xt_stored{n}") for n in range(2)]
        w_loaded = [sem(f"w_loaded{n}") for n in range(2)]

        block = ctx.enter_context(nc.Block())

        @block.sync
        def _(sp):
            def load_w(n):
                sp.dma_start(w_raw[:, n % 2, :, :].rearrange("p k n -> p (k n)"), wts["qkvo"][n]
                             ).then_inc(w_loaded[n % 2], 16)

            def load_x(batch, i):
                sp.dma_start(x[:, i, :], x_dram[bass.ds(batch * TPB + i, 1)].rearrange("o p n -> (o p) n")
                             ).then_inc(x_in[i], 16)

            def store_xt(t, odd):
                sp.wait_ge(xt["hi"], t + 1)
                sp.wait_ge(xt["lo"], t + 1)
                for part, buf in ((0, xt_hi[odd]), (1, xt_lo[odd])):
                    sp.dma_start(x_parts[part, bass.ds(t, 1)].rearrange("o p n -> (o p) n"),
                                 buf[:, :, :].bitcast(F32).rearrange("p k n -> p (k n)")).then_inc(xt_stored[odd], 16)

            load_x(0, 0)
            sp.dma_start(ident[:, :], tables["ident"]).then_inc(loaded["const"], 16)
            load_x(0, 1)
            load_w(0)
            load_w(1)
            small = ((g1_raw, wts["g1"]), (g2, wts["g2"]), (norm_w, wts["norm_w"]), (rope_cos, tables["cos"]),
                     (rope_sin, tables["sin"]), (decay_q, tables["decay_q"]), (decay_k, tables["decay_k"]),
                     (same_head, tables["same_head"]), (chunk_decay, tables["chunk_decay"]), (decay, tables["decay"]))
            for dst, src in small:
                sp.dma_start(dst[:], src).then_inc(loaded["const"], 16)
            load_x(0, 2)
            load_x(0, 3)
            for n in (2, 3):
                sp.wait_ge(w["split"], n - 1)
                load_w(n)
            store_xt(0, 0)
            store_xt(1, 1)
            with sp.Fori(0, BATCHES) as b:
                for i in range(TPB):
                    for done in ([i - 1] if i else []) + ([i] if i == TPB - 1 else []):
                        sp.wait_ge(out["y_added"], b * TPB + done + 2)
                        sp.dma_start(out_dram[bass.ds(b * TPB + done, 1)].rearrange("o p n -> (o p) n"),
                                     x[:, done, :]).then_inc(y_stored[done], 16)
                        sp.wait_ge(y_stored[done], 16 * b + 16)
                        load_x((b + 1) % BATCHES, done)
                    store_xt(b * TPB + i + 2, i % 2)
            for n in range(TPB):
                sp.wait_ge(x_in[n], 16 * (BATCHES + 1))
            for n in range(2):
                sp.wait_ge(xt_stored[n], 16 * (TILES + 2))

        @block.tensor
        def _(pe):
            def turn(to, src, ready):
                for k in range(KT):
                    last = pe.transpose(to[:, k * P:(k + 1) * P], src[:, k * P:(k + 1) * P], ident[:, :])
                last.then_inc(ready, 1)

            def sums(to, l_hi, l_lo, r_hi, r_lo, k):
                pe.matmul(to, l_hi, r_hi, start=k == 0, stop=False)
                pe.matmul(to, l_hi, r_lo, start=False, stop=False)
                return pe.matmul(to, l_lo, r_hi, start=False, stop=k == KT - 1)

            def project(bank_, n, odd, ready):
                for k in range(KT):
                    last = sums(bank_[:, :], xt_hi[odd][:, k, :], xt_lo[odd][:, k, :], w_hi[:, n, k, :], w_lo[:, n, k, :], k)
                last.then_inc(ready, 1)

            def x_turned(t, odd):
                pe.wait_ge(ln["normed"], t + 1)
                turn(misc_ps[1], xn[:, odd, :], xt["ps"])

            def q_proj(t, odd, first=False):
                pe.wait_ge(xt["hi"], t + 1)
                pe.wait_ge(xt["lo"], t + 1)
                if not first:
                    pe.wait_ge(act_out["v"], t)
                project(proj_ps[0], 0, odd, ps["q"])

            def k_proj(t, odd, first=False):
                if not first:
                    pe.wait_ge(act_out["gate"], t)
                project(proj_ps[1], 1, odd, ps["k"])

            def v_proj(t, odd):
                pe.wait_ge(act_out["q"], t + 1)
                project(proj_ps[0], 2, odd, ps["v"])
                pe.wait_ge(act_out["k"], t + 1)
                for k in range(KT):
                    last = sums(proj_ps[1][0:HD, 0:P], g1_hi[:, k, :], g1_lo[:, k, :],
                                xt_hi[odd][:, k, :], xt_lo[odd][:, k, :], k)
                last.then_inc(ps["low"], 1)

            def gate_proj(t):
                pe.wait_ge(act_out["low"], t + 1)
                pe.matmul(proj_ps[1][:, :], gate_low[:, :], g2[:, :], start=True, stop=True).then_inc(ps["gate"], 1)

            def o_turned(t):
                pe.wait_ge(out["normed"], t + 1)
                turn(misc_ps[0], o_norm[:, :], ps["ot"])

            def y_proj(t):
                pe.wait_ge(act_out["ot_hi"], t + 1)
                pe.wait_ge(out["ot_lo"], t + 1)
                for k in range(KT):
                    last = sums(y_ps[:, :], ot_hi[:, k, :], ot_lo[:, k, :], w_hi[:, 3, k, :], w_lo[:, 3, k, :], k)
                last.then_inc(ps["y"], 1)

            def score(t, i):
                pe.wait_ge(act_out["qt"], t + 1)
                pe.wait_ge(act_out["kt"], t + 1)
                pe.wait_ge(out["gated"], t + 1)
                pe.wait_ge(out["y_added"], t if i else t + 1)
                for g in range(KT):
                    for r in range(HPT):
                        rows = slice(r * HD, (r + 1) * HD)
                        last = pe.matmul(score_ps[r][:, g * P:(g + 1) * P], kt_[rows, g, :], qt[rows, g, :],
                                         start=True, stop=True)
                        if g == KT - 1:
                            last.then_inc(ps["scores"], 1)

            def attend(t, odd):
                pe.wait_ge(masked, HPT * (t + 1))
                for h in range(HEADS):
                    last = pe.matmul(o_ps[:, h * HD:(h + 1) * HD], scores[:, h % HPT, h // HPT, :],
                                     v[odd][:, h * HD:(h + 1) * HD], start=True, stop=True)
                last.then_inc(ps["o"], 1)

            pe.wait_ge(loaded["const"], 16 * 11)
            x_turned(0, 0)
            pe.wait_ge(xt["hi"], 1)
            pe.wait_ge(xt["lo"], 1)
            x_turned(1, 1)
            pe.wait_ge(w["split"], 1)
            q_proj(0, 0, first=True)
            pe.wait_ge(w["split"], 2)
            k_proj(0, 0, first=True)
            pe.wait_ge(w["split"], 4)
            v_proj(0, 0)
            gate_proj(0)
            pe.wait_ge(w["split"], 5)
            with pe.Fori(0, BATCHES) as b:
                for i in range(TPB):
                    t = b * TPB + i
                    odd, other = i % 2, (i + 1) % 2
                    pe.wait_ge(rot["done"], t + 1)
                    if i == 1:
                        pe.wait_ge(st["ready"], 3 * b + 1)
                    elif i > 1:
                        pe.wait_ge(st["masked"], 2 * b + i - 1)
                    turn(misc_ps[0], qk_rot[odd][:, 0:HEADS, :].rearrange("p h d -> p (h d)"), ps["qt"])
                    pe.wait_ge(xt["hi"], t + 2)
                    pe.wait_ge(xt["lo"], t + 2)
                    turn(misc_ps[1], qk_rot[odd][:, HEADS:2 * HEADS, :].rearrange("p h d -> p (h d)"), ps["kt"])
                    q_proj(t + 1, other)
                    if i:
                        pe.wait_ge(act_out["qt"], t + 1)
                        o_turned(t - 1)
                    score(t, i)
                    if i:
                        pe.wait_ge(st["ready"], 3 * b + i)
                        for g in range(KT):
                            last = pe.matmul(misc_ps[1][:, g * P:(g + 1) * P], qt[:, g, :], state[:, g, :],
                                             start=True, stop=True)
                        last.then_inc(ps["inter"], 1)
                    if i == TPB - 1:
                        attend(t, odd)
                    k_proj(t + 1, other)
                    if i < TPB - 1:
                        pe.wait_ge(rot["k_decayed"], t + 1)
                        if i:
                            pe.wait_ge(act_out["ot_hi"], t)
                            pe.wait_ge(out["ot_lo"], t)
                        for g in range(KT):
                            cols = slice(g * P, (g + 1) * P)
                            last = pe.matmul(misc_ps[0][:, cols],
                                             k_dec[odd][:, :, :].rearrange("p h d -> p (h d)")[:, cols],
                                             v[odd][:, cols], start=True, stop=True)
                        last.then_inc(ps["state"], 1)
                    v_proj(t + 1, other)
                    if i < TPB - 1:
                        attend(t, odd)
                    if i:
                        y_proj(t - 1)
                    gate_proj(t + 1)
                    if i:
                        pe.wait_ge(out["inter_scaled"], 3 * b + i)
                    x_turned(t + 2, odd)
                    if i == TPB - 1:
                        o_turned(t)
                        pe.wait_ge(out["y_added"], t + 1)
                        y_proj(t)

        @block.scalar
        def _(act):
            qk_flat = qk[:, :, :].rearrange("p h d -> p (h d)")

            def x_high(t, odd, stored=None):
                act.wait_ge(xt["ps"], t + 1)
                if stored is not None:
                    act.wait_ge(ps["low"], t - 1)
                    act.wait_ge(xt_stored[odd], stored)
                act.copy(xt_hi[odd][:, :, :], misc_ps[1][:, :].rearrange("p (k n) -> p k n", k=KT)).then_inc(xt["hi"], 1)

            def projected(t, odd, first=False):
                act.wait_ge(ps["q"], t + 1)
                if not first:
                    act.wait_ge(rot["cos"], t)
                    act.wait_ge(rot["sin"], t)
                act.activation(qk_flat[:, 0:D], proj_ps[0][:, :], ACT.Silu).then_inc(act_out["q"], 1)
                act.wait_ge(ps["k"], t + 1)
                act.activation(qk_flat[:, D:2 * D], proj_ps[1][:, :], ACT.Silu).then_inc(act_out["k"], 1)
                act.wait_ge(ps["v"], t + 1)
                act.copy(v[odd][:, :], proj_ps[0][:, :]).then_inc(act_out["v"], 1)
                act.wait_ge(ps["low"], t + 1)
                act.copy(gate_low[:, :], proj_ps[1][0:HD, 0:P]).then_inc(act_out["low"], 1)

            def gated(t, odd):
                act.wait_ge(ps["gate"], t + 1)
                act.activation(gate[:, odd, :], proj_ps[1][:, :], ACT.Tanh, scale=0.5).then_inc(act_out["gate"], 1)

            def o_high(t):
                act.wait_ge(ps["ot"], t + 1)
                act.copy(ot_hi[:, :, :], misc_ps[0][:, :].rearrange("p (k n) -> p k n", k=KT)).then_inc(act_out["ot_hi"], 1)

            def w_high(n):
                act.wait_ge(w_loaded[n % 2], 16 * (n // 2 + 1))
                act.copy(w_hi[:, n, :, :], w_raw[:, n % 2, :, :]).then_inc(w["hi"], 1)

            x_high(0, 0)
            w_high(0)
            x_high(1, 1)
            w_high(1)
            w_high(2)
            act.wait_ge(loaded["const"], 16 * 11)
            act.copy(g1_hi[:, :, :], g1_raw[:, :, :]).then_inc(w["hi"], 1)
            projected(0, 0, first=True)
            gated(0, 0)
            act.wait_ge(w["normed"], KT)
            w_high(3)
            with act.Fori(0, BATCHES) as b:
                for i in range(TPB):
                    t = b * TPB + i
                    odd, other = i % 2, (i + 1) % 2
                    act.wait_ge(ps["qt"], t + 1)
                    act.copy(qt[:, :, :], misc_ps[0][:, :].rearrange("p (k n) -> p k n", k=KT)).then_inc(act_out["qt"], 1)
                    act.wait_ge(ps["kt"], t + 1)
                    act.copy(kt_[:, :, :], misc_ps[1][:, :].rearrange("p (k n) -> p k n", k=KT)).then_inc(act_out["kt"], 1)
                    if i:
                        o_high(t - 1)
                    projected(t + 1, other)
                    act.wait_ge(out["gated"], t + 2)
                    act.activation(sq[:, :], x2[:, :], ACT.Square).then_inc(act_out["sq"], 1)
                    gated(t + 1, other)
                    x_high(t + 2, odd, stored=16 * (t + 2 - odd))
                    if i == TPB - 1:
                        o_high(t)

        @block.gpsimd
        def _(pool):
            def ln_rstd(t, odd):
                pool.wait_ge(ln["stats"], t + 1)
                pool.tensor_tensor(ln_tmp[:, :], mean_var[:, odd, 1:2], eps_ln[:, :], ALU.add).then_inc(ln["rstd"], 1)
                pool.wait_ge(ln["rstd"], 2 * t + 1)
                pool.tensor_tensor(ln_rs[:, odd:odd + 1], ln_tmp[:, :], power[:, 0:1], ALU.pow).then_inc(ln["rstd"], 1)

            def swap(t, i, first=False):
                half = HD // 2
                pool.wait_ge(act_out["q"], t + 1)
                pool.wait_ge(act_out["k"], t + 1)
                if not first:
                    pool.wait_ge(rot["done"], t)
                for to, of in ((0, half), (half, 0)):
                    last = pool.tensor_tensor(qk_sin[:, :, to:to + half], qk[:, :, of:of + half],
                                              rope_sin[:, i:i + 1, to:to + half].to_broadcast([P, 2 * HEADS, half]), ALU.mult)
                last.then_inc(rot["sin"], 1)

            pool.memset(power[:, :], -0.5).then_inc(power_set, 1)
            pool.memset(eps_ln[:, :], 1e-5).then_inc(power_set, 1)
            pool.memset(eps_head[:, :], 4 * HD * 1e-6).then_inc(power_set, 1)
            pool.wait_ge(power_set, 3)
            ln_rstd(0, 0)
            ln_rstd(1, 1)
            pool.wait_ge(loaded["const"], 16 * 11)
            swap(0, 0, first=True)
            with pool.Fori(0, BATCHES) as b:
                for i in range(TPB):
                    t = b * TPB + i
                    if i in (1, 2):
                        pool.wait_ge(st["ready"], 3 * b + i)
                        pool.tensor_tensor(state_old[:, :, :], state[:, :, :], chunk_decay[:, :, :], ALU.mult).then_inc(st["old"], 1)
                    ln_rstd(t + 2, i % 2)
                    swap(t + 1, (i + 1) % TPB)
                    pool.wait_ge(out["squares"], t + 1)
                    pool.tensor_tensor(ms[:, :], ss[:, :], eps_head[:, :], ALU.add).then_inc(out["rstd"], 1)
                    pool.wait_ge(out["rstd"], 2 * t + 1)
                    pool.tensor_tensor(rs[:, :], ms[:, :], power[:, :], ALU.pow).then_inc(out["rstd"], 1)

        @block.vector
        def _(dve):
            def x_stats(t, odd, slot, count):
                dve.wait_ge(x_in[slot], 16 * count)
                dve.bn_stats(stats[:, :], x[:, slot, :]).then_inc(ln["stats_step"], 1)
                dve.wait_ge(ln["stats_step"], t + 1)
                dve.tensor_copy(stats_copy[:, :], stats[:, 0:1])
                dve.bn_aggr(mean_var[:, odd, :], stats[:, :]).then_inc(ln["stats"], 1)

            def x_normed(t, odd, slot, first=False):
                dve.wait_ge(ln["rstd"], 2 * t + 2)
                if not first:
                    dve.wait_ge(xt["ps"], t - 1)
                dve.tensor_scalar(xn[:, odd, :], x[:, slot, :], mean_var[:, odd, 0:1], ln_rs[:, odd:odd + 1],
                                  ALU.subtract, ALU.mult).then_inc(ln["normed"], 1)

            def x_low(t, odd):
                dve.wait_ge(xt["hi"], t + 1)
                dve.tensor_tensor(xt_lo[odd][:, :, :], misc_ps[1][:, :].rearrange("p (k n) -> p k n", k=KT),
                                  xt_hi[odd][:, :, :].bitcast(F32), ALU.subtract).then_inc(xt["lo"], 1)

            def rotate(t, i, odd):
                dve.wait_ge(act_out["q"], t + 1)
                dve.wait_ge(act_out["k"], t + 1)
                dve.tensor_tensor(qk_cos[:, :, :], qk[:, :, :], rope_cos[:, i:i + 1, :].to_broadcast([P, 2 * HEADS, HD]),
                                  ALU.mult).then_inc(rot["cos"], 1)
                dve.wait_ge(rot["cos"], t + 1)
                dve.wait_ge(rot["sin"], t + 1)
                dve.tensor_tensor(qk_rot[odd][:, :, :], qk_cos[:, :, :], qk_sin[:, :, :], ALU.add).then_inc(rot["done"], 1)
                dve.wait_ge(rot["done"], t + 1)
                dve.tensor_tensor(k_dec[odd][:, :, :], qk_rot[odd][:, HEADS:2 * HEADS, :],
                                  decay_k[:, :].unsqueeze(2).to_broadcast([P, HEADS, HD]), ALU.mult).then_inc(rot["k_decayed"], 1)

            def o_low(t):
                dve.wait_ge(act_out["ot_hi"], t + 1)
                dve.tensor_tensor(ot_lo[:, :, :], misc_ps[0][:, :].rearrange("p (k n) -> p k n", k=KT),
                                  ot_hi[:, :, :].bitcast(F32), ALU.subtract).then_inc(out["ot_lo"], 1)

            def add_y(t, slot):
                dve.wait_ge(ps["y"], t + 1)
                dve.tensor_tensor(x[:, slot, :], x[:, slot, :], y_ps[:, :], ALU.add).then_inc(out["y_added"], 1)

            def w_low(n, slot, count):
                dve.wait_ge(w["hi"], count)
                dve.tensor_tensor(w_lo[:, n, :, :], w_raw[:, slot, :, :], w_hi[:, n, :, :].bitcast(F32),
                                  ALU.subtract).then_inc(w["split"], 1)

            dve.sem_inc(out["gated"], 1)
            dve.sem_inc(out["y_added"], 1)
            x_stats(0, 0, 0, 1)
            x_normed(0, 0, 0, first=True)
            x_stats(1, 1, 1, 1)
            x_normed(1, 1, 1, first=True)
            x_low(0, 0)
            w_low(0, 0, 1)
            x_low(1, 1)
            w_low(1, 1, 2)
            w_low(2, 0, 3)
            dve.wait_ge(w["hi"], 4)
            dve.wait_ge(loaded["const"], 16 * 11)
            dve.tensor_tensor(g1_lo[:, :, :], g1_raw[:, :, :], g1_hi[:, :, :].bitcast(F32), ALU.subtract).then_inc(w["split"], 1)
            rotate(0, 0, 0)
            dve.wait_ge(w_loaded[1], 32)
            for k in range(KT):
                dve.tensor_scalar(w_raw[:, 1, k, :], w_raw[:, 1, k, :], norm_w[:, k:k + 1], 0.5 * (4 * HD) ** 0.5, ALU.mult, ALU.mult
                                  ).then_inc(w["normed"], 1)
            w_low(3, 1, 5)
            with dve.Fori(0, BATCHES) as b:
                for i in range(TPB):
                    t = b * TPB + i
                    odd, other = i % 2, (i + 1) % 2
                    ahead = (i + 2) % TPB
                    if i:
                        o_low(t - 1)
                    x_stats(t + 2, odd, ahead, b + (i + 2) // TPB + 1)
                    for r in range(HPT):
                        dve.wait_ge(ps["scores"], HPT * t + r + 1)
                        dve.tensor_tensor(scores[:, r, :, :], score_ps[r][:, :].rearrange("p (g n) -> p g n", g=HPT),
                                          decay[:, r, :, :], ALU.mult).then_inc(masked, 1)
                    if i:
                        dve.wait_ge(ps["inter"], 3 * b + i)
                        dve.tensor_tensor(inter[:, :].rearrange("p (h d) -> p h d", h=HEADS),
                                          misc_ps[1][:, :].rearrange("p (h d) -> p h d", h=HEADS),
                                          decay_q[:, :].unsqueeze(2).to_broadcast([P, HEADS, HD]),
                                          ALU.mult).then_inc(out["inter_scaled"], 1)
                    x_normed(t + 2, odd, ahead)
                    if i < TPB - 1:
                        to, ready = (state, st["ready"]) if i == 0 else (state_new, st["masked"])
                        dve.wait_ge(ps["state"], 3 * b + i + 1)
                        dve.tensor_tensor(to[:, :, :], misc_ps[0][:, :].rearrange("p (k n) -> p k n", k=KT),
                                          same_head[:, :].unsqueeze(1).to_broadcast([P, KT, P]), ALU.mult).then_inc(ready, 1)
                        if i:
                            dve.wait_ge(st["masked"], 2 * b + i)
                            dve.wait_ge(st["old"], 2 * b + i)
                            dve.tensor_tensor(state[:, :, :], state_old[:, :, :], state_new[:, :, :],
                                              ALU.add).then_inc(st["ready"], 1)
                    rotate(t + 1, (i + 1) % TPB, other)
                    dve.wait_ge(ps["o"], t + 1)
                    dve.wait_ge(act_out["gate"], t + 1)
                    src = o_ps
                    if i:
                        dve.wait_ge(out["inter_scaled"], 3 * b + i)
                        dve.tensor_tensor(o_sum[:, :], o_ps[:, :], inter[:, :], ALU.add).then_inc(out["summed"], 1)
                        dve.wait_ge(out["summed"], 3 * b + i)
                        src = o_sum
                    dve.scalar_tensor_tensor(x2[:, :], gate[:, odd, :], 1.0, src[:, :], ALU.add, ALU.mult).then_inc(out["gated"], 1)
                    if i:
                        add_y(t - 1, i - 1)
                    dve.wait_ge(act_out["sq"], t + 1)
                    dve.tensor_reduce(ss[:, :], sq[:, :].rearrange("p (h d) -> p h d", h=HEADS), AX_X, ALU.add
                                      ).then_inc(out["squares"], 1)
                    dve.wait_ge(out["gated"], t + 2)
                    dve.wait_ge(out["rstd"], 2 * t + 2)
                    dve.tensor_tensor(o_norm[:, :].rearrange("p (h d) -> p h d", h=HEADS),
                                      x2[:, :].rearrange("p (h d) -> p h d", h=HEADS),
                                      rs[:, :].unsqueeze(2).to_broadcast([P, HEADS, HD]), ALU.mult).then_inc(out["normed"], 1)
                    x_low(t + 2, odd)
                    if i == TPB - 1:
                        o_low(t)
                        add_y(t, i)


def attention0_tables():
    import numpy as np

    f = np.float32
    half = HD // 2
    theta = f(10000.0) ** (f(-2.0) * np.arange(half, dtype=f) / f(HD))
    ang = np.arange(BT, dtype=f)[:, None] * theta[None, :].astype(f)
    cos, sin = np.cos(ang.astype(f)), np.sin(ang.astype(f))

    def tiled(a):
        return np.ascontiguousarray(a.reshape(TPB, P, HD).transpose(1, 0, 2).astype(f))

    log_lam = -(f(2.0) ** (f(-8.0) * (np.arange(HEADS, dtype=f) + f(1.0)) / f(HEADS))).astype(f)
    i = np.arange(P, dtype=f)
    diff = i[None, :] - i[:, None]
    d = np.exp(log_lam[:, None, None] * np.maximum(diff, 0)[None]) * (diff >= 0)[None]
    block = np.kron(np.eye(HPT), np.ones((HD, HD)))
    lam = np.exp(log_lam * f(P)).reshape(KT, HPT)
    chunk = np.stack([block * np.repeat(lam[g], HD)[:, None] for g in range(KT)], axis=1)
    return {
        "ident": np.eye(P, dtype=f),
        "cos": tiled(np.concatenate([cos, cos], axis=1)),
        "sin": tiled(np.concatenate([-sin, sin], axis=1)),
        "decay": np.ascontiguousarray(d.reshape(KT, HPT, P, P).transpose(2, 1, 0, 3).astype(f)),
        "decay_q": np.exp(log_lam[None, :] * (i[:, None] + f(1.0))).astype(f),
        "decay_k": np.exp(log_lam[None, :] * (f(P) - f(1.0) - i[:, None])).astype(f),
        "same_head": block.astype(f),
        "chunk_decay": np.ascontiguousarray(chunk.astype(f)),
    }


def swiglu_phase(nc, name, x_parts, up_src, down_src, groups, routed, fp4, out_dram):
    chunks = 3 * JT
    last_g = groups - 1
    steps_before_last = last_g * BATCHES

    semaphores = []
    with ExitStack() as ctx:
        ctx.callback(clear_semaphores, nc, semaphores)

        def sb(label, shape, dt=F32):
            return ctx.enter_context(nc.sbuf_tensor(f"{name}_{label}", shape, dt))

        def bank(label):
            return ctx.enter_context(nc.psum_tensor(f"{name}_{label}", [P, BANK], F32))

        def sem(label):
            semaphores.append(nc.alloc_semaphore(f"{name}_{label}"))
            return semaphores[-1]

        x_hi = sb("x_hi", [P, TILES, KT, P], F32R)
        x_lo = sb("x_lo", [P, TILES, KT, P], F32R)
        acc = sb("acc", [P, TILES, D])
        up_f32 = sb("up_f32", [P, JT, 2, KT, P])
        up_hi = sb("up_hi", [P, JT, 2, KT, P], F32R)
        up_lo = sb("up_lo", [P, JT, 2, KT, P], F32R)
        down_f32 = sb("down_f32", [P, JT, D])
        down_hi = sb("down_hi", [P, JT, D], F32R)
        down_lo = sb("down_lo", [P, JT, D], F32R)
        silu_g = sb("silu_g", [P, 2, BT])
        h_f32 = sb("h_f32", [P, 2, BT])
        h_hi = sb("h_hi", [P, JT, BT], F32R)
        h_lo = sb("h_lo", [P, JT, BT], F32R)
        gate_ps = [bank(f"gate{n}") for n in range(2)]
        up_ps = [bank(f"up{n}") for n in range(2)]
        y_ps = [bank(f"y{n}") for n in range(TPB)]

        x_loaded = [sem(f"x_loaded{b}") for b in range(BATCHES)]
        aux_loaded = sem("aux_loaded")
        weights_loaded = sem("weights_loaded")
        weights_hi = sem("weights_hi")
        weights_lo = sem("weights_lo")
        gu_ready = sem("gu_ready")
        silu_ready = sem("silu_ready")
        gu_free = sem("gu_free")
        hhi_ready = sem("hhi_ready")
        h_ready = sem("h_ready")
        y_ready = sem("y_ready")
        y_free = sem("y_free")
        stored = sem("stored")
        if fp4:
            words = sb("words", [P, 2, D], I32)
            scales = sb("scales", [P, 2, D], F16)
            magnitude = sb("magnitude", [P, D], I32)
            sign_bit = sb("sign_bit", [P, D], I32)
            above4 = sb("above4", [P, D], BF16)
            above6 = sb("above6", [P, D], BF16)
            half_sign = sb("half_sign", [P, D], BF16)
            twice = sb("twice", [P, D], BF16)
            value = sb("value", [P, D], BF16)
            shift = sb("shift", [P, 1], I32)
            resid = sb("resid", [P, TPB, D])
            meansq = sb("meansq", [P, TILES])
            rstd = sb("rstd", [P, TILES])
            power = sb("power", [P, TILES])
            square = sb("square", [P, D])
            chunk_loaded = [sem(f"chunk_loaded{n}") for n in range(2)]
            bits_ready = sem("bits_ready")
            lines_ready = sem("lines_ready")
            dq_step = sem("dq_step")
            value_ready = sem("value_ready")
            decoded = sem("decoded")
            power_set = sem("power_set")
            meansq_ready = sem("meansq_ready")
            rstd_step = sem("rstd_step")
            resid_loaded = sem("resid_loaded")
            final = sem("final")
            bias_m4 = sb("bias_m4", [P, 1])
            bias_m12 = sb("bias_m12", [P, 1])
            bias_half = sb("bias_half", [P, 1])
            bias_set = sem("bias_set")
        else:
            weight, start = routed
            comb = sb("comb", [P, TILES, groups])

        def sums(pe, out, w_hi, w_lo, v_hi, v_lo, start, stop):
            pe.matmul(out, w_hi, v_hi, start=start, stop=False)
            pe.matmul(out, w_hi, v_lo, start=False, stop=False)
            return pe.matmul(out, w_lo, v_hi, start=False, stop=stop)

        def tiles_before(g, b):
            if isinstance(g, int) and g == last_g:
                return steps_before_last * JT + b * LAST_JT
            return (g * BATCHES + b) * JT

        block = ctx.enter_context(nc.Block())

        @block.sync
        def _(sp):
            def load_weights(g):
                sp.dma_start(up_f32[:, :, :, :, :].rearrange("p j m k f -> p (j m k f)"),
                             up_src[bass.ds(g, 1)].rearrange("o p n -> (o p) n")).then_inc(weights_loaded, 16)
                sp.dma_start(down_f32[:, :, :],
                             down_src[bass.ds(g, 1)].rearrange("o (j p) n -> p (o j) n", p=P)).then_inc(weights_loaded, 16)

            def load_chunk(g, c):
                sp.dma_start(words[:, c % 2, :], up_src[bass.ds(g, 1), c].rearrange("o p n -> (o p) n")
                             ).then_inc(chunk_loaded[c % 2], 16)
                sp.dma_start(scales[:, c % 2, :], fp4["scales"][bass.ds(g, 1), c].rearrange("o n -> (o n)").partition_broadcast(P)
                             ).then_inc(chunk_loaded[c % 2], 16)

            def load_x(b):
                for part, dst in ((0, x_hi), (1, x_lo)):
                    sp.dma_start(dst[:, b * TPB:(b + 1) * TPB].bitcast(F32).rearrange("p t k n -> p t (k n)"),
                                 x_parts[part, b * TPB:(b + 1) * TPB].rearrange("t p n -> p t n"),
                                 ).then_inc(x_loaded[b], 16)

            def store(b):
                sp.dma_start(out_dram[bass.ds(b * TPB, TPB)].rearrange("t p n -> p t n"),
                             acc[:, bass.ds(b * TPB, TPB), :]).then_inc(stored, 16)

            if fp4:
                sp.dma_start(shift[:, :], fp4["shift"]).then_inc(aux_loaded, 16)
                load_chunk(0, 0)
                load_chunk(0, 1)
                load_x(0)
                for c in range(2, chunks):
                    sp.wait_ge(decoded, c - 1)
                    load_chunk(0, c)
                    if c in (4, 6, 8):
                        load_x(c // 2 - 1)
                with sp.Fori(0, last_g) as g:
                    for c in range(chunks):
                        back = {0: 0, 1: -1}.get(c, c - 1)
                        sp.wait_ge(decoded, chunks * (g + 1) + back)
                        load_chunk(g + 1, c)
                for b in range(BATCHES):
                    if b:
                        sp.wait_ge(final, TPB * b)
                    sp.dma_start(resid[:, :, :], fp4["resid"][b * TPB:(b + 1) * TPB].rearrange("t p n -> p t n")
                                 ).then_inc(resid_loaded, 16)
                    if b:
                        store(b - 1)
                sp.wait_ge(final, TPB * BATCHES)
                store(BATCHES - 1)
                sp.wait_ge(stored, 16 * BATCHES)
            else:
                load_weights(0)
                load_x(0)
                sp.dma_start(comb[:, :, :], weight).then_inc(aux_loaded, 16)
                load_x(1)
                sp.dma_start(acc[:, :, :], start.rearrange("t p n -> p t n")).then_inc(aux_loaded, 16)
                for b in range(2, BATCHES):
                    load_x(b)
                with sp.Fori(1, groups) as g:
                    sp.wait_ge(weights_lo, 2 * JT * g)
                    load_weights(g)
                with sp.Fori(0, BATCHES) as b:
                    sp.wait_ge(y_free, TPB * (steps_before_last + 1) + TPB * (b + 1))
                    store(b)
                sp.wait_ge(stored, 16 * BATCHES)

        @block.tensor
        def _(pe):
            def step(g, b, odd, tiles=JT):
                n = g * BATCHES + b
                before = tiles_before(g, b)
                tokens = bass.ds(b * TPB, TPB)
                for j in range(tiles):
                    q = (odd * JT + j) % 2
                    pe.wait_ge(gu_free, before + j + 1)
                    pe.wait_ge(weights_lo, 2 * JT * g + j + 1)
                    for m, ps in ((0, gate_ps[q]), (1, up_ps[q])):
                        for k in range(KT):
                            last = sums(pe, ps[:, :], up_hi[:, j, m, k, :], up_lo[:, j, m, k, :],
                                        x_hi[:, tokens, k, :], x_lo[:, tokens, k, :], k == 0, k == KT - 1)
                        last.then_inc(gu_ready, 1)
                for j in range(tiles):
                    pe.wait_ge(h_ready, before + j + 1)
                    pe.wait_ge(weights_lo, 2 * JT * g + JT + j + 1)
                    for t in range(TPB):
                        if j == 0:
                            pe.wait_ge(y_free, n * TPB + t + 1)
                        last = sums(pe, y_ps[t][:, :], h_hi[:, j, t * P:(t + 1) * P], h_lo[:, j, t * P:(t + 1) * P],
                                    down_hi[:, j, :], down_lo[:, j, :], j == 0, j == tiles - 1)
                        if j == tiles - 1:
                            last.then_inc(y_ready, 1)

            for b in range(BATCHES):
                pe.wait_ge(x_loaded[b], 32)
                step(0, b, b % 2)
            with pe.Fori(1, last_g) as g:
                if fp4:
                    for b in range(BATCHES):
                        step(g, b, b % 2)
                else:
                    with pe.Fori(0, BATCHES // 2) as pair:
                        step(g, 2 * pair, 0)
                        step(g, 2 * pair + 1, 1)
            for b in range(BATCHES):
                step(last_g, b, 0, LAST_JT)

        @block.scalar
        def _(act):
            def high_parts(g, first=False):
                if not fp4:
                    act.wait_ge(weights_loaded, 32 * (g + 1))
                for j in range(JT):
                    if fp4:
                        act.wait_ge(decoded, chunks * g + 2 * j + 2)
                    if not first:
                        act.wait_ge(gu_ready, 2 * JT * BATCHES * g - 2 * JT + 2 * j + 2)
                    act.copy(up_hi[:, j], up_f32[:, j]).then_inc(weights_hi, 1)
                    if first and fp4:
                        for c in range(2 * j + 4, min(2 * j + 6, chunks)):
                            curve(c, c)
                if not first:
                    act.wait_ge(y_ready, TPB * BATCHES * g)
                for j in range(JT):
                    if fp4:
                        act.wait_ge(decoded, chunks * g + 2 * JT + j + 1)
                    act.copy(down_hi[:, j, :], down_f32[:, j, :]).then_inc(weights_hi, 1)

            def curve(c_all, c):
                act.wait_ge(bits_ready, c_all + 1)
                act.activation(above4[:, :], magnitude[:, :], ACT.Relu, bias=bias_m4[:, :], scale=1.0)
                act.activation(above6[:, :], magnitude[:, :], ACT.Relu, bias=bias_m12[:, :], scale=2.0)
                act.activation(half_sign[:, :], sign_bit[:, :], ACT.Identity, bias=bias_half[:, :],
                               scale=-0.125).then_inc(lines_ready, 1)

            def step(g, b, odd, tiles=JT):
                for j in range(tiles):
                    q = (odd * JT + j) % 2
                    k = tiles_before(g, b) + j
                    act.wait_ge(gu_ready, 2 * k + 1)
                    act.activation(silu_g[:, q, :], gate_ps[q][:, :], ACT.Silu).then_inc(silu_ready, 1)
                    act.wait_ge(gu_free, k + 3)
                    act.copy(h_hi[:, j, :], h_f32[:, q, :]).then_inc(hhi_ready, 1)
                    if fp4 and tiles == JT:
                        c = b * JT + j
                        if c < chunks:
                            curve(chunks * (g + 1) + c, c)

            if fp4:
                act.wait_ge(bias_set, 3)
                for c in range(4):
                    curve(c, c)
            high_parts(0, first=True)
            if fp4:
                with act.Fori(0, last_g) as g:
                    for b in range(BATCHES):
                        step(g, b, b % 2)
                    high_parts(g + 1)
            else:
                with act.Fori(0, last_g) as g:
                    with act.Fori(0, BATCHES // 2) as pair:
                        step(g, 2 * pair, 0)
                        step(g, 2 * pair + 1, 1)
                    high_parts(g + 1)
            for b in range(BATCHES):
                step(last_g, b, 0, LAST_JT)

        @block.gpsimd
        def _(pool):
            def low_part(g, n):
                pool.wait_ge(weights_hi, 2 * JT * g + n + 1)
                whole, high, low = ((up_f32[:, n], up_hi[:, n], up_lo[:, n]) if n < JT else
                                    (down_f32[:, n - JT, :], down_hi[:, n - JT, :], down_lo[:, n - JT, :]))
                pool.tensor_tensor(low, whole, high.bitcast(F32), ALU.subtract).then_inc(weights_lo, 1)

            def scale_chunk(c_all, c):
                pool.wait_ge(value_ready, c_all + 1)
                to, shape = (up_f32[:, c // 2, c % 2], "p (k f) -> p k f") if c < 2 * JT else (down_f32[:, c - 2 * JT, :], None)
                values, by = value[:, :], scales[:, c % 2, :]
                if shape:
                    values, by = values.rearrange(shape, f=P), by.rearrange(shape, f=P)
                pool.tensor_tensor(to, values, by, ALU.mult).then_inc(decoded, 1)

            if fp4:
                pool.memset(power[:, :], -0.5).then_inc(power_set, 1)
                for c in range(chunks):
                    scale_chunk(c, c)
                    if c in (3, 5):
                        low_part(0, (c - 3) // 2)
                for n in range(2, 2 * JT):
                    low_part(0, n)
                with pool.Fori(0, last_g) as g:
                    pool.wait_ge(weights_lo, 2 * JT * (g + 1))
                    for c in range(chunks):
                        scale_chunk(chunks * (g + 1) + c, c)
                    for n in range(2 * JT):
                        low_part(g + 1, n)
                pool.wait_ge(power_set, 1)
                for b in range(BATCHES):
                    tiles = slice(b * TPB, (b + 1) * TPB)
                    pool.wait_ge(meansq_ready, TPB * (b + 1))
                    pool.tensor_scalar(meansq[:, tiles], meansq[:, tiles], 1.0 / D, 1e-6, ALU.mult, ALU.add).then_inc(rstd_step, 1)
                    pool.wait_ge(rstd_step, 2 * b + 1)
                    pool.tensor_tensor(rstd[:, tiles], meansq[:, tiles], power[:, tiles], ALU.pow).then_inc(rstd_step, 1)
            else:
                with pool.Fori(0, groups) as g:
                    for n in range(2 * JT):
                        low_part(g, n)

        @block.vector
        def _(dve):
            def bits(g, c):
                per_group = (chunks + 1 - c % 2) // 2
                dve.wait_ge(chunk_loaded[c % 2], 32 * (per_group * g + c // 2 + 1))
                for to, mask in ((magnitude, 7), (sign_bit, 8)):
                    last = dve.tensor_scalar(to[:, :], words[:, c % 2, :], shift[:, :], mask,
                                             ALU.logical_shift_right, ALU.bitwise_and)
                last.then_inc(bits_ready, 1)

            def values(g, c):
                c_all = chunks * g + c
                dve.wait_ge(bits_ready, c_all + 1)
                dve.wait_ge(lines_ready, c_all + 1)
                dve.tensor_tensor(twice[:, :], magnitude[:, :], above4[:, :], ALU.add).then_inc(dq_step, 1)
                dve.wait_ge(dq_step, 2 * c_all + 1)
                dve.tensor_tensor(twice[:, :], twice[:, :], above6[:, :], ALU.add).then_inc(dq_step, 1)
                dve.wait_ge(dq_step, 2 * c_all + 2)
                if not (isinstance(c_all, int) and c_all == 0):
                    dve.wait_ge(decoded, c_all)
                dve.tensor_tensor(value[:, :], twice[:, :], half_sign[:, :], ALU.mult).then_inc(value_ready, 1)

            def step(g, b, odd, tiles=JT):
                n = g * BATCHES + b
                for j in range(tiles):
                    q = (odd * JT + j) % 2
                    k = tiles_before(g, b) + j
                    dve.wait_ge(silu_ready, k + 1)
                    dve.wait_ge(gu_ready, 2 * k + 2)
                    dve.tensor_tensor(h_f32[:, q, :], silu_g[:, q, :], up_ps[q][:, :], ALU.mult).then_inc(gu_free, 1)
                    dve.wait_ge(gu_free, k + 3)
                    dve.wait_ge(hhi_ready, k + 1)
                    dve.tensor_tensor(h_lo[:, j, :], h_f32[:, q, :], h_hi[:, j, :].bitcast(F32),
                                      ALU.subtract).then_inc(h_ready, 1)
                    if fp4 and tiles == JT:
                        c = b * JT + j
                        if 1 <= c <= chunks:
                            values(g + 1, c - 1)
                        if c < chunks:
                            bits(g + 1, c)
                for t in range(TPB):
                    tile = acc[:, bass.ds(b * TPB + t, 1), :].rearrange("p o n -> p (o n)")
                    dve.wait_ge(y_ready, n * TPB + t + 1)
                    dve.wait_ge(y_free, n * TPB + t + 1)
                    if fp4:
                        dve.tensor_tensor(tile, tile, y_ps[t][:, :], ALU.add).then_inc(y_free, 1)
                    else:
                        by = comb[:, bass.ds(b * TPB + t, 1), bass.ds(g, 1)].rearrange("p o n -> p (o n)")
                        dve.scalar_tensor_tensor(tile, y_ps[t][:, :], by, tile, ALU.mult, ALU.add).then_inc(y_free, 1)

            def squares(b):
                for i in range(TPB):
                    t = b * TPB + i
                    dve.wait_ge(y_free, TPB * (steps_before_last + 1) + t + 1)
                    if t:
                        dve.wait_ge(meansq_ready, t)
                    dve.tensor_tensor_reduce(square[:, :], acc[:, t, :], acc[:, t, :], 1.0, 0.0, ALU.mult, ALU.add,
                                             meansq[:, t:t + 1]).then_inc(meansq_ready, 1)

            def finish(b):
                dve.wait_ge(rstd_step, 2 * (b + 1))
                dve.wait_ge(resid_loaded, 16 * (b + 1))
                for i in range(TPB):
                    t = b * TPB + i
                    dve.scalar_tensor_tensor(acc[:, t, :], acc[:, t, :], rstd[:, t:t + 1], resid[:, i, :],
                                             ALU.mult, ALU.add).then_inc(final, 1)

            dve.sem_inc(gu_free, 2)
            if fp4:
                dve.memset(bias_m4[:, :], -4.0).then_inc(bias_set, 1)
                dve.memset(bias_m12[:, :], -12.0).then_inc(bias_set, 1)
                dve.memset(bias_half[:, :], 0.5).then_inc(bias_set, 1)
                dve.wait_ge(aux_loaded, 16)
                for c in range(chunks):
                    bits(0, c)
                    values(0, c)
                dve.memset(acc[:, :, :], 0.0).then_inc(y_free, TPB)
                with dve.Fori(0, last_g) as g:
                    for b in range(BATCHES):
                        step(g, b, b % 2)
                for b in range(BATCHES):
                    step(last_g, b, 0, LAST_JT)
                    squares(b)
                    if b:
                        finish(b - 1)
                finish(BATCHES - 1)
            else:
                dve.sem_inc(y_free, TPB)
                dve.wait_ge(aux_loaded, 32)
                with dve.Fori(0, last_g) as g:
                    with dve.Fori(0, BATCHES // 2) as pair:
                        step(g, 2 * pair, 0)
                        step(g, 2 * pair + 1, 1)
                for b in range(BATCHES):
                    step(last_g, b, 0, LAST_JT)


SSM_HEADS = 16
SSM_P = 64
SSM_N = 64
E = SSM_HEADS * SSM_P
ET = E // P
TAPS = 4
CONV_TILES = ET + 2
EXPERTS = 8
SMALL = SSM_HEADS + EXPERTS + 2
HB = E // BANK
HPG = BANK // P
CONV_ORDER = (ET, ET + 1) + tuple(range(ET))
ATANH = tuple(1.0 / (2 * n + 1) for n in range(1, 8))


def ssm_phase(nc, x_dram, wts, tables, x_parts, out_dram, comb_dram):
    name = "a1"
    semaphores = []
    with ExitStack() as ctx:
        ctx.callback(clear_semaphores, nc, semaphores)

        def sb(label, shape, dt=F32):
            return ctx.enter_context(nc.sbuf_tensor(f"{name}_{label}", shape, dt))

        def sem(label):
            semaphores.append(nc.alloc_semaphore(f"{name}_{label}"))
            return semaphores[-1]

        def sems(group, labels):
            return {label: sem(f"{group}_{label}") for label in labels.split()}

        z_hi = sb("z_hi", [P, KT, E], F32R)
        z_lo = sb("z_lo", [P, KT, E], F32R)
        c_hi = sb("c_hi", [P, KT, E + 2 * SSM_N], F32R)
        c_lo = sb("c_lo", [P, KT, E + 2 * SSM_N], F32R)
        small_raw = sb("small_raw", [P, KT, SMALL])
        small_hi = sb("small_hi", [P, KT, SMALL], F32R)
        small_lo = sb("small_lo", [P, KT, SMALL], F32R)
        w_raw = sb("w_raw", [P, 2, KT, P])
        w_out = sb("w_out", [P, ET, D])
        norm_w = sb("norm_w", [P, ET])
        conv_w = sb("conv_w", [P, CONV_TILES, TAPS])
        conv_b = sb("conv_b", [P, CONV_TILES])
        dt_bias = sb("dt_bias", [P, SSM_HEADS])
        a_neg = sb("a_neg", [P, SSM_HEADS])
        skip_d = sb("skip_d", [P, SSM_HEADS])
        ident = sb("ident", [P, P])
        upto = sb("upto", [P, P])
        after = sb("after", [P, P])
        ones = sb("ones", [P, P])
        earlier = sb("earlier", [P, EXPERTS, EXPERTS])
        power = sb("power", [P, 1])
        eps_ln = sb("eps_ln", [P, 1])
        eps_rms = sb("eps_rms", [P, 1])

        x = sb("x", [P, TPB, D])
        x_last = sb("x_last", [P, D])
        stats = sb("stats", [P, TPB, 6])
        mean_var = sb("mean_var", [P, TPB, 2])
        ln_tmp = sb("ln_tmp", [P, TPB])
        ln_rs = sb("ln_rs", [P, TPB])
        ln_tmp2 = sb("ln_tmp2", [P, 1])
        xn = sb("xn", [P, 2, D])
        xt_hi = sb("xt_hi", [P, TPB, KT, P], F32R)
        xt_lo = sb("xt_lo", [P, TPB, KT, P], F32R)
        tph = [P, TPB, SSM_HEADS]
        dt_raw, dt_abs, dt_exp, dt_den, dt_z, dt_z2, dt_q, dt_pos, dt, a = (
            sb(label, tph) for label in
            ("dt_raw", "dt_abs", "dt_exp", "dt_den", "dt_z", "dt_z2", "dt_q", "dt_pos", "dt", "a"))
        decays = sb("decays", [P, 3, TPB, SSM_HEADS])
        logits = sb("logits", [P, TPB, EXPERTS + 1])
        top = sb("top", [P, TPB])
        probs = sb("probs", [P, TPB, EXPERTS])
        total = sb("total", [P, TPB])
        greater = sb("greater", [P, TPB, EXPERTS, EXPERTS])
        equal = sb("equal", [P, TPB, EXPERTS, EXPERTS])
        rank = sb("rank", [P, TPB, EXPERTS])
        shared = sb("shared", [P, TPB])
        comb = sb("comb", [P, TPB, EXPERTS + 4])

        conv_acc = sb("conv_acc", [P, 2, BT])
        conv = sb("conv", [P, CONV_TILES, BT])
        b_tok = sb("b_tok", [P, TPB, SSM_N])
        g_mask = sb("g_mask", [P, TPB, P])
        a_mask = sb("a_mask", [P, SSM_HEADS, P])
        l_exp = sb("l_exp", [P, 2, HPG, P])
        m_t = sb("m_t", [P, SSM_HEADS, P])
        h_tok = sb("h_tok", [P, SSM_HEADS, SSM_P])
        h_dt = sb("h_dt", [P, SSM_HEADS, SSM_P])
        h_dec = sb("h_dec", [P, SSM_HEADS, SSM_P])
        z_silu = sb("z_silu", [P, E])
        y = sb("y", [P, SSM_HEADS, SSM_P])
        sq_out = sb("sq_out", [P, E], BF16)
        ss = sb("ss", [P, 1])
        ms = sb("ms", [P, 1])
        y_rs = sb("y_rs", [P, 1])
        yt = sb("yt", [P, ET, P])
        state = sb("state", [SSM_N, SSM_HEADS, SSM_P])

        def banks(label):
            return ctx.enter_context(nc.psum_tensor(f"{name}_{label}", [P, 2, BANK], F32))

        seg_ps, y_ps, off_ps, proj_ps = banks("seg_ps"), banks("y_ps"), banks("off_ps"), banks("proj_ps")

        loaded = sems("loaded", "const")
        w = sems("w", "hi split small normed a consts")
        ln = sems("ln", "stats_step stats rstd normed")
        xt = sems("xt", "ps hi lo")
        sm = sems("sm", "ps dt_raw logits abs exp step dt a")
        rt = sems("rt", "step exp tanh rank ready")
        cv = sems("cv", "ps init step done silu")
        bc = sems("bc", "g_ps g_masked b_ps b_tok cum_ps decays")
        sg = sems("sg", "a_mask ps exp m")
        zz = sems("zz", "ps silu")
        hh = sems("hh", "ps tok dt dec skip")
        yy = sems("yy", "diag_ps off_ps off_scaled diag_added skip_added gated ss ms rs t_ps t_sb out_ps x_added")
        st = sems("st", "ps scaled ready")
        x_in = [sem(f"x_in{n}") for n in range(TPB)]
        last_in = sem("last_in")
        y_stored = [sem(f"y_stored{n}") for n in range(TPB)]
        xt_stored = sem("xt_stored")
        comb_stored = sem("comb_stored")
        w_loaded = [sem(f"w_loaded{n}") for n in range(2)]
        out_loaded = sem("out_loaded")

        Z_PIECES, C_PIECES = E // P, E // P + 1
        PIECES = Z_PIECES + C_PIECES
        N_CONST = 12

        def piece(hi_or_lo, n):
            z, c = hi_or_lo
            return z[:, :, n * P:(n + 1) * P] if n < Z_PIECES else c[:, :, (n - Z_PIECES) * P:(n - Z_PIECES + 1) * P]

        def heads(ap, n_inner):
            return ap.unsqueeze(2).to_broadcast([ap.shape[0], SSM_HEADS, n_inner])

        block = ctx.enter_context(nc.Block())

        def whole(bank_pair):
            return bank_pair[:, :, :].rearrange("p b n -> p (b n)").rearrange("p (h d) -> p h d", h=SSM_HEADS)

        @block.sync
        def _(sp):
            def load_x(batch, i):
                sp.dma_start(x[:, i, :], x_dram[bass.ds(batch * TPB + i, 1)].rearrange("o p n -> (o p) n")
                             ).then_inc(x_in[i], 16)

            def load_last(batch):
                sp.dma_start(x_last[:, :], x_dram[bass.ds(batch * TPB + TPB - 1, 1)].rearrange("o p n -> (o p) n")
                             ).then_inc(last_in, 16)

            def store_batch_parts(b):
                sp.wait_ge(xt["hi"], TPB * b + TPB)
                sp.wait_ge(xt["lo"], TPB * b + TPB)
                for part, buf in ((0, xt_hi), (1, xt_lo)):
                    sp.dma_start(x_parts[part, bass.ds(b * TPB, TPB)].rearrange("t p n -> p t n"),
                                 buf[:, :, :, :].bitcast(F32).rearrange("p t k n -> p t (k n)")).then_inc(xt_stored, 16)

            def store_y(b, i):
                sp.wait_ge(yy["x_added"], b * TPB + i + 1)
                src = x_last[:, :] if i == TPB - 1 else x[:, i, :]
                sp.dma_start(out_dram[bass.ds(b * TPB + i, 1)].rearrange("o p n -> (o p) n"), src).then_inc(y_stored[i], 16)
                sp.wait_ge(y_stored[i], 16 * b + 16)

            def store_comb(b):
                sp.wait_ge(rt["ready"], b + 1)
                sp.dma_start(comb_dram[:, bass.ds(b * TPB, TPB), :], comb[:, :, :]).then_inc(comb_stored, 16)

            for i in range(TPB):
                load_x(0, i)
            consts = ((ident, tables["ident"]), (small_raw, wts["small"]), (conv_w, wts["conv_w"]), (conv_b, wts["conv_b"]),
                      (dt_bias, wts["dt_bias"].partition_broadcast(P)), (a_neg, wts["a_log"].partition_broadcast(P)),
                      (skip_d, wts["skip_d"].partition_broadcast(P)), (norm_w, wts["norm_w"]),
                      (upto, tables["upto"]), (after, tables["after"]), (ones, tables["ones"]),
                      (earlier, tables["earlier"].partition_broadcast(P)))
            assert len(consts) == N_CONST
            for dst, src in consts:
                sp.dma_start(dst[:], src).then_inc(loaded["const"], 16)
            load_last(0)
            for m in range(PIECES):
                n = piece_order(m, Z_PIECES, PIECES)
                if m >= 2:
                    sp.wait_ge(w["split"], m - 1)
                sp.dma_start(w_raw[:, m % 2, :, :], wts["in_proj"][n]).then_inc(w_loaded[m % 2], 16)
                if m == 1:
                    sp.dma_start(w_out[:, :, :], wts["out_proj"]).then_inc(out_loaded, 16)
            store_batch_parts(0)
            sp.wait_ge(ln["normed"], TPB)
            load_x(1, 3)

            def body(b, last):
                store_comb(b)
                for i in range(TPB - 1):
                    store_y(b, i)
                    if not last:
                        load_x(b + 1, i)
                if not last:
                    store_batch_parts(b + 1)
                    sp.wait_ge(ln["normed"], TPB * (b + 2))
                    load_x((b + 2) % BATCHES, 3)
                store_y(b, TPB - 1)
                if not last:
                    load_last(b + 1)

            with sp.Fori(0, BATCHES - 1) as b:
                body(b, False)
            body(BATCHES - 1, True)
            sp.wait_ge(comb_stored, 16 * BATCHES)
            sp.wait_ge(xt_stored, 32 * BATCHES)
            sp.wait_ge(x_in[3], 16 * (BATCHES + 1))

        @block.tensor
        def _(pe):
            def sums(to, l_hi, l_lo, r_hi, r_lo, k):
                pe.matmul(to, l_hi, r_hi, start=k == 0, stop=False)
                pe.matmul(to, l_hi, r_lo, start=False, stop=False)
                return pe.matmul(to, l_lo, r_hi, start=False, stop=k == KT - 1)

            def x_turned(b, first):
                for i in range(TPB):
                    pe.wait_ge(ln["normed"], TPB * b + i + 1)
                    if i >= 2:
                        pe.wait_ge(xt["hi"], TPB * b + i - 1)
                        pe.wait_ge(xt["lo"], TPB * b + i - 1)
                    elif not first:
                        pe.wait_ge(sg["exp"], HPG * TPB * b)
                    for k in range(KT):
                        last = pe.transpose(seg_ps[:, i % 2, k * P:(k + 1) * P], xn[:, i % 2, k * P:(k + 1) * P], ident[:, :])
                    last.then_inc(xt["ps"], 1)
                pe.wait_ge(xt["hi"], TPB * (b + 1))
                pe.wait_ge(xt["lo"], TPB * (b + 1))

            def small_proj(b):
                for i in range(TPB):
                    for k in range(KT):
                        last = sums(seg_ps[:, 0, i * SMALL:(i + 1) * SMALL], xt_hi[:, i, k, :], xt_lo[:, i, k, :],
                                    small_hi[:, k, :], small_lo[:, k, :], k)
                last.then_inc(sm["ps"], 1)

            def conv_proj(b, q, first):
                f = CONV_ORDER[q]
                rows, cols = (P, slice(f * P, (f + 1) * P)) if f < ET else (
                    SSM_N, slice(E + (f - ET) * SSM_N, E + (f - ET + 1) * SSM_N))
                if q >= 2:
                    pe.wait_ge(cv["done"], CONV_TILES * b + q - 1)
                elif not first:
                    pe.wait_ge(hh["tok"], HB * TPB * b)
                for k in range(KT):
                    last = sums(proj_ps[0:rows, q % 2, :], c_hi[:, k, cols], c_lo[:, k, cols], xt_hi[:, :, k, :], xt_lo[:, :, k, :], k)
                last.then_inc(cv["ps"], 1)

            def grams(b):
                pe.wait_ge(cv["silu"], CONV_TILES * b + 2)
                pe.wait_ge(sm["logits"], b + 1)
                for i in range(TPB):
                    cols = slice(i * P, (i + 1) * P)
                    last = pe.matmul(seg_ps[:, 1, cols], conv[0:SSM_N, ET, cols], conv[0:SSM_N, ET + 1, cols], start=True, stop=True)
                last.then_inc(bc["g_ps"], 1)
                for i in range(TPB):
                    last = pe.transpose(seg_ps[:, 0, i * SSM_N:(i + 1) * SSM_N], conv[0:SSM_N, ET, i * P:(i + 1) * P],
                                        ident[0:SSM_N, 0:SSM_N])
                last.then_inc(bc["b_ps"], 1)

            def cumulate(b):
                pe.wait_ge(sm["a"], b + 1)
                pe.wait_ge(bc["b_tok"], b + 1)
                n = TPB * SSM_HEADS
                for m, mask in enumerate((after, upto, ones)):
                    last = pe.matmul(seg_ps[:, 0, m * n:(m + 1) * n], mask[:, :], a[:, :, :].rearrange("p t h -> p (t h)"),
                                     start=True, stop=True)
                last.then_inc(bc["cum_ps"], 1)

            def segments(t, i, b):
                pe.wait_ge(sg["a_mask"], t + 1)
                for g in range(HPG):
                    if g >= 2:
                        pe.wait_ge(sg["exp"], HPG * t + g - 1)
                    elif i:
                        pe.wait_ge(sg["exp"], HPG * t - 1 + g)
                    elif g == 0:
                        pe.wait_ge(bc["decays"], b + 1)
                    else:
                        pe.wait_ge(bc["g_masked"], b + 1)
                    pe.matmul(seg_ps[:, g % 2, :], after[:, :], a_mask[:, g * HPG:(g + 1) * HPG, :],
                              start=True, stop=True).then_inc(sg["ps"], 1)

            def z_proj(t, i, b):
                for half in range(HB):
                    if i:
                        pe.wait_ge(hh["tok"], HB * t - 1 + half)
                    else:
                        pe.wait_ge(cv["done"], CONV_TILES * b + CONV_TILES - 1 + half)
                    for k in range(KT):
                        cols = slice(half * BANK, (half + 1) * BANK)
                        last = sums(proj_ps[:, half, :], xt_hi[:, i, k, :], xt_lo[:, i, k, :], z_hi[:, k, cols], z_lo[:, k, cols], k)
                    last.then_inc(zz["ps"], 1)

            def h_turned(t, i, b):
                if i == 0:
                    pe.wait_ge(cv["silu"], CONV_TILES * (b + 1))
                for half in range(HB):
                    pe.wait_ge(zz["silu"], HB * t + half + 1)
                    for f in range(ET // HB):
                        last = pe.transpose(proj_ps[:, half, f * P:(f + 1) * P],
                                            conv[:, half * (ET // HB) + f, i * P:(i + 1) * P], ident[:, :])
                    last.then_inc(hh["ps"], 1)

            def y_turned(t):
                pe.wait_ge(yy["gated"], t + 1)
                for f in range(ET):
                    last = pe.transpose(y_ps[:, f // HPG, (f % HPG) * P:(f % HPG + 1) * P],
                                        y[:, 2 * f:2 * f + 2, :].rearrange("p h d -> p (h d)"), ident[:, :])
                last.then_inc(yy["t_ps"], 1)

            def out_proj(t):
                pe.wait_ge(yy["t_sb"], t + 1)
                for f in range(ET):
                    last = pe.matmul(off_ps[:, 0, :], yt[:, f, :], w_out[:, f, :], start=f == 0, stop=f == ET - 1)
                last.then_inc(yy["out_ps"], 1)

            def project_batch(b, before):
                first = before is None
                x_turned(b, first)
                small_proj(b)
                for q in range(CONV_TILES):
                    conv_proj(b, q, first)
                    if q == 3 and not first:
                        y_turned(before)
                    if q == 4:
                        grams(b)
                    if q == 6 and not first:
                        out_proj(before)
                cumulate(b)

            def ahead(t, i, b):
                segments(t, i, b)
                z_proj(t, i, b)
                h_turned(t, i, b)

            pe.wait_ge(loaded["const"], 16 * N_CONST)
            pe.wait_ge(w["split"], PIECES)
            pe.wait_ge(w["small"], 1)
            project_batch(0, None)
            ahead(0, 0, 0)

            def body(b, last):
                for i in range(TPB):
                    t = b * TPB + i
                    if i:
                        pe.wait_ge(st["ready"], 3 * b + i)
                        pe.wait_ge(yy["x_added"], t)
                        for half in range(HB):
                            mm = pe.matmul(off_ps[:, half, :], conv[0:SSM_N, ET + 1, i * P:(i + 1) * P],
                                           state[:, half * 8:(half + 1) * 8, :], start=True, stop=True)
                        mm.then_inc(yy["off_ps"], 1)
                    pe.wait_ge(sg["m"], HPG * (t + 1))
                    pe.wait_ge(hh["dt"], t + 1)
                    if not (isinstance(b, int) and b == 0 and i == 0) and i:
                        pe.wait_ge(yy["t_sb"], t)
                    for h in range(SSM_HEADS):
                        mm = pe.matmul(y_ps[:, h // 8, (h % 8) * SSM_P:(h % 8 + 1) * SSM_P], m_t[:, h, :], h_dt[:, h, :],
                                       start=True, stop=True)
                    mm.then_inc(yy["diag_ps"], 1)
                    if i < TPB - 1:
                        segments(t + 1, i + 1, b)
                        pe.wait_ge(hh["dec"], t + 1)
                        if i:
                            pe.wait_ge(yy["off_scaled"], 3 * b + i)
                        for half in range(HB):
                            mm = pe.matmul(off_ps[0:SSM_N, half, :], b_tok[:, i, :], h_dec[:, half * 8:(half + 1) * 8, :],
                                           start=True, stop=True)
                        mm.then_inc(st["ps"], 1)
                        z_proj(t + 1, i + 1, b)
                        h_turned(t + 1, i + 1, b)
                        y_turned(t)
                        pe.wait_ge(st["ready"], 3 * b + i + 1)
                        out_proj(t)
                    elif last:
                        y_turned(t)
                        out_proj(t)
                    else:
                        project_batch(b + 1, t)
                        ahead(t + 1, 0, b + 1)

            with pe.Fori(0, BATCHES - 1) as b:
                body(b, False)
            body(BATCHES - 1, True)

        @block.scalar
        def _(act):
            def project_batch(b, before):
                first = before is None
                if not first:
                    act.wait_ge(zz["ps"], HB * TPB * b)
                    act.wait_ge(xt_stored, 32 * b)
                for i in range(TPB):
                    act.wait_ge(xt["ps"], TPB * b + i + 1)
                    act.copy(xt_hi[:, i, :, :], seg_ps[:, i % 2, :].rearrange("p (k n) -> p k n", k=KT)).then_inc(xt["hi"], 1)
                act.wait_ge(sm["dt_raw"], b + 1)
                act.activation(dt_abs[:, :, :], dt_raw[:, :, :], ACT.Abs).then_inc(sm["abs"], 1)
                act.wait_ge(sm["abs"], b + 1)
                act.activation(dt_exp[:, :, :], dt_abs[:, :, :], ACT.Exp, scale=-1.0).then_inc(sm["exp"], 1)
                act.wait_ge(rt["step"], 7 * b + 2)
                act.activation(probs[:, :, :], logits[:, :, 0:EXPERTS], ACT.Exp).then_inc(rt["exp"], 1)
                act.activation(shared[:, :], logits[:, :, EXPERTS], ACT.Tanh, scale=0.5).then_inc(rt["tanh"], 1)
                for q in range(CONV_TILES + 1):
                    if q < CONV_TILES:
                        f = CONV_ORDER[q]
                        rows = slice(0, P if f < ET else SSM_N)
                        act.wait_ge(cv["ps"], CONV_TILES * b + q + 1)
                        if q >= 2:
                            act.wait_ge(cv["silu"], CONV_TILES * b + q - 1)
                        act.activation(conv_acc[rows, q % 2, :], proj_ps[rows, q % 2, :], ACT.Identity,
                                       bias=conv_b[rows, f:f + 1], scale=conv_w[rows, f, TAPS - 1:TAPS]).then_inc(cv["init"], 1)
                    if q:
                        f = CONV_ORDER[q - 1]
                        rows = slice(0, P if f < ET else SSM_N)
                        act.wait_ge(cv["done"], CONV_TILES * b + q)
                        act.activation(conv[rows, f, :], conv_acc[rows, (q - 1) % 2, :], ACT.Silu).then_inc(cv["silu"], 1)
                    if q == 3 and not first:
                        y_out(before)
                    if q == 5:
                        act.wait_ge(bc["b_ps"], b + 1)
                        act.copy(b_tok[:, :, :], seg_ps[:, 0, 0:TPB * SSM_N].rearrange("p (t n) -> p t n", t=TPB)
                                 ).then_inc(bc["b_tok"], 1)
                act.wait_ge(bc["cum_ps"], b + 1)
                act.activation(decays[:, :, :, :].rearrange("p m t h -> p (m t h)"), seg_ps[:, 0, 0:3 * TPB * SSM_HEADS],
                               ACT.Exp).then_inc(bc["decays"], 1)

            def segments(t):
                for g in range(HPG):
                    act.wait_ge(sg["ps"], HPG * t + g + 1)
                    if not (isinstance(t, int) and t == 0 and g < 2):
                        act.wait_ge(sg["m"], HPG * t + g - 1)
                    act.activation(l_exp[:, g % 2, :, :], seg_ps[:, g % 2, :].rearrange("p (h l) -> p h l", h=HPG),
                                   ACT.Exp).then_inc(sg["exp"], 1)

            def ahead(t):
                if not (isinstance(t, int) and t == 0):
                    act.wait_ge(yy["gated"], t)
                for half in range(HB):
                    act.wait_ge(zz["ps"], HB * t + half + 1)
                    act.activation(z_silu[:, half * BANK:(half + 1) * BANK], proj_ps[:, half, :], ACT.Silu).then_inc(zz["silu"], 1)
                if not (isinstance(t, int) and t == 0):
                    act.wait_ge(yy["skip_added"], t)
                    act.wait_ge(hh["dec"], t)
                for half in range(HB):
                    act.wait_ge(hh["ps"], HB * t + half + 1)
                    act.copy(h_tok[:, half * 8:(half + 1) * 8, :], proj_ps[:, half, :].rearrange("p (h d) -> p h d", d=SSM_P)
                             ).then_inc(hh["tok"], 1)

            def square(t):
                act.wait_ge(yy["gated"], t + 1)
                if not (isinstance(t, int) and t == 0):
                    act.wait_ge(yy["ms"], t)
                act.activation(sq_out[:, :], y[:, :, :].rearrange("p h d -> p (h d)"), ACT.Square,
                               accum_out=ss[:, :]).then_inc(yy["ss"], 1)

            def y_out(t):
                act.wait_ge(yy["t_ps"], t + 1)
                act.copy(yt[:, :, :], y_ps[:, :, :].rearrange("p b (f n) -> p (b f) n", n=P)).then_inc(yy["t_sb"], 1)

            act.wait_ge(w["consts"], 3)
            for m in range(PIECES):
                n = piece_order(m, Z_PIECES, PIECES)
                act.wait_ge(w_loaded[m % 2], 16 * (m // 2 + 1))
                act.copy(piece((z_hi, c_hi), n), w_raw[:, m % 2, :, :]).then_inc(w["hi"], 1)
            act.wait_ge(loaded["const"], 16 * N_CONST)
            act.copy(small_hi[:, :, :], small_raw[:, :, :]).then_inc(w["hi"], 1)
            act.activation(a_neg[:, :], a_neg[:, :], ACT.Exp).then_inc(w["a"], 1)
            project_batch(0, None)
            segments(0)
            ahead(0)

            def body(b, last):
                for i in range(TPB):
                    t = b * TPB + i
                    if i < TPB - 1:
                        segments(t + 1)
                        square(t)
                        ahead(t + 1)
                        y_out(t)
                    elif last:
                        square(t)
                        y_out(t)
                    else:
                        square(t)
                        project_batch(b + 1, t)
                        segments(t + 1)
                        ahead(t + 1)

            with act.Fori(0, BATCHES - 1) as b:
                body(b, False)
            body(BATCHES - 1, True)

        @block.gpsimd
        def _(pool):
            def rstd_batch(b):
                pool.wait_ge(ln["stats"], TPB * (b + 1))
                pool.tensor_tensor(ln_tmp[:, :], mean_var[:, :, 1], eps_ln[:, :].to_broadcast([P, TPB]), ALU.add).then_inc(ln["rstd"], 1)
                pool.wait_ge(ln["rstd"], 2 * b + 1)
                pool.tensor_tensor(ln_rs[:, :], ln_tmp[:, :], power[:, :].to_broadcast([P, TPB]), ALU.pow).then_inc(ln["rstd"], 1)

            def mask_a(t, i, b):
                if i == 0:
                    pool.wait_ge(sm["a"], b + 1)
                if not (isinstance(t, int) and t == 0):
                    pool.wait_ge(sg["ps"], HPG * t)
                pool.tensor_tensor(a_mask[:, :, :], heads(a[:, i, :], P), upto[:, :].unsqueeze(1).to_broadcast([P, SSM_HEADS, P]),
                                   ALU.mult).then_inc(sg["a_mask"], 1)

            def h_products(t, i, b):
                pool.wait_ge(hh["tok"], HB * (t + 1))
                if not (isinstance(t, int) and t == 0):
                    pool.wait_ge(yy["diag_ps"], t)
                pool.tensor_tensor(h_dt[:, :, :], h_tok[:, :, :], heads(dt[:, i, :], SSM_P), ALU.mult).then_inc(hh["dt"], 1)
                pool.wait_ge(hh["dt"], t + 1)
                if i == 0:
                    pool.wait_ge(bc["decays"], b + 1)
                if i:
                    pool.wait_ge(st["ps"], 3 * b + i)
                pool.tensor_tensor(h_dec[:, :, :], h_dt[:, :, :], heads(decays[:, 0, i, :], SSM_P), ALU.mult).then_inc(hh["dec"], 1)
                pool.tensor_tensor(h_tok[:, :, :], h_tok[:, :, :], heads(skip_d[:, :], SSM_P), ALU.mult).then_inc(hh["skip"], 1)

            def rms(t):
                pool.wait_ge(yy["ss"], t + 1)
                pool.tensor_tensor(ms[:, :], ss[:, :], eps_rms[:, :], ALU.add).then_inc(yy["ms"], 1)
                pool.wait_ge(yy["ms"], t + 1)
                if not (isinstance(t, int) and t == 0):
                    pool.wait_ge(yy["x_added"], t)
                pool.tensor_tensor(y_rs[:, :], ms[:, :], power[:, :], ALU.pow).then_inc(yy["rs"], 1)

            pool.memset(power[:, :], -0.5).then_inc(w["consts"], 1)
            pool.memset(eps_ln[:, :], 1e-5).then_inc(w["consts"], 1)
            pool.memset(eps_rms[:, :], E * 1e-6).then_inc(w["consts"], 1)
            pool.wait_ge(w["consts"], 3)
            rstd_batch(0)
            pool.wait_ge(loaded["const"], 16 * N_CONST)
            mask_a(0, 0, 0)
            h_products(0, 0, 0)
            mask_a(1, 1, 0)

            def body(b, last):
                for i in range(TPB):
                    t = b * TPB + i
                    if i in (1, 2):
                        pool.wait_ge(yy["off_ps"], 3 * b + i)
                        pool.tensor_tensor(state[:, :, :], state[:, :, :], heads(decays[0:SSM_N, 2, i, :], SSM_P),
                                           ALU.mult).then_inc(st["scaled"], 1)
                    if i == TPB - 1 and not last:
                        rstd_batch(b + 1)
                    rms(t)
                    if i < TPB - 1:
                        h_products(t + 1, i + 1, b)
                        if i < TPB - 2:
                            mask_a(t + 2, i + 2, b)
                    elif not last:
                        mask_a(t + 1, 0, b + 1)
                        h_products(t + 1, 0, b + 1)
                        mask_a(t + 2, 1, b + 1)

            with pool.Fori(0, BATCHES - 1) as b:
                body(b, False)
            body(BATCHES - 1, True)

        @block.vector
        def _(dve):
            def softplus(b):
                dve.wait_ge(sm["ps"], b + 1)
                small = seg_ps[:, 0, 0:TPB * SMALL].rearrange("p (t c) -> p t c", t=TPB)
                dve.tensor_tensor(dt_raw[:, :, :], small[:, :, 0:SSM_HEADS], dt_bias[:, :].unsqueeze(1).to_broadcast(tph),
                                  ALU.add).then_inc(sm["dt_raw"], 1)
                dve.tensor_copy(logits[:, :, :], small[:, :, SSM_HEADS:SSM_HEADS + EXPERTS + 1]).then_inc(sm["logits"], 1)
                dve.wait_ge(sm["dt_raw"], b + 1)
                STEPS = 5 + len(ATANH)
                n = [STEPS * b]

                def step(ins):
                    ins.then_inc(sm["step"], 1)
                    n[0] = n[0] + 1
                    dve.wait_ge(sm["step"], n[0])

                dve.tensor_scalar(dt_pos[:, :, :], dt_raw[:, :, :], 0.0, None, ALU.max)
                softmax_max(b)
                dve.wait_ge(sm["exp"], b + 1)
                step(dve.tensor_scalar(dt_den[:, :, :], dt_exp[:, :, :], 2.0, None, ALU.add))
                step(dve.reciprocal(dt_den[:, :, :], dt_den[:, :, :]))
                step(dve.tensor_tensor(dt_z[:, :, :], dt_exp[:, :, :], dt_den[:, :, :], ALU.mult))
                step(dve.tensor_tensor(dt_z2[:, :, :], dt_z[:, :, :], dt_z[:, :, :], ALU.mult))
                step(dve.tensor_scalar(dt_q[:, :, :], dt_z2[:, :, :], ATANH[-1], None, ALU.mult))
                for c in ATANH[-2::-1]:
                    step(dve.scalar_tensor_tensor(dt_q[:, :, :], dt_q[:, :, :], c, dt_z2[:, :, :], ALU.add, ALU.mult))
                step(dve.scalar_tensor_tensor(dt_q[:, :, :], dt_q[:, :, :], 1.0, dt_z[:, :, :], ALU.add, ALU.mult))
                dve.scalar_tensor_tensor(dt[:, :, :], dt_q[:, :, :], 2.0, dt_pos[:, :, :], ALU.mult, ALU.add).then_inc(sm["dt"], 1)
                dve.wait_ge(sm["dt"], b + 1)
                dve.scalar_tensor_tensor(a[:, :, :], dt[:, :, :], -1.0, a_neg[:, :].unsqueeze(1).to_broadcast(tph),
                                         ALU.mult, ALU.mult).then_inc(sm["a"], 1)

            def softmax_max(b):
                dve.wait_ge(sm["logits"], b + 1)
                dve.tensor_reduce(top[:, :], logits[:, :, 0:EXPERTS], AX_X, ALU.max).then_inc(rt["step"], 1)
                dve.wait_ge(rt["step"], 7 * b + 1)
                dve.tensor_tensor(logits[:, :, 0:EXPERTS], logits[:, :, 0:EXPERTS],
                                  top[:, :].unsqueeze(2).to_broadcast([P, TPB, EXPERTS]), ALU.subtract).then_inc(rt["step"], 1)

            def route(b):
                pairs = [P, TPB, EXPERTS, EXPERTS]
                dve.wait_ge(rt["exp"], b + 1)
                dve.tensor_reduce(total[:, :], probs[:, :, :], AX_X, ALU.add).then_inc(rt["step"], 1)
                dve.wait_ge(rt["step"], 7 * b + 3)
                dve.reciprocal(total[:, :], total[:, :]).then_inc(rt["step"], 1)
                dve.wait_ge(rt["step"], 7 * b + 4)
                dve.tensor_tensor(probs[:, :, :], probs[:, :, :], total[:, :].unsqueeze(2).to_broadcast([P, TPB, EXPERTS]),
                                  ALU.mult).then_inc(rt["step"], 1)
                dve.wait_ge(rt["step"], 7 * b + 5)
                other = probs[:, :, :].unsqueeze(2).to_broadcast(pairs)
                own = probs[:, :, :].unsqueeze(3).to_broadcast(pairs)
                dve.tensor_tensor(greater[:, :, :, :], other, own, ALU.is_gt)
                dve.tensor_tensor(equal[:, :, :, :], other, own, ALU.is_equal).then_inc(rt["step"], 1)
                dve.wait_ge(rt["step"], 7 * b + 6)
                dve.tensor_tensor(equal[:, :, :, :], equal[:, :, :, :], earlier[:, :, :].unsqueeze(1).to_broadcast(pairs),
                                  ALU.mult).then_inc(rt["step"], 1)
                dve.wait_ge(rt["step"], 7 * b + 7)
                dve.tensor_tensor(greater[:, :, :, :], greater[:, :, :, :], equal[:, :, :, :], ALU.add).then_inc(rt["rank"], 1)
                dve.wait_ge(rt["rank"], 2 * b + 1)
                dve.tensor_reduce(rank[:, :, :], greater[:, :, :, :], AX_X, ALU.add).then_inc(rt["rank"], 1)
                dve.wait_ge(rt["rank"], 2 * b + 2)
                if not (isinstance(b, int) and b == 0):
                    dve.wait_ge(comb_stored, 16 * b)
                dve.scalar_tensor_tensor(comb[:, :, 0:EXPERTS], rank[:, :, :], 2.0, probs[:, :, :], ALU.is_lt, ALU.mult)
                dve.wait_ge(rt["tanh"], b + 1)
                dve.tensor_scalar(comb[:, :, EXPERTS:EXPERTS + 4], shared[:, :].unsqueeze(2).to_broadcast([P, TPB, 4]), 0.5, 0.5,
                                  ALU.mult, ALU.add).then_inc(rt["ready"], 1)

            def project_batch(b, before):
                first = before is None
                for i in range(TPB):
                    dve.wait_ge(x_in[i], 16 * b + 16)
                    last = dve.bn_stats(stats[:, i, :], x[:, i, :])
                last.then_inc(ln["stats_step"], 1)
                dve.wait_ge(ln["stats_step"], b + 1)
                dve.tensor_copy(ln_tmp2[:, :], stats[:, TPB - 1, 0:1])
                for i in range(TPB):
                    dve.bn_aggr(mean_var[:, i, :], stats[:, i, :]).then_inc(ln["stats"], 1)
                for i in range(TPB + 2):
                    if i < TPB:
                        if i == 0:
                            dve.wait_ge(ln["rstd"], 2 * b + 2)
                        if i >= 2:
                            dve.wait_ge(xt["ps"], TPB * b + i - 1)
                        dve.tensor_scalar(xn[:, i % 2, :], x[:, i, :], mean_var[:, i, 0:1], ln_rs[:, i:i + 1],
                                          ALU.subtract, ALU.mult).then_inc(ln["normed"], 1)
                    if 1 <= i <= TPB:
                        j = i - 1
                        dve.wait_ge(xt["hi"], TPB * b + j + 1)
                        dve.tensor_tensor(xt_lo[:, j, :, :], seg_ps[:, j % 2, :].rearrange("p (k n) -> p k n", k=KT),
                                          xt_hi[:, j, :, :].bitcast(F32), ALU.subtract).then_inc(xt["lo"], 1)
                softplus(b)
                for q in range(CONV_TILES):
                    f = CONV_ORDER[q]
                    rows = slice(0, P if f < ET else SSM_N)
                    for tap in range(1, TAPS):
                        if tap == 1:
                            dve.wait_ge(cv["init"], CONV_TILES * b + q + 1)
                        else:
                            dve.wait_ge(cv["step"], (TAPS - 2) * (CONV_TILES * b + q) + tap - 1)
                        acc = conv_acc[rows, q % 2, tap:BT]
                        last = dve.scalar_tensor_tensor(acc, proj_ps[rows, q % 2, 0:BT - tap],
                                                        conv_w[rows, f, TAPS - 1 - tap:TAPS - tap], acc, ALU.mult, ALU.add)
                        last.then_inc(cv["done"] if tap == TAPS - 1 else cv["step"], 1)
                    if q == 6:
                        dve.wait_ge(bc["g_ps"], b + 1)
                        dve.tensor_tensor(g_mask[:, :, :], seg_ps[:, 1, :].rearrange("p (t l) -> p t l", t=TPB),
                                          upto[:, :].unsqueeze(1).to_broadcast([P, TPB, P]), ALU.mult).then_inc(bc["g_masked"], 1)
                    if q == 7:
                        if not first:
                            add_out(before, TPB - 1, b - 1)
                        route(b)

            def m_products(t, i):
                for g in range(HPG):
                    dve.wait_ge(sg["exp"], HPG * t + g + 1)
                    dve.tensor_tensor(m_t[:, g * HPG:(g + 1) * HPG, :], l_exp[:, g % 2, :, :],
                                      g_mask[:, i:i + 1, :].to_broadcast([P, HPG, P]), ALU.mult).then_inc(sg["m"], 1)

            def add_out(t, i, b):
                dve.wait_ge(yy["out_ps"], t + 1)
                dve.wait_ge(yy["rs"], t + 1)
                if i == TPB - 1:
                    dve.wait_ge(last_in, 16 * b + 16)
                to = x_last[:, :] if i == TPB - 1 else x[:, i, :]
                dve.scalar_tensor_tensor(to, off_ps[:, 0, :], y_rs[:, :], to, ALU.mult, ALU.add).then_inc(yy["x_added"], 1)

            for m in range(PIECES):
                n = piece_order(m, Z_PIECES, PIECES)
                dve.wait_ge(w["hi"], m + 1)
                dve.tensor_tensor(piece((z_lo, c_lo), n), w_raw[:, m % 2, :, :], piece((z_hi, c_hi), n).bitcast(F32),
                                  ALU.subtract).then_inc(w["split"], 1)
            dve.wait_ge(w["hi"], PIECES + 1)
            dve.wait_ge(loaded["const"], 16 * N_CONST)
            dve.tensor_tensor(small_lo[:, :, :], small_raw[:, :, :], small_hi[:, :, :].bitcast(F32), ALU.subtract).then_inc(w["small"], 1)
            dve.wait_ge(out_loaded, 16)
            for f in range(ET):
                dve.tensor_scalar(w_out[:, f, :], w_out[:, f, :], norm_w[:, f:f + 1], float(E) ** 0.5, ALU.mult, ALU.mult
                                  ).then_inc(w["normed"], 1)
            dve.wait_ge(w["a"], 1)
            project_batch(0, None)
            m_products(0, 0)

            def body(b, last):
                for i in range(TPB):
                    t = b * TPB + i
                    y_halves = whole(y_ps)
                    if i:
                        dve.wait_ge(yy["off_ps"], 3 * b + i)
                        dve.tensor_tensor(y[:, :, :], whole(off_ps), heads(decays[:, 1, i, :], SSM_P), ALU.mult).then_inc(yy["off_scaled"], 1)
                        dve.wait_ge(yy["off_scaled"], 3 * b + i)
                        dve.wait_ge(yy["diag_ps"], t + 1)
                        dve.tensor_tensor(y[:, :, :], y[:, :, :], y_halves, ALU.add).then_inc(yy["diag_added"], 1)
                        dve.wait_ge(yy["diag_added"], 3 * b + i)
                        dve.wait_ge(hh["skip"], t + 1)
                        dve.tensor_tensor(y[:, :, :], y[:, :, :], h_tok[:, :, :], ALU.add).then_inc(yy["skip_added"], 1)
                    else:
                        dve.wait_ge(yy["diag_ps"], t + 1)
                        dve.wait_ge(hh["skip"], t + 1)
                        dve.tensor_tensor(y[:, :, :], h_tok[:, :, :], y_halves, ALU.add).then_inc(yy["skip_added"], 1)
                    dve.wait_ge(yy["skip_added"], t + 1)
                    dve.wait_ge(zz["silu"], HB * (t + 1))
                    dve.tensor_tensor(y[:, :, :], y[:, :, :], z_silu[:, :].rearrange("p (h d) -> p h d", d=SSM_P),
                                      ALU.mult).then_inc(yy["gated"], 1)
                    if i < TPB - 1:
                        m_products(t + 1, i + 1)
                        dve.wait_ge(st["ps"], 3 * b + i + 1)
                        src = off_ps[0:SSM_N, :, :].rearrange("p b n -> p (b n)").rearrange("p (h d) -> p h d", d=SSM_P)
                        if i == 0:
                            dve.tensor_copy(state[:, :, :], src).then_inc(st["ready"], 1)
                        else:
                            dve.wait_ge(st["scaled"], 2 * b + i)
                            dve.tensor_tensor(state[:, :, :], state[:, :, :], src, ALU.add).then_inc(st["ready"], 1)
                        add_out(t, i, b)
                    elif last:
                        add_out(t, i, b)
                    else:
                        project_batch(b + 1, t)
                        m_products(t + 1, 0)

            with dve.Fori(0, BATCHES - 1) as b:
                body(b, False)
            body(BATCHES - 1, True)


def piece_order(m, z_pieces, pieces):
    order = [pieces - 1] + list(range(z_pieces, pieces - 1)) + list(range(z_pieces))
    return order[m]


def ssm_tables():
    import numpy as np

    i = np.arange(P)
    e = np.arange(EXPERTS)
    f = np.float32
    return {
        "ident": np.eye(P, dtype=f),
        "upto": (i[:, None] <= i[None, :]).astype(f),
        "after": (i[:, None] > i[None, :]).astype(f),
        "ones": np.ones((P, P), f),
        "earlier": (e[None, :] < e[:, None]).astype(f),
    }


def model_kernel(nc, ins, out):
    x_parts = nc.dram_tensor("x_parts", (2, TILES + 2, P, D), F32, kind="Internal").ap()
    after_attention0 = nc.dram_tensor("after_attention0", (TILES, P, D), F32, kind="Internal").ap()
    after_layer0 = nc.dram_tensor("after_layer0", (TILES, P, D), F32, kind="Internal").ap()
    after_attention1 = nc.dram_tensor("after_attention1", (TILES, P, D), F32, kind="Internal").ap()
    expert_weights = nc.dram_tensor("expert_weights", (P, TILES, EXPERTS + SHARED_GROUPS), F32, kind="Internal").ap()

    def named(prefix, labels):
        return {label: ins[f"{prefix}_{label}"] for label in labels.split()}

    linear_attention_phase(nc, ins["x"], named("a0", "qkvo g1 g2 norm_w"),
                           named("t0", "ident cos sin decay decay_q decay_k same_head chunk_decay"),
                           x_parts, after_attention0)
    fp4 = named("f0", "scales shift")
    fp4["resid"] = after_attention0
    swiglu_phase(nc, "f0", x_parts, ins["f0_words"], None, FP4_GROUPS, None, fp4, after_layer0)
    ssm_phase(nc, after_layer0, named("a1", "in_proj small conv_w conv_b dt_bias a_log skip_d norm_w out_proj"),
              named("t1", "ident upto after ones earlier"), x_parts, after_attention1, expert_weights)
    swiglu_phase(nc, "f1", x_parts, ins["f1_up"], ins["f1_down"], EXPERTS + SHARED_GROUPS,
                 (expert_weights, after_attention1), None, out)


def rows_on_partitions(w):
    return w.reshape(-1, P, w.shape[-1]).transpose(1, 0, 2)


def lay_attention0(wq, wk, wv, wo, wg1, wg2, norm_weight):
    import numpy as np

    return {
        "a0_qkvo": np.stack([rows_on_partitions(w).reshape(P, KT * D) for w in (wq, wk, wv, wo)]),
        "a0_g1": rows_on_partitions(wg1),
        "a0_g2": wg2,
        "a0_norm_w": norm_weight.reshape(KT, P).T,
    }


def in_groups(w):
    import numpy as np

    pad = np.zeros((SHARED_GROUPS * GF - w.shape[0],) + w.shape[1:], w.dtype)
    return np.concatenate([w, pad]).reshape((SHARED_GROUPS, GF) + w.shape[1:])


def lay_fp4(up_packed, up_scales, down_packed, down_scales):
    import numpy as np

    inter = up_packed.shape[0] // 2
    gate_up = np.stack([in_groups(w) for w in up_packed.reshape(2, inter, -1)])
    words = gate_up.reshape(2, FP4_GROUPS, JT, P, KT, P // 8).transpose(1, 2, 0, 5, 4, 3)
    words = np.repeat(words, 8, axis=3).reshape(FP4_GROUPS, 2 * JT, P, D)
    down = in_groups(np.repeat(down_packed.T, 8, axis=0)).reshape(FP4_GROUPS, JT, P, D)
    up_by = np.stack([in_groups(w) for w in up_scales.T.reshape(2, inter, KT)])
    up_by = up_by.reshape(2, FP4_GROUPS, JT, P, KT).transpose(1, 2, 0, 4, 3).reshape(FP4_GROUPS, 2 * JT, D)
    down_by = np.concatenate([down_scales, np.zeros((FP4_GROUPS * JT - len(down_scales), D), down_scales.dtype)])
    return {
        "f0_words": np.concatenate([words, down], 1),
        "f0_scales": np.concatenate([up_by, down_by.reshape(FP4_GROUPS, JT, D)], 1),
        "f0_shift": (4 * (np.arange(P, dtype=np.int32) % 8)).reshape(P, 1),
    }


def lay_attention1(in_proj_w, conv_w, conv_b, dt_bias, a_log, skip_d, norm_w, out_proj_w, gate_w, shared_gate_w):
    import numpy as np

    w = in_proj_w.T
    wide = rows_on_partitions(w[:, :2 * E + 2 * SSM_N])
    zero = np.zeros((D, 1), np.float32)

    def by_feature_tile(a):
        pad = np.zeros((1, P - SSM_N, a.shape[1]), np.float32)
        b_c = [np.concatenate([a[None, n:n + SSM_N], pad], 1) for n in (E, E + SSM_N)]
        return np.concatenate([a[:E].reshape(ET, P, -1)] + b_c).transpose(1, 0, 2)

    return {
        "a1_in_proj": wide.reshape(P, KT, -1, P).transpose(2, 0, 1, 3),
        "a1_small": rows_on_partitions(np.concatenate([w[:, 2 * E + 2 * SSM_N:], gate_w.T, shared_gate_w.T, zero], 1)),
        "a1_conv_w": by_feature_tile(conv_w),
        "a1_conv_b": by_feature_tile(conv_b[:, None])[:, :, 0],
        "a1_dt_bias": dt_bias,
        "a1_a_log": a_log,
        "a1_skip_d": skip_d,
        "a1_norm_w": norm_w.reshape(ET, P).T,
        "a1_out_proj": rows_on_partitions(out_proj_w.T),
    }


def lay_experts(fc1, fc2, proj, shared_fc1, shared_fc2, shared_proj):
    import numpy as np

    def filled(w):
        return np.concatenate([w, np.zeros((EXPERTS, GF - w.shape[1], D), np.float32)], 1)

    w1 = np.concatenate([filled(fc1), in_groups(shared_fc1)])
    w2 = np.concatenate([filled(fc2), in_groups(shared_fc2)])
    up = np.stack([w1, w2], 1).reshape(-1, 2, JT, P, KT, P)
    return {
        "f1_up": up.transpose(0, 5, 2, 1, 4, 3).reshape(-1, P, JT * 2 * KT * P),
        "f1_down": np.concatenate([filled(proj.transpose(0, 2, 1)), in_groups(shared_proj.T)]),
    }


def kernel(**inputs):
    import concourse.bacc as bacc
    import numpy as np
    from concourse.bass_utils import run_bass_kernel_spmd

    given = {name: np.asarray(a) for name, a in inputs.items()}

    def take(prefix, labels):
        return [given[f"{prefix}_{label}"] for label in labels.split()]

    x = given["L0_attn_x"]
    arrays = {"x": x.reshape(TILES, P, D)}
    arrays.update(lay_attention0(*take("L0_attn", "Wq Wk Wv Wo Wg1 Wg2 norm_weight")))
    arrays.update(lay_fp4(*take("L0_ffn", "gate_up_packed gate_up_scales down_packed down_scales")))
    arrays.update(lay_attention1(*take("L1_attn", "in_proj_w conv_w conv_b dt_bias A_log D norm_w out_proj_w"),
                                 *take("L1_ffn", "gate_w shared_gate_w")))
    arrays.update(lay_experts(*take("L1_ffn", "expert_fc1 expert_fc2 expert_proj shared_fc1 shared_fc2 shared_proj")))
    arrays.update({f"t0_{label}": table for label, table in attention0_tables().items()})
    arrays.update({f"t1_{label}": table for label, table in ssm_tables().items()})

    nc = bacc.Bacc("TRN2", target_bir_lowering=False, num_devices=1)
    arrays = {name: np.ascontiguousarray(a) for name, a in arrays.items()}
    ins = {name: nc.dram_tensor(f"in_{name}", a.shape, mybir.dt.from_np(a.dtype), kind="ExternalInput").ap()
           for name, a in arrays.items()}
    out = nc.dram_tensor("out", (TILES, P, D), F32, kind="ExternalOutput").ap()
    model_kernel(nc, ins, out)
    result = run_bass_kernel_spmd(nc, [{f"in_{name}": a for name, a in arrays.items()}], core_ids=[0])
    return result.results[0]["out"].reshape(x.shape)
```

```python
from contextlib import ExitStack

import concourse.bass as bass
from concourse import mybir

F32 = mybir.dt.float32
F32R = mybir.dt.float32r
F16 = mybir.dt.float16
BF16 = mybir.dt.bfloat16
I32 = mybir.dt.int32
ALU = mybir.AluOpType
ACT = mybir.ActivationFunctionType
AX_X = mybir.AxisListType.X

P = 128
BANK = 512
BATCHES = 4
BT = 512
TPB = BT // P
TILES = BATCHES * TPB
D = 512
KT = D // P
JT = 3
LAST_JT = 2
GF = JT * P



def clear_semaphores(nc, semaphores):
    nc.clear_and_free_semaphores(semaphores)
    nc.all_engine_barrier()


FP4_GROUPS = 4
SHARED_GROUPS = FP4_GROUPS


HEADS = 16
HD = 32
HPT = P // HD


def linear_attention_phase(nc, x_dram, wts, tables, x_parts, out_dram):
    name = "a0"
    semaphores = []
    with ExitStack() as ctx:
        ctx.callback(clear_semaphores, nc, semaphores)

        def sb(label, shape, dt=F32):
            return ctx.enter_context(nc.sbuf_tensor(f"{name}_{label}", shape, dt))

        def bank(label):
            return ctx.enter_context(nc.psum_tensor(f"{name}_{label}", [P, BANK], F32))

        def sem(label):
            semaphores.append(nc.alloc_semaphore(f"{name}_{label}"))
            return semaphores[-1]

        w_raw = sb("w_raw", [P, 2, KT, D])
        w_hi = sb("w_hi", [P, 4, KT, D], F32R)
        w_lo = sb("w_lo", [P, 4, KT, D], F32R)
        g1_raw = sb("g1_raw", [P, KT, HD])
        g1_hi = sb("g1_hi", [P, KT, HD], F32R)
        g1_lo = sb("g1_lo", [P, KT, HD], F32R)
        g2 = sb("g2", [HD, D])
        norm_w = sb("norm_w", [P, KT])
        ident = sb("ident", [P, P])
        rope_cos = sb("rope_cos", [P, TPB, HD])
        rope_sin = sb("rope_sin", [P, TPB, HD])
        decay = sb("decay", [P, HPT, HPT, P])
        decay_q = sb("decay_q", [P, HEADS])
        decay_k = sb("decay_k", [P, HEADS])
        same_head = sb("same_head", [P, P])
        chunk_decay = sb("chunk_decay", [P, KT, P])
        power = sb("power", [P, HEADS])

        x = sb("x", [P, TPB, D])
        stats = sb("stats", [P, 6])
        mean_var = sb("mean_var", [P, 2, 2])
        ln_tmp = sb("ln_tmp", [P, 1])
        stats_copy = sb("stats_copy", [P, 1])
        eps_ln = sb("eps_ln", [P, 1])
        eps_head = sb("eps_head", [P, HEADS])
        ln_rs = sb("ln_rs", [P, 2])
        xn = sb("xn", [P, 2, D])
        xt_hi = [sb(f"xt_hi{n}", [P, KT, P], F32R) for n in range(2)]
        xt_lo = [sb(f"xt_lo{n}", [P, KT, P], F32R) for n in range(2)]
        qk = sb("qk", [P, 2 * HEADS, HD])
        qk_cos = sb("qk_cos", [P, 2 * HEADS, HD])
        qk_sin = sb("qk_sin", [P, 2 * HEADS, HD])
        qk_rot = [sb(f"qk_rot{n}", [P, 2 * HEADS, HD]) for n in range(2)]
        k_dec = [sb(f"k_dec{n}", [P, HEADS, HD]) for n in range(2)]
        v = [sb(f"v{n}", [P, D]) for n in range(2)]
        gate_low = sb("gate_low", [HD, P])
        gate = sb("gate", [P, 2, D])
        qt = sb("qt", [P, KT, P])
        kt_ = sb("kt", [P, KT, P])
        scores = sb("scores", [P, HPT, HPT, P])
        inter = sb("inter", [P, D])
        o_sum = sb("o_sum", [P, D])
        x2 = sb("x2", [P, D])
        sq = sb("sq", [P, D])
        ss = sb("ss", [P, HEADS])
        ms = sb("ms", [P, HEADS])
        rs = sb("rs", [P, HEADS])
        o_norm = sb("o_norm", [P, D])
        ot_hi = sb("ot_hi", [P, KT, P], F32R)
        ot_lo = sb("ot_lo", [P, KT, P], F32R)
        state = sb("state", [P, KT, P])
        state_new = sb("state_new", [P, KT, P])
        state_old = sb("state_old", [P, KT, P])

        proj_ps = [bank(f"proj{n}") for n in range(2)]
        score_ps = [bank(f"score{n}") for n in range(HPT)]
        misc_ps = [bank(f"misc{n}") for n in range(2)]
        o_ps, y_ps = score_ps[0], score_ps[1]

        def sems(group, labels):
            return {label: sem(f"{group}_{label}") for label in labels.split()}

        loaded = sems("loaded", "const q_k_v_low")
        w = sems("w", "hi split normed")
        ln = sems("ln", "stats_step stats rstd normed")
        xt = sems("xt", "ps hi lo")
        ps = sems("ps", "q k v low gate qt kt scores inter state o ot y")
        act_out = sems("act_out", "q k v low gate qt kt sq ot_hi")
        rot = sems("rot", "cos sin done k_decayed")
        st = sems("st", "masked old ready")
        masked = sem("masked")
        out = sems("out", "inter_scaled summed gated squares rstd normed ot_lo y_added")
        power_set = sem("power_set")
        x_in = [sem(f"x_in{n}") for n in range(TPB)]
        y_stored = [sem(f"y_stored{n}") for n in range(TPB)]
        xt_stored = [sem(f"xt_stored{n}") for n in range(2)]
        w_loaded = [sem(f"w_loaded{n}") for n in range(2)]

        block = ctx.enter_context(nc.Block())

        @block.sync
        def _(sp):
            def load_w(n):
                sp.dma_start(w_raw[:, n % 2, :, :].rearrange("p k n -> p (k n)"), wts["qkvo"][n]
                             ).then_inc(w_loaded[n % 2], 16)

            def load_x(batch, i):
                sp.dma_start(x[:, i, :], x_dram[bass.ds(batch * TPB + i, 1)].rearrange("o p n -> (o p) n")
                             ).then_inc(x_in[i], 16)

            def store_xt(t, odd):
                sp.wait_ge(xt["hi"], t + 1)
                sp.wait_ge(xt["lo"], t + 1)
                for part, buf in ((0, xt_hi[odd]), (1, xt_lo[odd])):
                    sp.dma_start(x_parts[part, bass.ds(t, 1)].rearrange("o p n -> (o p) n"),
                                 buf[:, :, :].bitcast(F32).rearrange("p k n -> p (k n)")).then_inc(xt_stored[odd], 16)

            load_x(0, 0)
            sp.dma_start(ident[:, :], tables["ident"]).then_inc(loaded["const"], 16)
            load_x(0, 1)
            load_w(0)
            load_w(1)
            small = ((g1_raw, wts["g1"]), (g2, wts["g2"]), (norm_w, wts["norm_w"]), (rope_cos, tables["cos"]),
                     (rope_sin, tables["sin"]), (decay_q, tables["decay_q"]), (decay_k, tables["decay_k"]),
                     (same_head, tables["same_head"]), (chunk_decay, tables["chunk_decay"]), (decay, tables["decay"]))
            for dst, src in small:
                sp.dma_start(dst[:], src).then_inc(loaded["const"], 16)
            load_x(0, 2)
            load_x(0, 3)
            for n in (2, 3):
                sp.wait_ge(w["split"], n - 1)
                load_w(n)
            store_xt(0, 0)
            store_xt(1, 1)
            def body(b, first, last):
                for i in range(TPB):
                    t = b * TPB + i
                    if not (first and i == 0):
                        store_y(t - 1, (i - 1) % TPB)
                        if i == 0:
                            sp.wait_ge(y_stored[TPB - 1], 16 * b)
                            load_x(b, TPB - 1)
                        elif not last:
                            sp.wait_ge(y_stored[i - 1], 16 * b + 16)
                            load_x(b + 1, i - 1)
                    if not (last and i >= TPB - 2):
                        store_xt(t + 2, i % 2)

            def store_y(t, slot):
                sp.wait_ge(out["y_added"], t + 2)
                sp.dma_start(out_dram[bass.ds(t, 1)].rearrange("o p n -> (o p) n"), x[:, slot, :]).then_inc(y_stored[slot], 16)

            body(0, True, False)
            with sp.Fori(1, BATCHES - 1) as b:
                body(b, False, False)
            body(BATCHES - 1, False, True)
            store_y(TILES - 1, TPB - 1)
            for n in range(TPB):
                sp.wait_ge(y_stored[n], 16 * BATCHES)
            for n in range(2):
                sp.wait_ge(xt_stored[n], 16 * TILES)

        @block.tensor
        def _(pe):
            def turn(to, src, ready):
                for k in range(KT):
                    last = pe.transpose(to[:, k * P:(k + 1) * P], src[:, k * P:(k + 1) * P], ident[:, :])
                last.then_inc(ready, 1)

            def sums(to, l_hi, l_lo, r_hi, r_lo, k):
                pe.matmul(to, l_hi, r_hi, start=k == 0, stop=False)
                pe.matmul(to, l_hi, r_lo, start=False, stop=False)
                return pe.matmul(to, l_lo, r_hi, start=False, stop=k == KT - 1)

            def project(bank_, n, odd, ready):
                for k in range(KT):
                    last = sums(bank_[:, :], xt_hi[odd][:, k, :], xt_lo[odd][:, k, :], w_hi[:, n, k, :], w_lo[:, n, k, :], k)
                last.then_inc(ready, 1)

            def x_turned(t, odd):
                pe.wait_ge(ln["normed"], t + 1)
                turn(misc_ps[1], xn[:, odd, :], xt["ps"])

            def q_proj(t, odd, first=False):
                pe.wait_ge(xt["hi"], t + 1)
                pe.wait_ge(xt["lo"], t + 1)
                if not first:
                    pe.wait_ge(act_out["v"], t)
                project(proj_ps[0], 0, odd, ps["q"])

            def k_proj(t, odd, first=False):
                if not first:
                    pe.wait_ge(act_out["gate"], t)
                project(proj_ps[1], 1, odd, ps["k"])

            def v_proj(t, odd):
                pe.wait_ge(act_out["q"], t + 1)
                project(proj_ps[0], 2, odd, ps["v"])
                pe.wait_ge(act_out["k"], t + 1)
                for k in range(KT):
                    last = sums(proj_ps[1][0:HD, 0:P], g1_hi[:, k, :], g1_lo[:, k, :],
                                xt_hi[odd][:, k, :], xt_lo[odd][:, k, :], k)
                last.then_inc(ps["low"], 1)

            def gate_proj(t):
                pe.wait_ge(act_out["low"], t + 1)
                pe.matmul(proj_ps[1][:, :], gate_low[:, :], g2[:, :], start=True, stop=True).then_inc(ps["gate"], 1)

            def o_turned(t):
                pe.wait_ge(out["normed"], t + 1)
                turn(misc_ps[0], o_norm[:, :], ps["ot"])

            def y_proj(t):
                pe.wait_ge(act_out["ot_hi"], t + 1)
                pe.wait_ge(out["ot_lo"], t + 1)
                for k in range(KT):
                    last = sums(y_ps[:, :], ot_hi[:, k, :], ot_lo[:, k, :], w_hi[:, 3, k, :], w_lo[:, 3, k, :], k)
                last.then_inc(ps["y"], 1)

            def score(t, i):
                pe.wait_ge(act_out["qt"], t + 1)
                pe.wait_ge(act_out["kt"], t + 1)
                pe.wait_ge(out["gated"], t + 1)
                if not (isinstance(t, int) and t == 0):
                    pe.wait_ge(out["y_added"], t)
                for g in range(KT):
                    for r in range(HPT):
                        rows = slice(r * HD, (r + 1) * HD)
                        last = pe.matmul(score_ps[r][:, g * P:(g + 1) * P], kt_[rows, g, :], qt[rows, g, :],
                                         start=True, stop=True)
                        if g == KT - 1:
                            last.then_inc(ps["scores"], 1)

            def attend(t, odd):
                pe.wait_ge(masked, HPT * (t + 1))
                for h in range(HEADS):
                    last = pe.matmul(o_ps[:, h * HD:(h + 1) * HD], scores[:, h % HPT, h // HPT, :],
                                     v[odd][:, h * HD:(h + 1) * HD], start=True, stop=True)
                last.then_inc(ps["o"], 1)

            pe.wait_ge(loaded["const"], 16 * 11)
            x_turned(0, 0)
            pe.wait_ge(xt["hi"], 1)
            pe.wait_ge(xt["lo"], 1)
            x_turned(1, 1)
            pe.wait_ge(w["split"], 1)
            q_proj(0, 0, first=True)
            pe.wait_ge(w["split"], 2)
            k_proj(0, 0, first=True)
            pe.wait_ge(w["split"], 4)
            v_proj(0, 0)
            gate_proj(0)
            pe.wait_ge(w["split"], 5)
            def body(b, first, last):
                for i in range(TPB):
                    t = b * TPB + i
                    odd, other = i % 2, (i + 1) % 2
                    some_before = not (first and i == 0)
                    some_next = not (last and i == TPB - 1)
                    pe.wait_ge(rot["done"], t + 1)
                    if i == 1:
                        pe.wait_ge(st["ready"], 3 * b + 1)
                    elif i > 1:
                        pe.wait_ge(st["masked"], 2 * b + i - 1)
                    elif some_before:
                        pe.wait_ge(act_out["ot_hi"], t - 1)
                        pe.wait_ge(out["ot_lo"], t - 1)
                    turn(misc_ps[0], qk_rot[odd][:, 0:HEADS, :].rearrange("p h d -> p (h d)"), ps["qt"])
                    if some_next:
                        pe.wait_ge(xt["hi"], t + 2)
                        pe.wait_ge(xt["lo"], t + 2)
                    else:
                        pe.wait_ge(out["inter_scaled"], 3 * b + i - 1)
                    turn(misc_ps[1], qk_rot[odd][:, HEADS:2 * HEADS, :].rearrange("p h d -> p (h d)"), ps["kt"])
                    if some_next:
                        q_proj(t + 1, other)
                    score(t, i)
                    if some_before:
                        o_turned(t - 1)
                    if i:
                        pe.wait_ge(st["ready"], 3 * b + i)
                        for g in range(KT):
                            last_mm = pe.matmul(misc_ps[1][:, g * P:(g + 1) * P], qt[:, g, :], state[:, g, :],
                                                start=True, stop=True)
                        last_mm.then_inc(ps["inter"], 1)
                    if some_next:
                        k_proj(t + 1, other)
                    if i < TPB - 1:
                        pe.wait_ge(rot["k_decayed"], t + 1)
                        if some_before:
                            pe.wait_ge(act_out["ot_hi"], t)
                            pe.wait_ge(out["ot_lo"], t)
                        for g in range(KT):
                            cols = slice(g * P, (g + 1) * P)
                            last_mm = pe.matmul(misc_ps[0][:, cols],
                                                k_dec[odd][:, :, :].rearrange("p h d -> p (h d)")[:, cols],
                                                v[odd][:, cols], start=True, stop=True)
                        last_mm.then_inc(ps["state"], 1)
                    if not (last and i >= TPB - 2):
                        if i:
                            pe.wait_ge(out["inter_scaled"], 3 * b + i)
                        x_turned(t + 2, odd)
                    if some_next:
                        v_proj(t + 1, other)
                    attend(t, odd)
                    if some_before:
                        y_proj(t - 1)
                    if some_next:
                        gate_proj(t + 1)

            body(0, True, False)
            with pe.Fori(1, BATCHES - 1) as b:
                body(b, False, False)
            body(BATCHES - 1, False, True)
            o_turned(TILES - 1)
            pe.wait_ge(out["y_added"], TILES)
            y_proj(TILES - 1)

        @block.scalar
        def _(act):
            qk_flat = qk[:, :, :].rearrange("p h d -> p (h d)")

            def x_high(t, odd, stored=None):
                act.wait_ge(xt["ps"], t + 1)
                if stored is not None:
                    act.wait_ge(ps["low"], t - 1)
                    act.wait_ge(xt_stored[odd], stored)
                act.copy(xt_hi[odd][:, :, :], misc_ps[1][:, :].rearrange("p (k n) -> p k n", k=KT)).then_inc(xt["hi"], 1)

            def projected(t, odd, first=False, turned_next=False):
                act.wait_ge(ps["q"], t + 1)
                if not first:
                    act.wait_ge(rot["cos"], t)
                    act.wait_ge(rot["sin"], t)
                act.activation(qk_flat[:, 0:D], proj_ps[0][:, :], ACT.Silu).then_inc(act_out["q"], 1)
                act.wait_ge(ps["k"], t + 1)
                act.activation(qk_flat[:, D:2 * D], proj_ps[1][:, :], ACT.Silu).then_inc(act_out["k"], 1)
                if turned_next:
                    x_high(t + 1, 1 - odd, stored=16 * (t + 1 - (1 - odd)))
                act.wait_ge(ps["v"], t + 1)
                act.copy(v[odd][:, :], proj_ps[0][:, :]).then_inc(act_out["v"], 1)
                act.wait_ge(ps["low"], t + 1)
                act.copy(gate_low[:, :], proj_ps[1][0:HD, 0:P]).then_inc(act_out["low"], 1)

            def gated(t, odd):
                act.wait_ge(ps["gate"], t + 1)
                act.activation(gate[:, odd, :], proj_ps[1][:, :], ACT.Tanh, scale=0.5).then_inc(act_out["gate"], 1)

            def o_high(t):
                act.wait_ge(ps["ot"], t + 1)
                act.copy(ot_hi[:, :, :], misc_ps[0][:, :].rearrange("p (k n) -> p k n", k=KT)).then_inc(act_out["ot_hi"], 1)

            def w_high(n):
                act.wait_ge(w_loaded[n % 2], 16 * (n // 2 + 1))
                act.copy(w_hi[:, n, :, :], w_raw[:, n % 2, :, :]).then_inc(w["hi"], 1)

            x_high(0, 0)
            w_high(0)
            x_high(1, 1)
            w_high(1)
            w_high(2)
            act.wait_ge(loaded["const"], 16 * 11)
            act.copy(g1_hi[:, :, :], g1_raw[:, :, :]).then_inc(w["hi"], 1)
            projected(0, 0, first=True)
            gated(0, 0)
            act.wait_ge(w["normed"], KT)
            w_high(3)
            def body(b, first, last):
                for i in range(TPB):
                    t = b * TPB + i
                    odd, other = i % 2, (i + 1) % 2
                    act.wait_ge(ps["qt"], t + 1)
                    act.copy(qt[:, :, :], misc_ps[0][:, :].rearrange("p (k n) -> p k n", k=KT)).then_inc(act_out["qt"], 1)
                    act.wait_ge(ps["kt"], t + 1)
                    act.copy(kt_[:, :, :], misc_ps[1][:, :].rearrange("p (k n) -> p k n", k=KT)).then_inc(act_out["kt"], 1)
                    if not (first and i == 0):
                        o_high(t - 1)
                    if not (last and i == TPB - 1):
                        projected(t + 1, other, turned_next=not (last and i == TPB - 2))
                    act.wait_ge(out["gated"], t + 2)
                    act.activation(sq[:, :], x2[:, :], ACT.Square).then_inc(act_out["sq"], 1)
                    if not (last and i == TPB - 1):
                        gated(t + 1, other)

            body(0, True, False)
            with act.Fori(1, BATCHES - 1) as b:
                body(b, False, False)
            body(BATCHES - 1, False, True)
            o_high(TILES - 1)

        @block.gpsimd
        def _(pool):
            def ln_rstd(t, odd):
                pool.wait_ge(ln["stats"], t + 1)
                pool.tensor_tensor(ln_tmp[:, :], mean_var[:, odd, 1:2], eps_ln[:, :], ALU.add).then_inc(ln["rstd"], 1)
                pool.wait_ge(ln["rstd"], 2 * t + 1)
                pool.tensor_tensor(ln_rs[:, odd:odd + 1], ln_tmp[:, :], power[:, 0:1], ALU.pow).then_inc(ln["rstd"], 1)

            def swap(t, i, first=False):
                half = HD // 2
                pool.wait_ge(act_out["q"], t + 1)
                pool.wait_ge(act_out["k"], t + 1)
                if not first:
                    pool.wait_ge(rot["done"], t)
                for to, of in ((0, half), (half, 0)):
                    last = pool.tensor_tensor(qk_sin[:, :, to:to + half], qk[:, :, of:of + half],
                                              rope_sin[:, i:i + 1, to:to + half].to_broadcast([P, 2 * HEADS, half]), ALU.mult)
                last.then_inc(rot["sin"], 1)

            pool.memset(power[:, :], -0.5).then_inc(power_set, 1)
            pool.memset(eps_ln[:, :], 1e-5).then_inc(power_set, 1)
            pool.memset(eps_head[:, :], 4 * HD * 1e-6).then_inc(power_set, 1)
            pool.wait_ge(power_set, 3)
            ln_rstd(0, 0)
            ln_rstd(1, 1)
            pool.wait_ge(loaded["const"], 16 * 11)
            swap(0, 0, first=True)

            def body(b, first, last):
                for i in range(TPB):
                    t = b * TPB + i
                    if i in (1, 2):
                        pool.wait_ge(st["ready"], 3 * b + i)
                        pool.tensor_tensor(state_old[:, :, :], state[:, :, :], chunk_decay[:, :, :], ALU.mult).then_inc(st["old"], 1)
                    if not (last and i >= TPB - 2):
                        ln_rstd(t + 2, i % 2)
                    if not (last and i == TPB - 1):
                        swap(t + 1, (i + 1) % TPB)
                    pool.wait_ge(out["squares"], t + 1)
                    pool.tensor_tensor(ms[:, :], ss[:, :], eps_head[:, :], ALU.add).then_inc(out["rstd"], 1)
                    pool.wait_ge(out["rstd"], 2 * t + 1)
                    pool.tensor_tensor(rs[:, :], ms[:, :], power[:, :], ALU.pow).then_inc(out["rstd"], 1)

            body(0, True, False)
            with pool.Fori(1, BATCHES - 1) as b:
                body(b, False, False)
            body(BATCHES - 1, False, True)

        @block.vector
        def _(dve):
            def x_stats(t, odd, slot, count):
                dve.wait_ge(x_in[slot], 16 * count)
                dve.bn_stats(stats[:, :], x[:, slot, :]).then_inc(ln["stats_step"], 1)
                dve.wait_ge(ln["stats_step"], t + 1)
                dve.tensor_copy(stats_copy[:, :], stats[:, 0:1])
                dve.bn_aggr(mean_var[:, odd, :], stats[:, :]).then_inc(ln["stats"], 1)

            def x_normed(t, odd, slot, first=False):
                dve.wait_ge(ln["rstd"], 2 * t + 2)
                if not first:
                    dve.wait_ge(xt["ps"], t - 1)
                dve.tensor_scalar(xn[:, odd, :], x[:, slot, :], mean_var[:, odd, 0:1], ln_rs[:, odd:odd + 1],
                                  ALU.subtract, ALU.mult).then_inc(ln["normed"], 1)

            def x_low(t, odd):
                dve.wait_ge(xt["hi"], t + 1)
                dve.tensor_tensor(xt_lo[odd][:, :, :], misc_ps[1][:, :].rearrange("p (k n) -> p k n", k=KT),
                                  xt_hi[odd][:, :, :].bitcast(F32), ALU.subtract).then_inc(xt["lo"], 1)

            def rotate(t, i, odd):
                dve.wait_ge(act_out["q"], t + 1)
                dve.wait_ge(act_out["k"], t + 1)
                dve.tensor_tensor(qk_cos[:, :, :], qk[:, :, :], rope_cos[:, i:i + 1, :].to_broadcast([P, 2 * HEADS, HD]),
                                  ALU.mult).then_inc(rot["cos"], 1)
                dve.wait_ge(rot["cos"], t + 1)
                dve.wait_ge(rot["sin"], t + 1)
                dve.tensor_tensor(qk_rot[odd][:, :, :], qk_cos[:, :, :], qk_sin[:, :, :], ALU.add).then_inc(rot["done"], 1)
                dve.wait_ge(rot["done"], t + 1)
                dve.tensor_tensor(k_dec[odd][:, :, :], qk_rot[odd][:, HEADS:2 * HEADS, :],
                                  decay_k[:, :].unsqueeze(2).to_broadcast([P, HEADS, HD]), ALU.mult).then_inc(rot["k_decayed"], 1)

            def o_low(t):
                dve.wait_ge(act_out["ot_hi"], t + 1)
                dve.tensor_tensor(ot_lo[:, :, :], misc_ps[0][:, :].rearrange("p (k n) -> p k n", k=KT),
                                  ot_hi[:, :, :].bitcast(F32), ALU.subtract).then_inc(out["ot_lo"], 1)

            def add_y(t, slot):
                dve.wait_ge(ps["y"], t + 1)
                dve.tensor_tensor(x[:, slot, :], x[:, slot, :], y_ps[:, :], ALU.add).then_inc(out["y_added"], 1)

            def w_low(n, slot, count):
                dve.wait_ge(w["hi"], count)
                dve.tensor_tensor(w_lo[:, n, :, :], w_raw[:, slot, :, :], w_hi[:, n, :, :].bitcast(F32),
                                  ALU.subtract).then_inc(w["split"], 1)

            dve.sem_inc(out["gated"], 1)
            dve.sem_inc(out["y_added"], 1)
            x_stats(0, 0, 0, 1)
            x_normed(0, 0, 0, first=True)
            x_stats(1, 1, 1, 1)
            x_normed(1, 1, 1, first=True)
            x_low(0, 0)
            w_low(0, 0, 1)
            x_low(1, 1)
            w_low(1, 1, 2)
            w_low(2, 0, 3)
            dve.wait_ge(w["hi"], 4)
            dve.wait_ge(loaded["const"], 16 * 11)
            dve.tensor_tensor(g1_lo[:, :, :], g1_raw[:, :, :], g1_hi[:, :, :].bitcast(F32), ALU.subtract).then_inc(w["split"], 1)
            rotate(0, 0, 0)
            dve.wait_ge(w_loaded[1], 32)
            for k in range(KT):
                dve.tensor_scalar(w_raw[:, 1, k, :], w_raw[:, 1, k, :], norm_w[:, k:k + 1], 0.5 * (4 * HD) ** 0.5, ALU.mult, ALU.mult
                                  ).then_inc(w["normed"], 1)
            w_low(3, 1, 5)

            def body(b, first, last):
                for i in range(TPB):
                    t = b * TPB + i
                    odd, other = i % 2, (i + 1) % 2
                    ahead = (i + 2) % TPB
                    some_before = not (first and i == 0)
                    two_ahead = not (last and i >= TPB - 2)
                    if some_before:
                        o_low(t - 1)
                    if two_ahead:
                        x_stats(t + 2, odd, ahead, b + (i + 2) // TPB + 1)
                    for r in range(HPT):
                        dve.wait_ge(ps["scores"], HPT * t + r + 1)
                        dve.tensor_tensor(scores[:, r, :, :], score_ps[r][:, :].rearrange("p (g n) -> p g n", g=HPT),
                                          decay[:, r, :, :], ALU.mult).then_inc(masked, 1)
                    if i:
                        dve.wait_ge(ps["inter"], 3 * b + i)
                        dve.tensor_tensor(inter[:, :].rearrange("p (h d) -> p h d", h=HEADS),
                                          misc_ps[1][:, :].rearrange("p (h d) -> p h d", h=HEADS),
                                          decay_q[:, :].unsqueeze(2).to_broadcast([P, HEADS, HD]),
                                          ALU.mult).then_inc(out["inter_scaled"], 1)
                    if two_ahead:
                        x_normed(t + 2, odd, ahead)
                    if i < TPB - 1:
                        to, ready = (state, st["ready"]) if i == 0 else (state_new, st["masked"])
                        dve.wait_ge(ps["state"], 3 * b + i + 1)
                        dve.tensor_tensor(to[:, :, :], misc_ps[0][:, :].rearrange("p (k n) -> p k n", k=KT),
                                          same_head[:, :].unsqueeze(1).to_broadcast([P, KT, P]), ALU.mult).then_inc(ready, 1)
                        if i:
                            dve.wait_ge(st["masked"], 2 * b + i)
                            dve.wait_ge(st["old"], 2 * b + i)
                            dve.tensor_tensor(state[:, :, :], state_old[:, :, :], state_new[:, :, :],
                                              ALU.add).then_inc(st["ready"], 1)
                    if two_ahead:
                        x_low(t + 2, odd)
                    if not (last and i == TPB - 1):
                        rotate(t + 1, (i + 1) % TPB, other)
                    dve.wait_ge(ps["o"], t + 1)
                    dve.wait_ge(act_out["gate"], t + 1)
                    src = o_ps
                    if i:
                        dve.wait_ge(out["inter_scaled"], 3 * b + i)
                        dve.tensor_tensor(o_sum[:, :], o_ps[:, :], inter[:, :], ALU.add).then_inc(out["summed"], 1)
                        dve.wait_ge(out["summed"], 3 * b + i)
                        src = o_sum
                    dve.scalar_tensor_tensor(x2[:, :], gate[:, odd, :], 1.0, src[:, :], ALU.add, ALU.mult).then_inc(out["gated"], 1)
                    if some_before:
                        add_y(t - 1, (i - 1) % TPB)
                    dve.wait_ge(act_out["sq"], t + 1)
                    dve.tensor_reduce(ss[:, :], sq[:, :].rearrange("p (h d) -> p h d", h=HEADS), AX_X, ALU.add
                                      ).then_inc(out["squares"], 1)
                    dve.wait_ge(out["gated"], t + 2)
                    dve.wait_ge(out["rstd"], 2 * t + 2)
                    dve.tensor_tensor(o_norm[:, :].rearrange("p (h d) -> p h d", h=HEADS),
                                      x2[:, :].rearrange("p (h d) -> p h d", h=HEADS),
                                      rs[:, :].unsqueeze(2).to_broadcast([P, HEADS, HD]), ALU.mult).then_inc(out["normed"], 1)

            body(0, True, False)
            with dve.Fori(1, BATCHES - 1) as b:
                body(b, False, False)
            body(BATCHES - 1, False, True)
            o_low(TILES - 1)
            add_y(TILES - 1, TPB - 1)


def attention0_tables():
    import numpy as np

    f = np.float32
    half = HD // 2
    theta = f(10000.0) ** (f(-2.0) * np.arange(half, dtype=f) / f(HD))
    ang = np.arange(BT, dtype=f)[:, None] * theta[None, :].astype(f)
    cos, sin = np.cos(ang.astype(f)), np.sin(ang.astype(f))

    def tiled(a):
        return np.ascontiguousarray(a.reshape(TPB, P, HD).transpose(1, 0, 2).astype(f))

    log_lam = -(f(2.0) ** (f(-8.0) * (np.arange(HEADS, dtype=f) + f(1.0)) / f(HEADS))).astype(f)
    i = np.arange(P, dtype=f)
    diff = i[None, :] - i[:, None]
    d = np.exp(log_lam[:, None, None] * np.maximum(diff, 0)[None]) * (diff >= 0)[None]
    block = np.kron(np.eye(HPT), np.ones((HD, HD)))
    lam = np.exp(log_lam * f(P)).reshape(KT, HPT)
    chunk = np.stack([block * np.repeat(lam[g], HD)[:, None] for g in range(KT)], axis=1)
    return {
        "ident": np.eye(P, dtype=f),
        "cos": tiled(np.concatenate([cos, cos], axis=1)),
        "sin": tiled(np.concatenate([-sin, sin], axis=1)),
        "decay": np.ascontiguousarray(d.reshape(KT, HPT, P, P).transpose(2, 1, 0, 3).astype(f)),
        "decay_q": np.exp(log_lam[None, :] * (i[:, None] + f(1.0))).astype(f),
        "decay_k": np.exp(log_lam[None, :] * (f(P) - f(1.0) - i[:, None])).astype(f),
        "same_head": block.astype(f),
        "chunk_decay": np.ascontiguousarray(chunk.astype(f)),
    }


def swiglu_phase(nc, name, x_parts, up_src, down_src, groups, routed, fp4, out_dram):
    chunks = 3 * JT
    last_g = groups - 1
    steps_before_last = last_g * BATCHES

    semaphores = []
    with ExitStack() as ctx:
        ctx.callback(clear_semaphores, nc, semaphores)

        def sb(label, shape, dt=F32):
            return ctx.enter_context(nc.sbuf_tensor(f"{name}_{label}", shape, dt))

        def bank(label):
            return ctx.enter_context(nc.psum_tensor(f"{name}_{label}", [P, BANK], F32))

        def sem(label):
            semaphores.append(nc.alloc_semaphore(f"{name}_{label}"))
            return semaphores[-1]

        x_hi = sb("x_hi", [P, TILES, KT, P], F32R)
        x_lo = sb("x_lo", [P, TILES, KT, P], F32R)
        acc = sb("acc", [P, TILES, D])
        up_f32 = sb("up_f32", [P, JT, 2, KT, P])
        up_hi = sb("up_hi", [P, JT, 2, KT, P], F32R)
        up_lo = sb("up_lo", [P, JT, 2, KT, P], F32R)
        down_f32 = sb("down_f32", [P, JT, D])
        down_hi = sb("down_hi", [P, JT, D], F32R)
        down_lo = sb("down_lo", [P, JT, D], F32R)
        silu_g = sb("silu_g", [P, 2, BT])
        h_f32 = sb("h_f32", [P, 2, BT])
        h_hi = sb("h_hi", [P, JT, BT], F32R)
        h_lo = sb("h_lo", [P, JT, BT], F32R)
        gate_ps = [bank(f"gate{n}") for n in range(2)]
        up_ps = [bank(f"up{n}") for n in range(2)]
        y_ps = [bank(f"y{n}") for n in range(TPB)]

        x_loaded = [sem(f"x_loaded{b}") for b in range(BATCHES)]
        aux_loaded = sem("aux_loaded")
        weights_loaded = sem("weights_loaded")
        weights_hi = sem("weights_hi")
        weights_lo = sem("weights_lo")
        gu_ready = sem("gu_ready")
        silu_ready = sem("silu_ready")
        gu_free = sem("gu_free")
        hhi_ready = sem("hhi_ready")
        h_ready = sem("h_ready")
        y_ready = sem("y_ready")
        y_free = sem("y_free")
        stored = sem("stored")
        if fp4:
            words = sb("words", [P, 2, D], I32)
            scales = sb("scales", [P, 2, D], F16)
            magnitude = sb("magnitude", [P, D], I32)
            sign_bit = sb("sign_bit", [P, D], I32)
            above4 = sb("above4", [P, D], BF16)
            above6 = sb("above6", [P, D], BF16)
            half_sign = sb("half_sign", [P, D], BF16)
            twice = sb("twice", [P, D], BF16)
            value = sb("value", [P, D], BF16)
            shift = sb("shift", [P, 1], I32)
            resid = sb("resid", [P, TPB, D])
            meansq = sb("meansq", [P, TILES])
            rstd = sb("rstd", [P, TILES])
            power = sb("power", [P, TILES])
            square = sb("square", [P, D])
            chunk_loaded = [sem(f"chunk_loaded{n}") for n in range(2)]
            bits_ready = sem("bits_ready")
            lines_ready = sem("lines_ready")
            dq_step = sem("dq_step")
            value_ready = sem("value_ready")
            decoded = sem("decoded")
            power_set = sem("power_set")
            meansq_ready = sem("meansq_ready")
            rstd_step = sem("rstd_step")
            resid_loaded = sem("resid_loaded")
            final = sem("final")
            bias_m4 = sb("bias_m4", [P, 1])
            bias_m12 = sb("bias_m12", [P, 1])
            bias_half = sb("bias_half", [P, 1])
            bias_set = sem("bias_set")
        else:
            weight, start = routed
            comb = sb("comb", [P, TILES, groups])

        def sums(pe, out, w_hi, w_lo, v_hi, v_lo, start, stop):
            pe.matmul(out, w_hi, v_hi, start=start, stop=False)
            pe.matmul(out, w_hi, v_lo, start=False, stop=False)
            return pe.matmul(out, w_lo, v_hi, start=False, stop=stop)

        def tiles_before(g, b):
            if isinstance(g, int) and g == last_g:
                return steps_before_last * JT + b * LAST_JT
            return (g * BATCHES + b) * JT

        block = ctx.enter_context(nc.Block())

        @block.sync
        def _(sp):
            def load_weights(g):
                sp.dma_start(up_f32[:, :, :, :, :].rearrange("p j m k f -> p (j m k f)"),
                             up_src[bass.ds(g, 1)].rearrange("o p n -> (o p) n")).then_inc(weights_loaded, 16)
                sp.dma_start(down_f32[:, :, :],
                             down_src[bass.ds(g, 1)].rearrange("o (j p) n -> p (o j) n", p=P)).then_inc(weights_loaded, 16)

            def load_chunk(g, c):
                sp.dma_start(words[:, c % 2, :], up_src[bass.ds(g, 1), c].rearrange("o p n -> (o p) n")
                             ).then_inc(chunk_loaded[c % 2], 16)
                sp.dma_start(scales[:, c % 2, :], fp4["scales"][bass.ds(g, 1), c].rearrange("o n -> (o n)").partition_broadcast(P)
                             ).then_inc(chunk_loaded[c % 2], 16)

            def load_x(b):
                for part, dst in ((0, x_hi), (1, x_lo)):
                    sp.dma_start(dst[:, b * TPB:(b + 1) * TPB].bitcast(F32).rearrange("p t k n -> p t (k n)"),
                                 x_parts[part, b * TPB:(b + 1) * TPB].rearrange("t p n -> p t n"),
                                 ).then_inc(x_loaded[b], 16)

            def store(b):
                sp.dma_start(out_dram[bass.ds(b * TPB, TPB)].rearrange("t p n -> p t n"),
                             acc[:, bass.ds(b * TPB, TPB), :]).then_inc(stored, 16)

            if fp4:
                sp.dma_start(shift[:, :], fp4["shift"]).then_inc(aux_loaded, 16)
                load_chunk(0, 0)
                load_chunk(0, 1)
                load_x(0)
                for c in range(2, chunks):
                    sp.wait_ge(decoded, c - 1)
                    load_chunk(0, c)
                    if c in (4, 6, 8):
                        load_x(c // 2 - 1)
                with sp.Fori(0, last_g) as g:
                    for c in range(chunks):
                        back = {0: 0, 1: -1}.get(c, c - 1)
                        sp.wait_ge(decoded, chunks * (g + 1) + back)
                        load_chunk(g + 1, c)
                for b in range(BATCHES):
                    if b:
                        sp.wait_ge(final, TPB * b)
                    sp.dma_start(resid[:, :, :], fp4["resid"][b * TPB:(b + 1) * TPB].rearrange("t p n -> p t n")
                                 ).then_inc(resid_loaded, 16)
                    if b:
                        store(b - 1)
                sp.wait_ge(final, TPB * BATCHES)
                store(BATCHES - 1)
                sp.wait_ge(stored, 16 * BATCHES)
            else:
                load_weights(0)
                load_x(0)
                sp.dma_start(comb[:, :, :], weight).then_inc(aux_loaded, 16)
                load_x(1)
                sp.dma_start(acc[:, :, :], start.rearrange("t p n -> p t n")).then_inc(aux_loaded, 16)
                for b in range(2, BATCHES):
                    load_x(b)
                with sp.Fori(1, groups) as g:
                    sp.wait_ge(weights_lo, 2 * JT * g)
                    load_weights(g)
                with sp.Fori(0, BATCHES) as b:
                    sp.wait_ge(y_free, TPB * (steps_before_last + 1) + TPB * (b + 1))
                    store(b)
                sp.wait_ge(stored, 16 * BATCHES)

        @block.tensor
        def _(pe):
            def step(g, b, odd, tiles=JT):
                n = g * BATCHES + b
                before = tiles_before(g, b)
                tokens = bass.ds(b * TPB, TPB)
                for j in range(tiles):
                    q = (odd * JT + j) % 2
                    pe.wait_ge(gu_free, before + j + 1)
                    pe.wait_ge(weights_lo, 2 * JT * g + j + 1)
                    for m, ps in ((0, gate_ps[q]), (1, up_ps[q])):
                        for k in range(KT):
                            last = sums(pe, ps[:, :], up_hi[:, j, m, k, :], up_lo[:, j, m, k, :],
                                        x_hi[:, tokens, k, :], x_lo[:, tokens, k, :], k == 0, k == KT - 1)
                        last.then_inc(gu_ready, 1)
                for j in range(tiles):
                    pe.wait_ge(h_ready, before + j + 1)
                    pe.wait_ge(weights_lo, 2 * JT * g + JT + j + 1)
                    for t in range(TPB):
                        if j == 0:
                            pe.wait_ge(y_free, n * TPB + t + 1)
                        last = sums(pe, y_ps[t][:, :], h_hi[:, j, t * P:(t + 1) * P], h_lo[:, j, t * P:(t + 1) * P],
                                    down_hi[:, j, :], down_lo[:, j, :], j == 0, j == tiles - 1)
                        if j == tiles - 1:
                            last.then_inc(y_ready, 1)

            for b in range(BATCHES):
                pe.wait_ge(x_loaded[b], 32)
                step(0, b, b % 2)
            with pe.Fori(1, last_g) as g:
                if fp4:
                    for b in range(BATCHES):
                        step(g, b, b % 2)
                else:
                    with pe.Fori(0, BATCHES // 2) as pair:
                        step(g, 2 * pair, 0)
                        step(g, 2 * pair + 1, 1)
            for b in range(BATCHES):
                step(last_g, b, 0, LAST_JT)

        @block.scalar
        def _(act):
            def high_parts(g, first=False):
                if not fp4:
                    act.wait_ge(weights_loaded, 32 * (g + 1))
                for j in range(JT):
                    if fp4:
                        act.wait_ge(decoded, chunks * g + 2 * j + 2)
                    if not first:
                        act.wait_ge(gu_ready, 2 * JT * BATCHES * g - 2 * JT + 2 * j + 2)
                    act.copy(up_hi[:, j], up_f32[:, j]).then_inc(weights_hi, 1)
                    if first and fp4:
                        for c in range(2 * j + 4, min(2 * j + 6, chunks)):
                            curve(c, c)
                if not first:
                    act.wait_ge(y_ready, TPB * BATCHES * g)
                for j in range(JT):
                    if fp4:
                        act.wait_ge(decoded, chunks * g + 2 * JT + j + 1)
                    act.copy(down_hi[:, j, :], down_f32[:, j, :]).then_inc(weights_hi, 1)

            def curve(c_all, c):
                act.wait_ge(bits_ready, c_all + 1)
                act.activation(above4[:, :], magnitude[:, :], ACT.Relu, bias=bias_m4[:, :], scale=1.0)
                act.activation(above6[:, :], magnitude[:, :], ACT.Relu, bias=bias_m12[:, :], scale=2.0)
                act.activation(half_sign[:, :], sign_bit[:, :], ACT.Identity, bias=bias_half[:, :],
                               scale=-0.125).then_inc(lines_ready, 1)

            def step(g, b, odd, tiles=JT):
                for j in range(tiles):
                    q = (odd * JT + j) % 2
                    k = tiles_before(g, b) + j
                    act.wait_ge(gu_ready, 2 * k + 1)
                    act.activation(silu_g[:, q, :], gate_ps[q][:, :], ACT.Silu).then_inc(silu_ready, 1)
                    act.wait_ge(gu_free, k + 3)
                    act.copy(h_hi[:, j, :], h_f32[:, q, :]).then_inc(hhi_ready, 1)
                    if fp4 and tiles == JT:
                        c = b * JT + j
                        if c < chunks:
                            curve(chunks * (g + 1) + c, c)

            if fp4:
                act.wait_ge(bias_set, 3)
                for c in range(4):
                    curve(c, c)
            high_parts(0, first=True)
            if fp4:
                with act.Fori(0, last_g) as g:
                    for b in range(BATCHES):
                        step(g, b, b % 2)
                    high_parts(g + 1)
            else:
                with act.Fori(0, last_g) as g:
                    with act.Fori(0, BATCHES // 2) as pair:
                        step(g, 2 * pair, 0)
                        step(g, 2 * pair + 1, 1)
                    high_parts(g + 1)
            for b in range(BATCHES):
                step(last_g, b, 0, LAST_JT)

        @block.gpsimd
        def _(pool):
            def low_part(g, n):
                pool.wait_ge(weights_hi, 2 * JT * g + n + 1)
                whole, high, low = ((up_f32[:, n], up_hi[:, n], up_lo[:, n]) if n < JT else
                                    (down_f32[:, n - JT, :], down_hi[:, n - JT, :], down_lo[:, n - JT, :]))
                pool.tensor_tensor(low, whole, high.bitcast(F32), ALU.subtract).then_inc(weights_lo, 1)

            def scale_chunk(c_all, c):
                pool.wait_ge(value_ready, c_all + 1)
                to, shape = (up_f32[:, c // 2, c % 2], "p (k f) -> p k f") if c < 2 * JT else (down_f32[:, c - 2 * JT, :], None)
                values, by = value[:, :], scales[:, c % 2, :]
                if shape:
                    values, by = values.rearrange(shape, f=P), by.rearrange(shape, f=P)
                pool.tensor_tensor(to, values, by, ALU.mult).then_inc(decoded, 1)

            if fp4:
                pool.memset(power[:, :], -0.5).then_inc(power_set, 1)
                for c in range(chunks):
                    scale_chunk(c, c)
                    if c in (3, 5):
                        low_part(0, (c - 3) // 2)
                for n in range(2, 2 * JT):
                    low_part(0, n)
                with pool.Fori(0, last_g) as g:
                    pool.wait_ge(weights_lo, 2 * JT * (g + 1))
                    for c in range(chunks):
                        scale_chunk(chunks * (g + 1) + c, c)
                    for n in range(2 * JT):
                        low_part(g + 1, n)
                pool.wait_ge(power_set, 1)
                for b in range(BATCHES):
                    tiles = slice(b * TPB, (b + 1) * TPB)
                    pool.wait_ge(meansq_ready, TPB * (b + 1))
                    pool.tensor_scalar(meansq[:, tiles], meansq[:, tiles], 1.0 / D, 1e-6, ALU.mult, ALU.add).then_inc(rstd_step, 1)
                    pool.wait_ge(rstd_step, 2 * b + 1)
                    pool.tensor_tensor(rstd[:, tiles], meansq[:, tiles], power[:, tiles], ALU.pow).then_inc(rstd_step, 1)
            else:
                with pool.Fori(0, groups) as g:
                    for n in range(2 * JT):
                        low_part(g, n)

        @block.vector
        def _(dve):
            def bits(g, c):
                per_group = (chunks + 1 - c % 2) // 2
                dve.wait_ge(chunk_loaded[c % 2], 32 * (per_group * g + c // 2 + 1))
                for to, mask in ((magnitude, 7), (sign_bit, 8)):
                    last = dve.tensor_scalar(to[:, :], words[:, c % 2, :], shift[:, :], mask,
                                             ALU.logical_shift_right, ALU.bitwise_and)
                last.then_inc(bits_ready, 1)

            def values(g, c):
                c_all = chunks * g + c
                dve.wait_ge(bits_ready, c_all + 1)
                dve.wait_ge(lines_ready, c_all + 1)
                dve.tensor_tensor(twice[:, :], magnitude[:, :], above4[:, :], ALU.add).then_inc(dq_step, 1)
                dve.wait_ge(dq_step, 2 * c_all + 1)
                dve.tensor_tensor(twice[:, :], twice[:, :], above6[:, :], ALU.add).then_inc(dq_step, 1)
                dve.wait_ge(dq_step, 2 * c_all + 2)
                if not (isinstance(c_all, int) and c_all == 0):
                    dve.wait_ge(decoded, c_all)
                dve.tensor_tensor(value[:, :], twice[:, :], half_sign[:, :], ALU.mult).then_inc(value_ready, 1)

            def step(g, b, odd, tiles=JT):
                n = g * BATCHES + b
                for j in range(tiles):
                    q = (odd * JT + j) % 2
                    k = tiles_before(g, b) + j
                    dve.wait_ge(silu_ready, k + 1)
                    dve.wait_ge(gu_ready, 2 * k + 2)
                    dve.tensor_tensor(h_f32[:, q, :], silu_g[:, q, :], up_ps[q][:, :], ALU.mult).then_inc(gu_free, 1)
                    dve.wait_ge(gu_free, k + 3)
                    dve.wait_ge(hhi_ready, k + 1)
                    dve.tensor_tensor(h_lo[:, j, :], h_f32[:, q, :], h_hi[:, j, :].bitcast(F32),
                                      ALU.subtract).then_inc(h_ready, 1)
                    if fp4 and tiles == JT:
                        c = b * JT + j
                        if 1 <= c <= chunks:
                            values(g + 1, c - 1)
                        if c < chunks:
                            bits(g + 1, c)
                for t in range(TPB):
                    tile = acc[:, bass.ds(b * TPB + t, 1), :].rearrange("p o n -> p (o n)")
                    dve.wait_ge(y_ready, n * TPB + t + 1)
                    dve.wait_ge(y_free, n * TPB + t + 1)
                    if fp4:
                        dve.tensor_tensor(tile, tile, y_ps[t][:, :], ALU.add).then_inc(y_free, 1)
                    else:
                        by = comb[:, bass.ds(b * TPB + t, 1), bass.ds(g, 1)].rearrange("p o n -> p (o n)")
                        dve.scalar_tensor_tensor(tile, y_ps[t][:, :], by, tile, ALU.mult, ALU.add).then_inc(y_free, 1)

            def squares(b):
                for i in range(TPB):
                    t = b * TPB + i
                    dve.wait_ge(y_free, TPB * (steps_before_last + 1) + t + 1)
                    if t:
                        dve.wait_ge(meansq_ready, t)
                    dve.tensor_tensor_reduce(square[:, :], acc[:, t, :], acc[:, t, :], 1.0, 0.0, ALU.mult, ALU.add,
                                             meansq[:, t:t + 1]).then_inc(meansq_ready, 1)

            def finish(b):
                dve.wait_ge(rstd_step, 2 * (b + 1))
                dve.wait_ge(resid_loaded, 16 * (b + 1))
                for i in range(TPB):
                    t = b * TPB + i
                    dve.scalar_tensor_tensor(acc[:, t, :], acc[:, t, :], rstd[:, t:t + 1], resid[:, i, :],
                                             ALU.mult, ALU.add).then_inc(final, 1)

            dve.sem_inc(gu_free, 2)
            if fp4:
                dve.memset(bias_m4[:, :], -4.0).then_inc(bias_set, 1)
                dve.memset(bias_m12[:, :], -12.0).then_inc(bias_set, 1)
                dve.memset(bias_half[:, :], 0.5).then_inc(bias_set, 1)
                dve.wait_ge(aux_loaded, 16)
                for c in range(chunks):
                    bits(0, c)
                    values(0, c)
                dve.memset(acc[:, :, :], 0.0).then_inc(y_free, TPB)
                with dve.Fori(0, last_g) as g:
                    for b in range(BATCHES):
                        step(g, b, b % 2)
                for b in range(BATCHES):
                    step(last_g, b, 0, LAST_JT)
                    squares(b)
                    if b:
                        finish(b - 1)
                finish(BATCHES - 1)
            else:
                dve.sem_inc(y_free, TPB)
                dve.wait_ge(aux_loaded, 32)
                with dve.Fori(0, last_g) as g:
                    with dve.Fori(0, BATCHES // 2) as pair:
                        step(g, 2 * pair, 0)
                        step(g, 2 * pair + 1, 1)
                for b in range(BATCHES):
                    step(last_g, b, 0, LAST_JT)


SSM_HEADS = 16
SSM_P = 64
SSM_N = 64
E = SSM_HEADS * SSM_P
ET = E // P
TAPS = 4
CONV_TILES = ET + 2
EXPERTS = 8
SMALL = SSM_HEADS + EXPERTS + 2
HB = E // BANK
HPG = BANK // P
CONV_ORDER = (ET, ET + 1) + tuple(range(ET))
ATANH = tuple(1.0 / (2 * n + 1) for n in range(1, 8))


def ssm_phase(nc, x_dram, wts, tables, x_parts, out_dram, comb_dram):
    name = "a1"
    semaphores = []
    with ExitStack() as ctx:
        ctx.callback(clear_semaphores, nc, semaphores)

        def sb(label, shape, dt=F32):
            return ctx.enter_context(nc.sbuf_tensor(f"{name}_{label}", shape, dt))

        def sem(label):
            semaphores.append(nc.alloc_semaphore(f"{name}_{label}"))
            return semaphores[-1]

        def sems(group, labels):
            return {label: sem(f"{group}_{label}") for label in labels.split()}

        z_hi = sb("z_hi", [P, KT, E], F32R)
        z_lo = sb("z_lo", [P, KT, E], F32R)
        c_hi = sb("c_hi", [P, KT, E + 2 * SSM_N], F32R)
        c_lo = sb("c_lo", [P, KT, E + 2 * SSM_N], F32R)
        small_raw = sb("small_raw", [P, KT, SMALL])
        small_hi = sb("small_hi", [P, KT, SMALL], F32R)
        small_lo = sb("small_lo", [P, KT, SMALL], F32R)
        w_raw = sb("w_raw", [P, 2, KT, P])
        w_out = sb("w_out", [P, ET, D])
        norm_w = sb("norm_w", [P, ET])
        conv_w = sb("conv_w", [P, CONV_TILES, TAPS])
        conv_b = sb("conv_b", [P, CONV_TILES])
        dt_bias = sb("dt_bias", [P, SSM_HEADS])
        a_neg = sb("a_neg", [P, SSM_HEADS])
        skip_d = sb("skip_d", [P, SSM_HEADS])
        ident = sb("ident", [P, P])
        upto = sb("upto", [P, P])
        after = sb("after", [P, P])
        ones = sb("ones", [P, P])
        earlier = sb("earlier", [P, EXPERTS, EXPERTS])
        power = sb("power", [P, 1])
        eps_ln = sb("eps_ln", [P, 1])
        eps_rms = sb("eps_rms", [P, 1])

        x = sb("x", [P, TPB, D])
        x_last = sb("x_last", [P, D])
        y_out = w_raw[:, :, :, :].rearrange("p o k n -> p o (k n)")
        small_t = sb("small_t", [SMALL, BT])
        stats = sb("stats", [P, TPB, 6])
        mean_var = sb("mean_var", [P, TPB, 2])
        ln_tmp = sb("ln_tmp", [P, TPB])
        ln_rs = sb("ln_rs", [P, TPB])
        ln_tmp2 = sb("ln_tmp2", [P, 1])
        xn = sb("xn", [P, 2, D])
        xt_hi = sb("xt_hi", [P, TPB, KT, P], F32R)
        xt_lo = sb("xt_lo", [P, TPB, KT, P], F32R)
        tph = [P, TPB, SSM_HEADS]
        dt_raw, dt_abs, dt_exp, dt_den, dt_z, dt_z2, dt_q, dt_pos, dt, a = (
            sb(label, tph) for label in
            ("dt_raw", "dt_abs", "dt_exp", "dt_den", "dt_z", "dt_z2", "dt_q", "dt_pos", "dt", "a"))
        decays = sb("decays", [P, 3, TPB, SSM_HEADS])
        logits = sb("logits", [P, TPB, EXPERTS + 1])
        top = sb("top", [P, TPB])
        probs = sb("probs", [P, TPB, EXPERTS])
        total = sb("total", [P, TPB])
        greater = sb("greater", [P, TPB, EXPERTS, EXPERTS])
        equal = sb("equal", [P, TPB, EXPERTS, EXPERTS])
        rank = sb("rank", [P, TPB, EXPERTS])
        shared = sb("shared", [P, TPB])
        comb = sb("comb", [P, TPB, EXPERTS + 4])

        conv_acc = sb("conv_acc", [P, 2, BT])
        conv = sb("conv", [P, CONV_TILES, BT])
        b_tok = sb("b_tok", [P, TPB, SSM_N])
        g_mask = sb("g_mask", [P, TPB, P])
        a_mask = sb("a_mask", [P, SSM_HEADS, P])
        l_exp = sb("l_exp", [P, 2, HPG, P])
        m_t = sb("m_t", [P, SSM_HEADS, P])
        h_tok = sb("h_tok", [P, SSM_HEADS, SSM_P])
        h_dt = sb("h_dt", [P, SSM_HEADS, SSM_P])
        h_dec = sb("h_dec", [P, SSM_HEADS, SSM_P])
        z_silu = sb("z_silu", [P, E])
        y = sb("y", [P, SSM_HEADS, SSM_P])
        sq_out = sb("sq_out", [P, E], BF16)
        ss = sb("ss", [P, 1])
        ms = sb("ms", [P, 1])
        y_rs = sb("y_rs", [P, 1])
        yt = sb("yt", [P, ET, P])
        state = sb("state", [SSM_N, SSM_HEADS, SSM_P])

        def banks(label):
            return ctx.enter_context(nc.psum_tensor(f"{name}_{label}", [P, 2, BANK], F32))

        seg_ps, y_ps, off_ps, proj_ps = banks("seg_ps"), banks("y_ps"), banks("off_ps"), banks("proj_ps")

        loaded = sems("loaded", "const")
        w = sems("w", "hi small_hi z_hi split z_split small normed a consts")
        ln = sems("ln", "stats_step stats rstd normed")
        xt = sems("xt", "ps hi lo")
        sm = sems("sm", "sums sums_sb ps dt_raw logits abs exp step dt a")
        rt = sems("rt", "step exp tanh rank ready")
        cv = sems("cv", "ps init step done silu")
        bc = sems("bc", "g_ps g_masked b_ps b_tok cum_ps decays")
        sg = sems("sg", "a_mask ps exp m")
        zz = sems("zz", "ps tanh silu")
        hh = sems("hh", "ps tok dt dec skip")
        yy = sems("yy", "diag_ps off_ps off_scaled diag_added skip_added gated ss ms rs t_ps t_sb out_ps x_added")
        st = sems("st", "ps scaled ready")
        x_in = [sem(f"x_in{n}") for n in range(TPB)]
        last_in = sem("last_in")
        y_stored = [sem(f"y_stored{n}") for n in range(TPB)]
        xt_stored = sem("xt_stored")
        comb_stored = sem("comb_stored")
        w_loaded = [sem(f"w_loaded{n}") for n in range(2)]
        z_loaded = [sem(f"z_loaded{n}") for n in range(2)]
        out_loaded = sem("out_loaded")

        Z_PIECES, C_PIECES = E // P, E // P + 1
        z_raw = (m_t, a_mask)
        N_CONST = 12

        def c_piece(m):
            return Z_PIECES + (m - 1) % C_PIECES

        def c_columns(m):
            return slice(((m - 1) % C_PIECES) * P, ((m - 1) % C_PIECES + 1) * P)

        def z_whole(n):
            return z_raw[n // (Z_PIECES // 2)][:, n % (Z_PIECES // 2) * KT:(n % (Z_PIECES // 2) + 1) * KT, :]

        def heads(ap, n_inner):
            return ap.unsqueeze(2).to_broadcast([ap.shape[0], SSM_HEADS, n_inner])

        block = ctx.enter_context(nc.Block())

        def whole(bank_pair):
            return bank_pair[:, :, :].rearrange("p b n -> p (b n)").rearrange("p (h d) -> p h d", h=SSM_HEADS)

        @block.sync
        def _(sp):
            def load_x(batch, i):
                sp.dma_start(x[:, i, :], x_dram[bass.ds(batch * TPB + i, 1)].rearrange("o p n -> (o p) n")
                             ).then_inc(x_in[i], 16)

            def load_last(batch):
                sp.dma_start(x_last[:, :], x_dram[bass.ds(batch * TPB + TPB - 1, 1)].rearrange("o p n -> (o p) n")
                             ).then_inc(last_in, 16)

            def store_batch_parts(b):
                sp.wait_ge(xt["hi"], TPB * b + TPB)
                sp.wait_ge(xt["lo"], TPB * b + TPB)
                for part, buf in ((0, xt_hi), (1, xt_lo)):
                    sp.dma_start(x_parts[part, bass.ds(b * TPB, TPB)].rearrange("t p n -> p t n"),
                                 buf[:, :, :, :].bitcast(F32).rearrange("p t k n -> p t (k n)")).then_inc(xt_stored, 16)

            def store_y(b, i):
                sp.wait_ge(yy["x_added"], b * TPB + i + 1)
                sp.dma_start(out_dram[bass.ds(b * TPB + i, 1)].rearrange("o p n -> (o p) n"), y_out[:, i % 2, :]
                             ).then_inc(y_stored[i], 16)

            def store_comb(b):
                sp.wait_ge(rt["ready"], b + 1)
                sp.dma_start(comb_dram[:, bass.ds(b * TPB, TPB), :], comb[:, :, :]).then_inc(comb_stored, 16)

            for i in range(TPB):
                load_x(0, i)
            consts = ((ident, tables["ident"]), (small_raw, wts["small"]), (conv_w, wts["conv_w"]), (conv_b, wts["conv_b"]),
                      (dt_bias, wts["dt_bias"].partition_broadcast(P)), (a_neg, wts["a_log"].partition_broadcast(P)),
                      (skip_d, wts["skip_d"].partition_broadcast(P)), (norm_w, wts["norm_w"]),
                      (upto, tables["upto"]), (after, tables["after"]), (ones, tables["ones"]),
                      (earlier, tables["earlier"].partition_broadcast(P)))
            assert len(consts) == N_CONST
            for dst, src in consts:
                sp.dma_start(dst[:], src).then_inc(loaded["const"], 16)
            load_last(0)
            for m in range(C_PIECES):
                if m >= 2:
                    sp.wait_ge(w["split"], m - 1)
                sp.dma_start(w_raw[:, m % 2, :, :], wts["in_proj"][c_piece(m)]).then_inc(w_loaded[m % 2], 16)
                if m in (3, 5):
                    n = (m - 3) // 2
                    sp.dma_start(z_raw[n][:, :, :].rearrange("p (n k) f -> p n (k f)", k=KT),
                                 wts["in_proj"][n * Z_PIECES // 2:(n + 1) * Z_PIECES // 2].rearrange("n p k f -> p n (k f)")
                                 ).then_inc(z_loaded[n], 16)
            sp.dma_start(w_out[:, :, :], wts["out_proj"]).then_inc(out_loaded, 16)
            store_batch_parts(0)
            sp.wait_ge(ln["normed"], TPB)
            load_x(1, 3)

            def body(b, last):
                store_comb(b)
                for i in range(TPB - 1):
                    store_y(b, i)
                    if not last:
                        load_x(b + 1, i)
                if not last:
                    store_batch_parts(b + 1)
                    sp.wait_ge(ln["normed"], TPB * (b + 2))
                    load_x((b + 2) % BATCHES, 3)
                store_y(b, TPB - 1)
                if not last:
                    load_last(b + 1)

            with sp.Fori(0, BATCHES - 1) as b:
                body(b, False)
            body(BATCHES - 1, True)
            sp.wait_ge(comb_stored, 16 * BATCHES)
            sp.wait_ge(xt_stored, 32 * BATCHES)
            for i in range(TPB):
                sp.wait_ge(y_stored[i], 16 * BATCHES)
            sp.wait_ge(x_in[3], 16 * (BATCHES + 1))

        @block.tensor
        def _(pe):
            def sums(to, l_hi, l_lo, r_hi, r_lo, k):
                pe.matmul(to, l_hi, r_hi, start=k == 0, stop=False)
                pe.matmul(to, l_hi, r_lo, start=False, stop=False)
                return pe.matmul(to, l_lo, r_hi, start=False, stop=k == KT - 1)

            def x_turned(b, first):
                for i in range(TPB):
                    pe.wait_ge(ln["normed"], TPB * b + i + 1)
                    if i >= 2:
                        pe.wait_ge(xt["hi"], TPB * b + i - 1)
                        pe.wait_ge(xt["lo"], TPB * b + i - 1)
                    elif not first:
                        pe.wait_ge(sg["exp"], HPG * TPB * b)
                    for k in range(KT):
                        last = pe.transpose(seg_ps[:, i % 2, k * P:(k + 1) * P], xn[:, i % 2, k * P:(k + 1) * P], ident[:, :])
                    last.then_inc(xt["ps"], 1)
                pe.wait_ge(xt["hi"], TPB * (b + 1))
                pe.wait_ge(xt["lo"], TPB * (b + 1))

            def small_proj(b):
                for k in range(KT):
                    last = sums(seg_ps[0:SMALL, 1, :], small_hi[:, k, :], small_lo[:, k, :], xt_hi[:, :, k, :], xt_lo[:, :, k, :], k)
                last.then_inc(sm["sums"], 1)

            def small_turned(b):
                for i in range(TPB):
                    last = pe.transpose(seg_ps[:, 0, i * SMALL:(i + 1) * SMALL], small_t[:, i * P:(i + 1) * P],
                                        ident[0:SMALL, 0:SMALL])
                last.then_inc(sm["ps"], 1)

            def conv_proj(b, q, first):
                f = CONV_ORDER[q]
                rows, cols = (P, slice(f * P, (f + 1) * P)) if f < ET else (
                    SSM_N, slice(E + (f - ET) * SSM_N, E + (f - ET + 1) * SSM_N))
                if first:
                    pe.wait_ge(w["split"], max(q, 1))
                if q >= 2:
                    pe.wait_ge(cv["done"], CONV_TILES * b + q - 1)
                elif not first:
                    pe.wait_ge(zz["silu"], HB * TPB * b)
                for k in range(KT):
                    last = sums(proj_ps[0:rows, q % 2, :], c_hi[:, k, cols], c_lo[:, k, cols], xt_hi[:, :, k, :], xt_lo[:, :, k, :], k)
                last.then_inc(cv["ps"], 1)

            def grams(b):
                pe.wait_ge(cv["silu"], CONV_TILES * b + 2)
                pe.wait_ge(sm["logits"], b + 1)
                for i in range(TPB):
                    cols = slice(i * P, (i + 1) * P)
                    last = pe.matmul(seg_ps[:, 1, cols], conv[0:SSM_N, ET, cols], conv[0:SSM_N, ET + 1, cols], start=True, stop=True)
                last.then_inc(bc["g_ps"], 1)
                for i in range(TPB):
                    last = pe.transpose(seg_ps[:, 0, i * SSM_N:(i + 1) * SSM_N], conv[0:SSM_N, ET, i * P:(i + 1) * P],
                                        ident[0:SSM_N, 0:SSM_N])
                last.then_inc(bc["b_ps"], 1)

            def cumulate(b):
                pe.wait_ge(sm["a"], b + 1)
                pe.wait_ge(bc["b_tok"], b + 1)
                n = TPB * SSM_HEADS
                for m, mask in enumerate((after, upto, ones)):
                    last = pe.matmul(seg_ps[:, 0, m * n:(m + 1) * n], mask[:, :], a[:, :, :].rearrange("p t h -> p (t h)"),
                                     start=True, stop=True)
                last.then_inc(bc["cum_ps"], 1)

            def segments(t, i, b):
                pe.wait_ge(sg["a_mask"], t + 1)
                for g in range(HPG):
                    if g >= 2:
                        pe.wait_ge(sg["exp"], HPG * t + g - 1)
                    elif i:
                        pe.wait_ge(sg["exp"], HPG * t - 1 + g)
                    elif g == 0:
                        pe.wait_ge(bc["decays"], b + 1)
                    else:
                        pe.wait_ge(bc["g_masked"], b + 1)
                    pe.matmul(seg_ps[:, g % 2, :], after[:, :], a_mask[:, g * HPG:(g + 1) * HPG, :],
                              start=True, stop=True).then_inc(sg["ps"], 1)

            def z_proj(t, i, b, half):
                if isinstance(t, int) and half == 0:
                    pe.wait_ge(w["z_split"], Z_PIECES)
                pe.wait_ge(hh["tok"], HB * t + half + 1)
                for k in range(KT):
                    cols = slice(half * BANK, (half + 1) * BANK)
                    last = sums(proj_ps[:, half, :], xt_hi[:, i, k, :], xt_lo[:, i, k, :], z_hi[:, k, cols], z_lo[:, k, cols], k)
                last.then_inc(zz["ps"], 1)

            def h_turned(t, i, b, half):
                if i == 0:
                    pe.wait_ge(cv["silu"], CONV_TILES * (b + 1))
                else:
                    pe.wait_ge(zz["silu"], HB * t - 1 + half)
                for f in range(ET // HB):
                    last = pe.transpose(proj_ps[:, half, f * P:(f + 1) * P],
                                        conv[:, half * (ET // HB) + f, i * P:(i + 1) * P], ident[:, :])
                last.then_inc(hh["ps"], 1)

            def y_turned(t):
                pe.wait_ge(yy["gated"], t + 1)
                for f in range(ET):
                    last = pe.transpose(y_ps[:, f // HPG, (f % HPG) * P:(f % HPG + 1) * P],
                                        y[:, 2 * f:2 * f + 2, :].rearrange("p h d -> p (h d)"), ident[:, :])
                last.then_inc(yy["t_ps"], 1)

            def out_proj(t):
                pe.wait_ge(yy["t_sb"], t + 1)
                for f in range(ET):
                    last = pe.matmul(off_ps[:, 0, :], yt[:, f, :], w_out[:, f, :], start=f == 0, stop=f == ET - 1)
                last.then_inc(yy["out_ps"], 1)

            def project_batch(b, before):
                first = before is None
                x_turned(b, first)
                if first:
                    pe.wait_ge(w["small"], 1)
                small_proj(b)
                for q in range(CONV_TILES):
                    if q == 1:
                        pe.wait_ge(sm["sums_sb"], b + 1)
                    conv_proj(b, q, first)
                    if q == 1:
                        small_turned(b)
                    if q == 4:
                        grams(b)
                    if q == 6 and not first:
                        y_turned(before)
                cumulate(b)
                if not first:
                    out_proj(before)

            def ahead(t, i, b):
                for half in range(HB):
                    h_turned(t, i, b, half)
                segments(t, i, b)
                for half in range(HB):
                    z_proj(t, i, b, half)

            pe.wait_ge(loaded["const"], 16 * N_CONST)
            project_batch(0, None)
            ahead(0, 0, 0)

            def body(b, last):
                for i in range(TPB):
                    t = b * TPB + i
                    if i:
                        pe.wait_ge(st["ready"], 3 * b + i)
                        for half in (1, 0):
                            if half == 0:
                                pe.wait_ge(yy["x_added"], t)
                            mm = pe.matmul(off_ps[:, half, :], conv[0:SSM_N, ET + 1, i * P:(i + 1) * P],
                                           state[:, half * 8:(half + 1) * 8, :], start=True, stop=True)
                        mm.then_inc(yy["off_ps"], 1)
                    pe.wait_ge(sg["m"], HPG * (t + 1))
                    pe.wait_ge(hh["dt"], t + 1)
                    if not (isinstance(b, int) and b == 0 and i == 0) and i:
                        pe.wait_ge(yy["t_sb"], t)
                    for h in range(SSM_HEADS):
                        mm = pe.matmul(y_ps[:, h // 8, (h % 8) * SSM_P:(h % 8 + 1) * SSM_P], m_t[:, h, :], h_dt[:, h, :],
                                       start=True, stop=True)
                    mm.then_inc(yy["diag_ps"], 1)
                    if i < TPB - 1:
                        segments(t + 1, i + 1, b)
                        pe.wait_ge(hh["dec"], t + 1)
                        if i:
                            pe.wait_ge(yy["off_scaled"], 3 * b + i)
                        for half in range(HB):
                            mm = pe.matmul(off_ps[0:SSM_N, half, :], b_tok[:, i, :], h_dec[:, half * 8:(half + 1) * 8, :],
                                           start=True, stop=True)
                        mm.then_inc(st["ps"], 1)
                        for half in range(HB):
                            h_turned(t + 1, i + 1, b, half)
                        y_turned(t)
                        for half in range(HB):
                            z_proj(t + 1, i + 1, b, half)
                        pe.wait_ge(st["ready"], 3 * b + i + 1)
                        out_proj(t)
                    elif last:
                        y_turned(t)
                        out_proj(t)
                    else:
                        project_batch(b + 1, t)
                        ahead(t + 1, 0, b + 1)

            with pe.Fori(0, BATCHES - 1) as b:
                body(b, False)
            body(BATCHES - 1, True)

        @block.scalar
        def _(act):
            def project_batch(b, before):
                first = before is None
                if not first:
                    act.wait_ge(zz["ps"], HB * TPB * b)
                    act.wait_ge(xt_stored, 32 * b)
                for i in range(TPB):
                    act.wait_ge(xt["ps"], TPB * b + i + 1)
                    act.copy(xt_hi[:, i, :, :], seg_ps[:, i % 2, :].rearrange("p (k n) -> p k n", k=KT)).then_inc(xt["hi"], 1)
                    if i == 1:
                        if first:
                            w_small_high()
                            w_high(0)
                            w_high(1)
                act.wait_ge(sm["sums"], b + 1)
                act.copy(small_t[:, :], seg_ps[0:SMALL, 1, :]).then_inc(sm["sums_sb"], 1)
                if not first:
                    square(before)
                for q in range(CONV_TILES + 1):
                    if first:
                        if q + 2 < C_PIECES:
                            w_high(q + 2)
                        if 0 <= q - 3 < Z_PIECES:
                            z_high(q - 3)
                    if q < CONV_TILES:
                        f = CONV_ORDER[q]
                        rows = slice(0, P if f < ET else SSM_N)
                        act.wait_ge(cv["ps"], CONV_TILES * b + q + 1)
                        if q >= 2:
                            act.wait_ge(cv["silu"], CONV_TILES * b + q - 1)
                        act.activation(conv_acc[rows, q % 2, :], proj_ps[rows, q % 2, :], ACT.Identity,
                                       bias=conv_b[rows, f:f + 1], scale=conv_w[rows, f, TAPS - 1:TAPS]).then_inc(cv["init"], 1)
                    if q:
                        f = CONV_ORDER[q - 1]
                        rows = slice(0, P if f < ET else SSM_N)
                        act.wait_ge(cv["done"], CONV_TILES * b + q)
                        act.activation(conv[rows, f, :], conv_acc[rows, (q - 1) % 2, :], ACT.Silu).then_inc(cv["silu"], 1)
                    if q == 2:
                        act.wait_ge(sm["dt_raw"], b + 1)
                        act.activation(dt_abs[:, :, :], dt_raw[:, :, :], ACT.Abs).then_inc(sm["abs"], 1)
                        act.wait_ge(sm["abs"], b + 1)
                        act.activation(dt_exp[:, :, :], dt_abs[:, :, :], ACT.Exp, scale=-1.0).then_inc(sm["exp"], 1)
                        act.wait_ge(rt["step"], 7 * b + 2)
                        act.activation(probs[:, :, :], logits[:, :, 0:EXPERTS], ACT.Exp).then_inc(rt["exp"], 1)
                        act.activation(shared[:, :], logits[:, :, EXPERTS], ACT.Tanh, scale=0.5).then_inc(rt["tanh"], 1)
                    if q == 5:
                        act.wait_ge(bc["b_ps"], b + 1)
                        act.copy(b_tok[:, :, :], seg_ps[:, 0, 0:TPB * SSM_N].rearrange("p (t n) -> p t n", t=TPB)
                                 ).then_inc(bc["b_tok"], 1)
                    if q == 8 and not first:
                        y_out_copy(before)
                act.wait_ge(bc["cum_ps"], b + 1)
                act.activation(decays[:, :, :, :].rearrange("p m t h -> p (m t h)"), seg_ps[:, 0, 0:3 * TPB * SSM_HEADS],
                               ACT.Exp).then_inc(bc["decays"], 1)

            def w_small_high():
                act.wait_ge(loaded["const"], 16 * N_CONST)
                act.copy(small_hi[:, :, :], small_raw[:, :, :]).then_inc(w["small_hi"], 1)
                act.activation(a_neg[:, :], a_neg[:, :], ACT.Exp).then_inc(w["a"], 1)

            def w_high(m):
                act.wait_ge(w_loaded[m % 2], 16 * (m // 2 + 1))
                act.copy(c_hi[:, :, c_columns(m)], w_raw[:, m % 2, :, :]).then_inc(w["hi"], 1)

            def z_high(n):
                act.wait_ge(z_loaded[n // (Z_PIECES // 2)], 16)
                act.copy(z_hi[:, :, n * P:(n + 1) * P], z_whole(n)).then_inc(w["z_hi"], 1)

            def segments(t):
                for g in range(HPG):
                    act.wait_ge(sg["ps"], HPG * t + g + 1)
                    if not (isinstance(t, int) and t == 0 and g < 2):
                        act.wait_ge(sg["m"], HPG * t + g - 1)
                    act.activation(l_exp[:, g % 2, :, :], seg_ps[:, g % 2, :].rearrange("p (h l) -> p h l", h=HPG),
                                   ACT.Exp).then_inc(sg["exp"], 1)

            def z_tanh(t, half):
                if half == 0 and not (isinstance(t, int) and t == 0):
                    act.wait_ge(yy["gated"], t)
                act.wait_ge(zz["ps"], HB * t + half + 1)
                act.activation(z_silu[:, half * BANK:(half + 1) * BANK], proj_ps[:, half, :], ACT.Tanh, scale=0.5
                               ).then_inc(zz["tanh"], 1)

            def h_copied(t):
                if not (isinstance(t, int) and t == 0):
                    act.wait_ge(yy["skip_added"], t)
                    act.wait_ge(hh["dec"], t)
                for half in range(HB):
                    act.wait_ge(hh["ps"], HB * t + half + 1)
                    act.copy(h_tok[:, half * 8:(half + 1) * 8, :], proj_ps[:, half, :].rearrange("p (h d) -> p h d", d=SSM_P)
                             ).then_inc(hh["tok"], 1)

            def ahead(t):
                h_copied(t)
                segments(t)
                z_tanh(t, 0)
                z_tanh(t, 1)

            def square(t):
                act.wait_ge(yy["gated"], t + 1)
                if not (isinstance(t, int) and t == 0):
                    act.wait_ge(yy["ms"], t)
                act.activation(sq_out[:, :], y[:, :, :].rearrange("p h d -> p (h d)"), ACT.Square,
                               accum_out=ss[:, :]).then_inc(yy["ss"], 1)

            def y_out_copy(t):
                act.wait_ge(yy["t_ps"], t + 1)
                act.copy(yt[:, :, :], y_ps[:, :, :].rearrange("p b (f n) -> p (b f) n", n=P)).then_inc(yy["t_sb"], 1)

            act.wait_ge(w["consts"], 3)
            project_batch(0, None)
            ahead(0)

            def body(b, last):
                for i in range(TPB):
                    t = b * TPB + i
                    if i < TPB - 1:
                        segments(t + 1)
                        h_copied(t + 1)
                        y_out_copy(t)
                        z_tanh(t + 1, 0)
                        z_tanh(t + 1, 1)
                        square(t)
                    elif last:
                        square(t)
                        y_out_copy(t)
                    else:
                        project_batch(b + 1, t)
                        ahead(t + 1)

            with act.Fori(0, BATCHES - 1) as b:
                body(b, False)
            body(BATCHES - 1, True)

        @block.gpsimd
        def _(pool):
            def rstd_pair(b, pair):
                tiles = slice(2 * pair, 2 * pair + 2)
                pool.wait_ge(ln["stats"], TPB * b + 2 * pair + 2)
                pool.tensor_tensor(ln_tmp[:, tiles], mean_var[:, tiles, 1], eps_ln[:, :].to_broadcast([P, 2]), ALU.add
                                   ).then_inc(ln["rstd"], 1)
                pool.wait_ge(ln["rstd"], 4 * b + 2 * pair + 1)
                pool.tensor_tensor(ln_rs[:, tiles], ln_tmp[:, tiles], power[:, :].to_broadcast([P, 2]), ALU.pow).then_inc(ln["rstd"], 1)

            def mask_a(t, i, b):
                if i == 0:
                    pool.wait_ge(sm["a"], b + 1)
                if not (isinstance(t, int) and t == 0):
                    pool.wait_ge(sg["ps"], HPG * t)
                pool.tensor_tensor(a_mask[:, :, :], heads(a[:, i, :], P), upto[:, :].unsqueeze(1).to_broadcast([P, SSM_HEADS, P]),
                                   ALU.mult).then_inc(sg["a_mask"], 1)

            def h_products(t, i, b):
                pool.wait_ge(hh["tok"], HB * (t + 1))
                if not (isinstance(t, int) and t == 0):
                    pool.wait_ge(yy["diag_ps"], t)
                pool.tensor_tensor(h_dt[:, :, :], h_tok[:, :, :], heads(dt[:, i, :], SSM_P), ALU.mult).then_inc(hh["dt"], 1)
                pool.wait_ge(hh["dt"], t + 1)
                if i == 0:
                    pool.wait_ge(bc["decays"], b + 1)
                if i:
                    pool.wait_ge(st["ps"], 3 * b + i)
                pool.tensor_tensor(h_dec[:, :, :], h_dt[:, :, :], heads(decays[:, 0, i, :], SSM_P), ALU.mult).then_inc(hh["dec"], 1)
                pool.tensor_tensor(h_tok[:, :, :], h_tok[:, :, :], heads(skip_d[:, :], SSM_P), ALU.mult).then_inc(hh["skip"], 1)

            def rms(t):
                pool.wait_ge(yy["ss"], t + 1)
                pool.tensor_tensor(ms[:, :], ss[:, :], eps_rms[:, :], ALU.add).then_inc(yy["ms"], 1)
                pool.wait_ge(yy["ms"], t + 1)
                if not (isinstance(t, int) and t == 0):
                    pool.wait_ge(yy["x_added"], t)
                pool.tensor_tensor(y_rs[:, :], ms[:, :], power[:, :], ALU.pow).then_inc(yy["rs"], 1)

            pool.memset(power[:, :], -0.5).then_inc(w["consts"], 1)
            pool.memset(eps_ln[:, :], 1e-5).then_inc(w["consts"], 1)
            pool.memset(eps_rms[:, :], 4 * E * 1e-6).then_inc(w["consts"], 1)
            pool.wait_ge(w["consts"], 3)
            rstd_pair(0, 0)
            rstd_pair(0, 1)
            for n in range(Z_PIECES):
                cols = slice(n * P, (n + 1) * P)
                pool.wait_ge(w["z_hi"], n + 1)
                pool.tensor_tensor(z_lo[:, :, cols], z_whole(n), z_hi[:, :, cols].bitcast(F32), ALU.subtract
                                   ).then_inc(w["z_split"], 1)
            pool.wait_ge(loaded["const"], 16 * N_CONST)
            pool.wait_ge(w["z_split"], Z_PIECES)
            mask_a(0, 0, 0)
            h_products(0, 0, 0)
            mask_a(1, 1, 0)

            def body(b, last):
                for i in range(TPB):
                    t = b * TPB + i
                    if i in (1, 2):
                        pool.wait_ge(yy["off_ps"], 3 * b + i)
                        pool.tensor_tensor(state[:, :, :], state[:, :, :], heads(decays[0:SSM_N, 2, i, :], SSM_P),
                                           ALU.mult).then_inc(st["scaled"], 1)
                    if i == TPB - 1 and not last:
                        rstd_pair(b + 1, 0)
                        rstd_pair(b + 1, 1)
                    rms(t)
                    if i < TPB - 1:
                        h_products(t + 1, i + 1, b)
                        if i < TPB - 2:
                            mask_a(t + 2, i + 2, b)
                    elif not last:
                        mask_a(t + 1, 0, b + 1)
                        h_products(t + 1, 0, b + 1)
                        mask_a(t + 2, 1, b + 1)

            with pool.Fori(0, BATCHES - 1) as b:
                body(b, False)
            body(BATCHES - 1, True)

        @block.vector
        def _(dve):
            def small_parts(b):
                dve.wait_ge(sm["ps"], b + 1)
                small = seg_ps[:, 0, 0:TPB * SMALL].rearrange("p (t c) -> p t c", t=TPB)
                dve.tensor_tensor(dt_raw[:, :, :], small[:, :, 0:SSM_HEADS], dt_bias[:, :].unsqueeze(1).to_broadcast(tph),
                                  ALU.add).then_inc(sm["dt_raw"], 1)
                dve.tensor_copy(logits[:, :, :], small[:, :, SSM_HEADS:SSM_HEADS + EXPERTS + 1]).then_inc(sm["logits"], 1)
                dve.wait_ge(sm["dt_raw"], b + 1)
                dve.tensor_scalar(dt_pos[:, :, :], dt_raw[:, :, :], 0.0, None, ALU.max)
                softmax_max(b)

            def softplus(b, second_half):
                STEPS = 5 + len(ATANH)
                n = [STEPS * b + (5 if second_half else 0)]

                def step(ins):
                    ins.then_inc(sm["step"], 1)
                    n[0] = n[0] + 1
                    dve.wait_ge(sm["step"], n[0])

                if not second_half:
                    dve.wait_ge(sm["exp"], b + 1)
                    step(dve.tensor_scalar(dt_den[:, :, :], dt_exp[:, :, :], 2.0, None, ALU.add))
                    step(dve.reciprocal(dt_den[:, :, :], dt_den[:, :, :]))
                    step(dve.tensor_tensor(dt_z[:, :, :], dt_exp[:, :, :], dt_den[:, :, :], ALU.mult))
                    step(dve.tensor_tensor(dt_z2[:, :, :], dt_z[:, :, :], dt_z[:, :, :], ALU.mult))
                    step(dve.tensor_scalar(dt_q[:, :, :], dt_z2[:, :, :], ATANH[-1], None, ALU.mult))
                    return
                for c in ATANH[-2::-1]:
                    step(dve.scalar_tensor_tensor(dt_q[:, :, :], dt_q[:, :, :], c, dt_z2[:, :, :], ALU.add, ALU.mult))
                step(dve.scalar_tensor_tensor(dt_q[:, :, :], dt_q[:, :, :], 1.0, dt_z[:, :, :], ALU.add, ALU.mult))
                dve.scalar_tensor_tensor(dt[:, :, :], dt_q[:, :, :], 2.0, dt_pos[:, :, :], ALU.mult, ALU.add).then_inc(sm["dt"], 1)
                dve.wait_ge(sm["dt"], b + 1)
                dve.scalar_tensor_tensor(a[:, :, :], dt[:, :, :], -1.0, a_neg[:, :].unsqueeze(1).to_broadcast(tph),
                                         ALU.mult, ALU.mult).then_inc(sm["a"], 1)

            def softmax_max(b):
                dve.wait_ge(sm["logits"], b + 1)
                dve.tensor_reduce(top[:, :], logits[:, :, 0:EXPERTS], AX_X, ALU.max).then_inc(rt["step"], 1)
                dve.wait_ge(rt["step"], 7 * b + 1)
                dve.tensor_tensor(logits[:, :, 0:EXPERTS], logits[:, :, 0:EXPERTS],
                                  top[:, :].unsqueeze(2).to_broadcast([P, TPB, EXPERTS]), ALU.subtract).then_inc(rt["step"], 1)

            def route(b):
                pairs = [P, TPB, EXPERTS, EXPERTS]
                dve.wait_ge(rt["exp"], b + 1)
                dve.tensor_reduce(total[:, :], probs[:, :, :], AX_X, ALU.add).then_inc(rt["step"], 1)
                dve.wait_ge(rt["step"], 7 * b + 3)
                dve.reciprocal(total[:, :], total[:, :]).then_inc(rt["step"], 1)
                dve.wait_ge(rt["step"], 7 * b + 4)
                dve.tensor_tensor(probs[:, :, :], probs[:, :, :], total[:, :].unsqueeze(2).to_broadcast([P, TPB, EXPERTS]),
                                  ALU.mult).then_inc(rt["step"], 1)
                dve.wait_ge(rt["step"], 7 * b + 5)
                other = probs[:, :, :].unsqueeze(2).to_broadcast(pairs)
                own = probs[:, :, :].unsqueeze(3).to_broadcast(pairs)
                dve.tensor_tensor(greater[:, :, :, :], other, own, ALU.is_gt)
                dve.tensor_tensor(equal[:, :, :, :], other, own, ALU.is_equal).then_inc(rt["step"], 1)
                dve.wait_ge(rt["step"], 7 * b + 6)
                dve.tensor_tensor(equal[:, :, :, :], equal[:, :, :, :], earlier[:, :, :].unsqueeze(1).to_broadcast(pairs),
                                  ALU.mult).then_inc(rt["step"], 1)
                dve.wait_ge(rt["step"], 7 * b + 7)
                dve.tensor_tensor(greater[:, :, :, :], greater[:, :, :, :], equal[:, :, :, :], ALU.add).then_inc(rt["rank"], 1)
                dve.wait_ge(rt["rank"], 2 * b + 1)
                dve.tensor_reduce(rank[:, :, :], greater[:, :, :, :], AX_X, ALU.add).then_inc(rt["rank"], 1)
                dve.wait_ge(rt["rank"], 2 * b + 2)
                if not (isinstance(b, int) and b == 0):
                    dve.wait_ge(comb_stored, 16 * b)
                dve.scalar_tensor_tensor(comb[:, :, 0:EXPERTS], rank[:, :, :], 2.0, probs[:, :, :], ALU.is_lt, ALU.mult)
                dve.wait_ge(rt["tanh"], b + 1)
                dve.tensor_scalar(comb[:, :, EXPERTS:EXPERTS + 4], shared[:, :].unsqueeze(2).to_broadcast([P, TPB, 4]), 0.5, 0.5,
                                  ALU.mult, ALU.add).then_inc(rt["ready"], 1)

            def project_batch(b, before):
                first = before is None
                if first:
                    pair_stats(b, 0)
                    pair_normed(b, 0, 0)
                    pair_normed(b, 0, 1)
                    pair_stats(b, 1)
                low_part(b, 0)
                low_part(b, 1)
                pair_normed(b, 1, 0)
                pair_normed(b, 1, 1)
                if first:
                    w_small_low()
                    w_low(0)
                    w_low(1)
                low_part(b, 2)
                low_part(b, 3)
                if not first:
                    y_gated(before, TPB - 1, b - 1)
                for q in range(CONV_TILES):
                    f = CONV_ORDER[q]
                    rows = slice(0, P if f < ET else SSM_N)
                    for tap in range(1, TAPS):
                        if tap == 1:
                            dve.wait_ge(cv["init"], CONV_TILES * b + q + 1)
                        else:
                            dve.wait_ge(cv["step"], (TAPS - 2) * (CONV_TILES * b + q) + tap - 1)
                        acc = conv_acc[rows, q % 2, tap:BT]
                        last = dve.scalar_tensor_tensor(acc, proj_ps[rows, q % 2, 0:BT - tap],
                                                        conv_w[rows, f, TAPS - 1 - tap:TAPS - tap], acc, ALU.mult, ALU.add)
                        last.then_inc(cv["done"] if tap == TAPS - 1 else cv["step"], 1)
                    if q == 6:
                        dve.wait_ge(bc["g_ps"], b + 1)
                        dve.tensor_tensor(g_mask[:, :, :], seg_ps[:, 1, :].rearrange("p (t l) -> p t l", t=TPB),
                                          upto[:, :].unsqueeze(1).to_broadcast([P, TPB, P]), ALU.mult).then_inc(bc["g_masked"], 1)
                    if q == 1:
                        small_parts(b)
                    if q in (3, 4):
                        softplus(b, q == 4)
                    if first and q + 2 < C_PIECES:
                        w_low(q + 2)
                if not first:
                    add_out(before, TPB - 1, b - 1)
                route(b)

            def pair_stats(b, pair):
                for i in (2 * pair, 2 * pair + 1):
                    dve.wait_ge(x_in[i], 16 * b + 16)
                    last = dve.bn_stats(stats[:, i, :], x[:, i, :])
                last.then_inc(ln["stats_step"], 1)
                dve.wait_ge(ln["stats_step"], 2 * b + pair + 1)
                dve.tensor_copy(ln_tmp2[:, :], stats[:, 2 * pair + 1, 0:1])
                for i in (2 * pair, 2 * pair + 1):
                    dve.bn_aggr(mean_var[:, i, :], stats[:, i, :]).then_inc(ln["stats"], 1)

            def pair_normed(b, pair, n):
                i = 2 * pair + n
                dve.wait_ge(ln["rstd"], 4 * b + 2 * pair + 2)
                if pair:
                    dve.wait_ge(xt["ps"], TPB * b + i - 1)
                dve.tensor_scalar(xn[:, i % 2, :], x[:, i, :], mean_var[:, i, 0:1], ln_rs[:, i:i + 1],
                                  ALU.subtract, ALU.mult).then_inc(ln["normed"], 1)

            def low_part(b, i):
                dve.wait_ge(xt["hi"], TPB * b + i + 1)
                dve.tensor_tensor(xt_lo[:, i, :, :], seg_ps[:, i % 2, :].rearrange("p (k n) -> p k n", k=KT),
                                  xt_hi[:, i, :, :].bitcast(F32), ALU.subtract).then_inc(xt["lo"], 1)

            def w_small_low():
                dve.wait_ge(w["small_hi"], 1)
                dve.wait_ge(loaded["const"], 16 * N_CONST)
                dve.tensor_tensor(small_lo[:, :, :], small_raw[:, :, :], small_hi[:, :, :].bitcast(F32), ALU.subtract
                                  ).then_inc(w["small"], 1)
                dve.wait_ge(w["a"], 1)

            def w_low(m):
                dve.wait_ge(w["hi"], m + 1)
                dve.tensor_tensor(c_lo[:, :, c_columns(m)], w_raw[:, m % 2, :, :], c_hi[:, :, c_columns(m)].bitcast(F32),
                                  ALU.subtract).then_inc(w["split"], 1)

            def z_gated(t, half):
                dve.wait_ge(zz["tanh"], HB * t + half + 1)
                cols = slice(half * BANK, (half + 1) * BANK)
                dve.scalar_tensor_tensor(z_silu[:, cols], z_silu[:, cols], 1.0, proj_ps[:, half, :], ALU.add, ALU.mult
                                         ).then_inc(zz["silu"], 1)

            def m_products(t, i):
                for g in range(HPG):
                    dve.wait_ge(sg["exp"], HPG * t + g + 1)
                    dve.tensor_tensor(m_t[:, g * HPG:(g + 1) * HPG, :], l_exp[:, g % 2, :, :],
                                      g_mask[:, i:i + 1, :].to_broadcast([P, HPG, P]), ALU.mult).then_inc(sg["m"], 1)

            def add_out(t, i, b):
                dve.wait_ge(yy["out_ps"], t + 1)
                dve.wait_ge(yy["rs"], t + 1)
                if i == TPB - 1:
                    dve.wait_ge(last_in, 16 * b + 16)
                if i >= 2:
                    dve.wait_ge(y_stored[i - 2], 16 * b + 16)
                elif not (isinstance(b, int) and b == 0):
                    dve.wait_ge(y_stored[i + 2], 16 * b)
                residual = x_last[:, :] if i == TPB - 1 else x[:, i, :]
                dve.scalar_tensor_tensor(y_out[:, i % 2, :], off_ps[:, 0, :], y_rs[:, :], residual, ALU.mult, ALU.add
                                         ).then_inc(yy["x_added"], 1)

            project_batch(0, None)
            dve.wait_ge(out_loaded, 16)
            for f in range(ET):
                dve.tensor_scalar(w_out[:, f, :], w_out[:, f, :], norm_w[:, f:f + 1], float(E) ** 0.5, ALU.mult, ALU.mult
                                  ).then_inc(w["normed"], 1)
            dve.wait_ge(w["z_split"], Z_PIECES)
            m_products(0, 0)
            for half in range(HB):
                z_gated(0, half)

            def off_scaled(t, i, b):
                dve.wait_ge(yy["off_ps"], 3 * b + i)
                dve.tensor_tensor(y[:, :, :], whole(off_ps), heads(decays[:, 1, i, :], SSM_P), ALU.mult).then_inc(yy["off_scaled"], 1)

            def y_gated(t, i, b):
                if i:
                    dve.wait_ge(yy["off_scaled"], 3 * b + i)
                    dve.wait_ge(yy["diag_ps"], t + 1)
                    dve.tensor_tensor(y[:, :, :], y[:, :, :], whole(y_ps), ALU.add).then_inc(yy["diag_added"], 1)
                    dve.wait_ge(yy["diag_added"], 3 * b + i)
                    dve.wait_ge(hh["skip"], t + 1)
                    dve.tensor_tensor(y[:, :, :], y[:, :, :], h_tok[:, :, :], ALU.add).then_inc(yy["skip_added"], 1)
                else:
                    dve.wait_ge(yy["diag_ps"], t + 1)
                    dve.wait_ge(hh["skip"], t + 1)
                    dve.tensor_tensor(y[:, :, :], h_tok[:, :, :], whole(y_ps), ALU.add).then_inc(yy["skip_added"], 1)
                dve.wait_ge(yy["skip_added"], t + 1)
                dve.wait_ge(zz["silu"], HB * (t + 1))
                dve.tensor_tensor(y[:, :, :], y[:, :, :], z_silu[:, :].rearrange("p (h d) -> p h d", d=SSM_P),
                                  ALU.mult).then_inc(yy["gated"], 1)

            def body(b, last):
                for i in range(TPB):
                    t = b * TPB + i
                    if i < TPB - 1 or last:
                        if i:
                            off_scaled(t, i, b)
                        y_gated(t, i, b)
                    else:
                        pair_stats(b + 1, 0)
                        off_scaled(t, i, b)
                        pair_normed(b + 1, 0, 0)
                        pair_normed(b + 1, 0, 1)
                        pair_stats(b + 1, 1)
                    if i < TPB - 1:
                        m_products(t + 1, i + 1)
                        dve.wait_ge(st["ps"], 3 * b + i + 1)
                        src = off_ps[0:SSM_N, :, :].rearrange("p b n -> p (b n)").rearrange("p (h d) -> p h d", d=SSM_P)
                        if i == 0:
                            dve.tensor_copy(state[:, :, :], src).then_inc(st["ready"], 1)
                        else:
                            dve.wait_ge(st["scaled"], 2 * b + i)
                            dve.tensor_tensor(state[:, :, :], state[:, :, :], src, ALU.add).then_inc(st["ready"], 1)
                        for half in range(HB):
                            z_gated(t + 1, half)
                        add_out(t, i, b)
                    elif last:
                        add_out(t, i, b)
                    else:
                        project_batch(b + 1, t)
                        m_products(t + 1, 0)
                        for half in range(HB):
                            z_gated(t + 1, half)

            with dve.Fori(0, BATCHES - 1) as b:
                body(b, False)
            body(BATCHES - 1, True)


def ssm_tables():
    import numpy as np

    i = np.arange(P)
    e = np.arange(EXPERTS)
    f = np.float32
    return {
        "ident": np.eye(P, dtype=f),
        "upto": (i[:, None] <= i[None, :]).astype(f),
        "after": (i[:, None] > i[None, :]).astype(f),
        "ones": np.ones((P, P), f),
        "earlier": (e[None, :] < e[:, None]).astype(f),
    }


def model_kernel(nc, ins, out):
    x_parts = nc.dram_tensor("x_parts", (2, TILES + 2, P, D), F32, kind="Internal").ap()
    after_attention0 = nc.dram_tensor("after_attention0", (TILES, P, D), F32, kind="Internal").ap()
    after_layer0 = nc.dram_tensor("after_layer0", (TILES, P, D), F32, kind="Internal").ap()
    after_attention1 = nc.dram_tensor("after_attention1", (TILES, P, D), F32, kind="Internal").ap()
    expert_weights = nc.dram_tensor("expert_weights", (P, TILES, EXPERTS + SHARED_GROUPS), F32, kind="Internal").ap()

    def named(prefix, labels):
        return {label: ins[f"{prefix}_{label}"] for label in labels.split()}

    linear_attention_phase(nc, ins["x"], named("a0", "qkvo g1 g2 norm_w"),
                           named("t0", "ident cos sin decay decay_q decay_k same_head chunk_decay"),
                           x_parts, after_attention0)
    fp4 = named("f0", "scales shift")
    fp4["resid"] = after_attention0
    swiglu_phase(nc, "f0", x_parts, ins["f0_words"], None, FP4_GROUPS, None, fp4, after_layer0)
    ssm_phase(nc, after_layer0, named("a1", "in_proj small conv_w conv_b dt_bias a_log skip_d norm_w out_proj"),
              named("t1", "ident upto after ones earlier"), x_parts, after_attention1, expert_weights)
    swiglu_phase(nc, "f1", x_parts, ins["f1_up"], ins["f1_down"], EXPERTS + SHARED_GROUPS,
                 (expert_weights, after_attention1), None, out)


def rows_on_partitions(w):
    return w.reshape(-1, P, w.shape[-1]).transpose(1, 0, 2)


def lay_attention0(wq, wk, wv, wo, wg1, wg2, norm_weight):
    import numpy as np

    return {
        "a0_qkvo": np.stack([rows_on_partitions(w).reshape(P, KT * D) for w in (wq, wk, wv, wo)]),
        "a0_g1": rows_on_partitions(wg1),
        "a0_g2": wg2,
        "a0_norm_w": norm_weight.reshape(KT, P).T,
    }


def in_groups(w):
    import numpy as np

    pad = np.zeros((SHARED_GROUPS * GF - w.shape[0],) + w.shape[1:], w.dtype)
    return np.concatenate([w, pad]).reshape((SHARED_GROUPS, GF) + w.shape[1:])


def lay_fp4(up_packed, up_scales, down_packed, down_scales):
    import numpy as np

    inter = up_packed.shape[0] // 2
    gate_up = np.stack([in_groups(w) for w in up_packed.reshape(2, inter, -1)])
    words = gate_up.reshape(2, FP4_GROUPS, JT, P, KT, P // 8).transpose(1, 2, 0, 5, 4, 3)
    words = np.repeat(words, 8, axis=3).reshape(FP4_GROUPS, 2 * JT, P, D)
    down = in_groups(np.repeat(down_packed.T, 8, axis=0)).reshape(FP4_GROUPS, JT, P, D)
    up_by = np.stack([in_groups(w) for w in up_scales.T.reshape(2, inter, KT)])
    up_by = up_by.reshape(2, FP4_GROUPS, JT, P, KT).transpose(1, 2, 0, 4, 3).reshape(FP4_GROUPS, 2 * JT, D)
    down_by = np.concatenate([down_scales, np.zeros((FP4_GROUPS * JT - len(down_scales), D), down_scales.dtype)])
    return {
        "f0_words": np.concatenate([words, down], 1),
        "f0_scales": np.concatenate([up_by, down_by.reshape(FP4_GROUPS, JT, D)], 1),
        "f0_shift": (4 * (np.arange(P, dtype=np.int32) % 8)).reshape(P, 1),
    }


def lay_attention1(in_proj_w, conv_w, conv_b, dt_bias, a_log, skip_d, norm_w, out_proj_w, gate_w, shared_gate_w):
    import numpy as np

    w = in_proj_w.T
    wide = rows_on_partitions(w[:, :2 * E + 2 * SSM_N])
    zero = np.zeros((D, 1), np.float32)

    def by_feature_tile(a):
        pad = np.zeros((1, P - SSM_N, a.shape[1]), np.float32)
        b_c = [np.concatenate([a[None, n:n + SSM_N], pad], 1) for n in (E, E + SSM_N)]
        return np.concatenate([a[:E].reshape(ET, P, -1)] + b_c).transpose(1, 0, 2)

    return {
        "a1_in_proj": wide.reshape(P, KT, -1, P).transpose(2, 0, 1, 3),
        "a1_small": rows_on_partitions(np.concatenate([w[:, 2 * E + 2 * SSM_N:], gate_w.T, shared_gate_w.T, zero], 1)),
        "a1_conv_w": by_feature_tile(conv_w),
        "a1_conv_b": by_feature_tile(conv_b[:, None])[:, :, 0],
        "a1_dt_bias": dt_bias,
        "a1_a_log": a_log,
        "a1_skip_d": skip_d,
        "a1_norm_w": norm_w.reshape(ET, P).T,
        "a1_out_proj": rows_on_partitions(out_proj_w.T),
    }


def lay_experts(fc1, fc2, proj, shared_fc1, shared_fc2, shared_proj):
    import numpy as np

    def filled(w):
        return np.concatenate([w, np.zeros((EXPERTS, GF - w.shape[1], D), np.float32)], 1)

    w1 = np.concatenate([filled(fc1), in_groups(shared_fc1)])
    w2 = np.concatenate([filled(fc2), in_groups(shared_fc2)])
    up = np.stack([w1, w2], 1).reshape(-1, 2, JT, P, KT, P)
    return {
        "f1_up": up.transpose(0, 5, 2, 1, 4, 3).reshape(-1, P, JT * 2 * KT * P),
        "f1_down": np.concatenate([filled(proj.transpose(0, 2, 1)), in_groups(shared_proj.T)]),
    }


def kernel(**inputs):
    import concourse.bacc as bacc
    import numpy as np
    from concourse.bass_utils import run_bass_kernel_spmd

    given = {name: np.asarray(a) for name, a in inputs.items()}

    def take(prefix, labels):
        return [given[f"{prefix}_{label}"] for label in labels.split()]

    x = given["L0_attn_x"]
    arrays = {"x": x.reshape(TILES, P, D)}
    arrays.update(lay_attention0(*take("L0_attn", "Wq Wk Wv Wo Wg1 Wg2 norm_weight")))
    arrays.update(lay_fp4(*take("L0_ffn", "gate_up_packed gate_up_scales down_packed down_scales")))
    arrays.update(lay_attention1(*take("L1_attn", "in_proj_w conv_w conv_b dt_bias A_log D norm_w out_proj_w"),
                                 *take("L1_ffn", "gate_w shared_gate_w")))
    arrays.update(lay_experts(*take("L1_ffn", "expert_fc1 expert_fc2 expert_proj shared_fc1 shared_fc2 shared_proj")))
    arrays.update({f"t0_{label}": table for label, table in attention0_tables().items()})
    arrays.update({f"t1_{label}": table for label, table in ssm_tables().items()})

    nc = bacc.Bacc("TRN2", target_bir_lowering=False, num_devices=1)
    arrays = {name: np.ascontiguousarray(a) for name, a in arrays.items()}
    ins = {name: nc.dram_tensor(f"in_{name}", a.shape, mybir.dt.from_np(a.dtype), kind="ExternalInput").ap()
           for name, a in arrays.items()}
    out = nc.dram_tensor("out", (TILES, P, D), F32, kind="ExternalOutput").ap()
    model_kernel(nc, ins, out)
    result = run_bass_kernel_spmd(nc, [{f"in_{name}": a for name, a in arrays.items()}], core_ids=[0])
    return result.results[0]["out"].reshape(x.shape)
```

```python
from contextlib import ExitStack

import concourse.bass as bass
from concourse import mybir

F32 = mybir.dt.float32
F32R = mybir.dt.float32r
F16 = mybir.dt.float16
BF16 = mybir.dt.bfloat16
I32 = mybir.dt.int32
ALU = mybir.AluOpType
ACT = mybir.ActivationFunctionType
AX_X = mybir.AxisListType.X

P = 128
BANK = 512
BATCHES = 4
BT = 512
TPB = BT // P
TILES = BATCHES * TPB
D = 512
KT = D // P
JT = 3
GF = JT * P
FP4_GROUPS = 4
EXPERTS = 8
EXPERT_FEATURES = 352
SHARED_FEATURES = 1408
REST = EXPERT_FEATURES % P
MIXED_GROUPS = EXPERTS * REST // P // 2
SHARED_GROUPS = (SHARED_FEATURES // P - 3) // 2
MOE_GROUPS = EXPERTS + SHARED_GROUPS + MIXED_GROUPS + 1



def clear_semaphores(nc, semaphores):
    nc.clear_and_free_semaphores(semaphores)
    nc.all_engine_barrier()


HEADS = 16
HD = 32
HPT = P // HD


def linear_attention_phase(nc, x_dram, wts, tables, x_parts, out_dram):
    name = "a0"
    semaphores = []
    with ExitStack() as ctx:
        ctx.callback(clear_semaphores, nc, semaphores)

        def sb(label, shape, dt=F32):
            return ctx.enter_context(nc.sbuf_tensor(f"{name}_{label}", shape, dt))

        def bank(label):
            return ctx.enter_context(nc.psum_tensor(f"{name}_{label}", [P, BANK], F32))

        def sem(label):
            semaphores.append(nc.alloc_semaphore(f"{name}_{label}"))
            return semaphores[-1]

        w_raw = sb("w_raw", [P, 2, KT, D])
        w_hi = sb("w_hi", [P, 4, KT, D], F32R)
        w_lo = sb("w_lo", [P, 4, KT, D], F32R)
        g1_raw = sb("g1_raw", [P, KT, HD])
        g1_hi = sb("g1_hi", [P, KT, HD], F32R)
        g1_lo = sb("g1_lo", [P, KT, HD], F32R)
        g2 = sb("g2", [HD, D])
        norm_w = sb("norm_w", [P, KT])
        ident = sb("ident", [P, P])
        rope_cos = sb("rope_cos", [P, TPB, HD])
        rope_sin = sb("rope_sin", [P, TPB, HD])
        decay = sb("decay", [P, HPT, HPT, P])
        decay_q = sb("decay_q", [P, HEADS])
        decay_k = sb("decay_k", [P, HEADS])
        same_head = sb("same_head", [P, P])
        chunk_decay = sb("chunk_decay", [P, KT, P])
        power = sb("power", [P, HEADS])

        x = sb("x", [P, TPB, D])
        stats = sb("stats", [P, 6])
        mean_var = sb("mean_var", [P, 2, 2])
        ln_tmp = sb("ln_tmp", [P, 1])
        stats_copy = sb("stats_copy", [P, 1])
        eps_ln = sb("eps_ln", [P, 1])
        eps_head = sb("eps_head", [P, HEADS])
        ln_rs = sb("ln_rs", [P, 2])
        xn = sb("xn", [P, 2, D])
        xt_hi = [sb(f"xt_hi{n}", [P, KT, P], F32R) for n in range(2)]
        xt_lo = [sb(f"xt_lo{n}", [P, KT, P], F32R) for n in range(2)]
        qk = sb("qk", [P, 2 * HEADS, HD])
        qk_cos = sb("qk_cos", [P, 2 * HEADS, HD])
        qk_sin = sb("qk_sin", [P, 2 * HEADS, HD])
        qk_rot = [sb(f"qk_rot{n}", [P, 2 * HEADS, HD]) for n in range(2)]
        k_dec = [sb(f"k_dec{n}", [P, HEADS, HD]) for n in range(2)]
        v = [sb(f"v{n}", [P, D]) for n in range(2)]
        gate_low = sb("gate_low", [HD, P])
        gate = sb("gate", [P, 2, D])
        qt = sb("qt", [P, KT, P])
        kt_ = sb("kt", [P, KT, P])
        scores = sb("scores", [P, HPT, HPT, P])
        inter = sb("inter", [P, D])
        o_sum = sb("o_sum", [P, D])
        x2 = sb("x2", [P, D])
        sq = sb("sq", [P, D])
        ss = sb("ss", [P, HEADS])
        ms = sb("ms", [P, HEADS])
        rs = sb("rs", [P, HEADS])
        o_norm = sb("o_norm", [P, D])
        ot_hi = sb("ot_hi", [P, KT, P], F32R)
        ot_lo = sb("ot_lo", [P, KT, P], F32R)
        state = sb("state", [P, KT, P])
        state_new = sb("state_new", [P, KT, P])
        state_old = sb("state_old", [P, KT, P])

        proj_ps = [bank(f"proj{n}") for n in range(2)]
        score_ps = [bank(f"score{n}") for n in range(HPT)]
        misc_ps = [bank(f"misc{n}") for n in range(2)]
        o_ps, y_ps = score_ps[0], score_ps[1]

        def sems(group, labels):
            return {label: sem(f"{group}_{label}") for label in labels.split()}

        loaded = sems("loaded", "ident const")
        w = sems("w", "hi split normed")
        ln = sems("ln", "stats_step stats rstd normed")
        xt = sems("xt", "ps hi lo")
        ps = sems("ps", "q k v low gate qt kt scores inter state o ot y")
        act_out = sems("act_out", "q k v low gate qt kt sq ot_hi")
        rot = sems("rot", "cos sin done k_decayed")
        st = sems("st", "masked old ready")
        masked = sem("masked")
        out = sems("out", "inter_scaled summed gated squares rstd normed ot_lo y_added")
        power_set = sem("power_set")
        x_in = [sem(f"x_in{n}") for n in range(TPB)]
        y_stored = [sem(f"y_stored{n}") for n in range(TPB)]
        xt_stored = [sem(f"xt_stored{n}") for n in range(2)]
        w_loaded = [sem(f"w_loaded{n}") for n in range(2)]

        block = ctx.enter_context(nc.Block())

        @block.sync
        def _(sp):
            def load_w(n):
                sp.dma_start(w_raw[:, n % 2, :, :].rearrange("p k n -> p (k n)"), wts["qkvo"][n]
                             ).then_inc(w_loaded[n % 2], 16)

            def load_x(batch, i):
                sp.dma_start(x[:, i, :], x_dram[bass.ds(batch * TPB + i, 1)].rearrange("o p n -> (o p) n")
                             ).then_inc(x_in[i], 16)

            def store_xt(t, odd):
                sp.wait_ge(xt["hi"], t + 1)
                sp.wait_ge(xt["lo"], t + 1)
                for part, buf in ((0, xt_hi[odd]), (1, xt_lo[odd])):
                    sp.dma_start(x_parts[part, bass.ds(t, 1)].rearrange("o p n -> (o p) n"),
                                 buf[:, :, :].bitcast(F32).rearrange("p k n -> p (k n)")).then_inc(xt_stored[odd], 16)

            load_x(0, 0)
            sp.dma_start(ident[:, :], tables["ident"]).then_inc(loaded["ident"], 16)
            load_w(0)
            load_x(0, 1)
            load_w(1)
            small = ((g1_raw, wts["g1"]), (g2, wts["g2"]), (norm_w, wts["norm_w"]), (rope_cos, tables["cos"]),
                     (rope_sin, tables["sin"]), (decay_q, tables["decay_q"]), (decay_k, tables["decay_k"]),
                     (same_head, tables["same_head"]), (chunk_decay, tables["chunk_decay"]), (decay, tables["decay"]))
            for dst, src in small:
                sp.dma_start(dst[:], src).then_inc(loaded["const"], 16)
            load_x(0, 2)
            load_x(0, 3)
            for n in (2, 3):
                sp.wait_ge(w["split"], n - 1)
                load_w(n)
            store_xt(0, 0)
            store_xt(1, 1)
            def body(b, first, last):
                for i in range(TPB):
                    t = b * TPB + i
                    if not (first and i == 0):
                        store_y(t - 1, (i - 1) % TPB)
                        if i == 0:
                            sp.wait_ge(y_stored[TPB - 1], 16 * b)
                            load_x(b, TPB - 1)
                        elif not last:
                            sp.wait_ge(y_stored[i - 1], 16 * b + 16)
                            load_x(b + 1, i - 1)
                    if not (last and i >= TPB - 2):
                        store_xt(t + 2, i % 2)

            def store_y(t, slot):
                sp.wait_ge(out["y_added"], t + 2)
                sp.dma_start(out_dram[bass.ds(t, 1)].rearrange("o p n -> (o p) n"), x[:, slot, :]).then_inc(y_stored[slot], 16)

            body(0, True, False)
            with sp.Fori(1, BATCHES - 1) as b:
                body(b, False, False)
            body(BATCHES - 1, False, True)
            store_y(TILES - 1, TPB - 1)
            for n in range(TPB):
                sp.wait_ge(y_stored[n], 16 * BATCHES)
            for n in range(2):
                sp.wait_ge(xt_stored[n], 16 * TILES)

        @block.tensor
        def _(pe):
            def turn(to, src, ready):
                for k in range(KT):
                    last = pe.transpose(to[:, k * P:(k + 1) * P], src[:, k * P:(k + 1) * P], ident[:, :])
                last.then_inc(ready, 1)

            def sums(to, l_hi, l_lo, r_hi, r_lo, k):
                pe.matmul(to, l_hi, r_hi, start=k == 0, stop=False)
                pe.matmul(to, l_hi, r_lo, start=False, stop=False)
                return pe.matmul(to, l_lo, r_hi, start=False, stop=k == KT - 1)

            def project(bank_, n, odd, ready):
                for k in range(KT):
                    last = sums(bank_[:, :], xt_hi[odd][:, k, :], xt_lo[odd][:, k, :], w_hi[:, n, k, :], w_lo[:, n, k, :], k)
                last.then_inc(ready, 1)

            def x_turned(t, odd):
                pe.wait_ge(ln["normed"], t + 1)
                turn(misc_ps[1], xn[:, odd, :], xt["ps"])

            def q_proj(t, odd, first=False):
                pe.wait_ge(xt["hi"], t + 1)
                pe.wait_ge(xt["lo"], t + 1)
                if not first:
                    pe.wait_ge(act_out["v"], t)
                project(proj_ps[0], 0, odd, ps["q"])

            def k_proj(t, odd, first=False):
                if not first:
                    pe.wait_ge(act_out["gate"], t)
                project(proj_ps[1], 1, odd, ps["k"])

            def v_proj(t, odd):
                pe.wait_ge(act_out["q"], t + 1)
                project(proj_ps[0], 2, odd, ps["v"])
                pe.wait_ge(act_out["k"], t + 1)
                for k in range(KT):
                    last = sums(proj_ps[1][0:HD, 0:P], g1_hi[:, k, :], g1_lo[:, k, :],
                                xt_hi[odd][:, k, :], xt_lo[odd][:, k, :], k)
                last.then_inc(ps["low"], 1)

            def gate_proj(t):
                pe.wait_ge(act_out["low"], t + 1)
                pe.matmul(proj_ps[1][:, :], gate_low[:, :], g2[:, :], start=True, stop=True).then_inc(ps["gate"], 1)

            def o_turned(t):
                pe.wait_ge(out["normed"], t + 1)
                turn(misc_ps[0], o_norm[:, :], ps["ot"])

            def y_proj(t):
                pe.wait_ge(act_out["ot_hi"], t + 1)
                pe.wait_ge(out["ot_lo"], t + 1)
                for k in range(KT):
                    last = sums(y_ps[:, :], ot_hi[:, k, :], ot_lo[:, k, :], w_hi[:, 3, k, :], w_lo[:, 3, k, :], k)
                last.then_inc(ps["y"], 1)

            def score(t, i):
                pe.wait_ge(act_out["qt"], t + 1)
                pe.wait_ge(act_out["kt"], t + 1)
                pe.wait_ge(out["gated"], t + 1)
                if not (isinstance(t, int) and t == 0):
                    pe.wait_ge(out["y_added"], t)
                for g in range(KT):
                    for r in range(HPT):
                        rows = slice(r * HD, (r + 1) * HD)
                        last = pe.matmul(score_ps[r][:, g * P:(g + 1) * P], kt_[rows, g, :], qt[rows, g, :],
                                         start=True, stop=True)
                        if g == KT - 1:
                            last.then_inc(ps["scores"], 1)

            def attend(t, odd):
                pe.wait_ge(masked, HPT * (t + 1))
                for h in range(HEADS):
                    last = pe.matmul(o_ps[:, h * HD:(h + 1) * HD], scores[:, h % HPT, h // HPT, :],
                                     v[odd][:, h * HD:(h + 1) * HD], start=True, stop=True)
                last.then_inc(ps["o"], 1)

            pe.wait_ge(loaded["ident"], 16)
            x_turned(0, 0)
            pe.wait_ge(xt["hi"], 1)
            pe.wait_ge(xt["lo"], 1)
            x_turned(1, 1)
            pe.wait_ge(w["split"], 1)
            q_proj(0, 0, first=True)
            pe.wait_ge(w["split"], 2)
            k_proj(0, 0, first=True)
            pe.wait_ge(w["split"], 4)
            v_proj(0, 0)
            pe.wait_ge(loaded["const"], 16 * 10)
            gate_proj(0)
            def body(b, first, last):
                for i in range(TPB):
                    t = b * TPB + i
                    odd, other = i % 2, (i + 1) % 2
                    some_before = not (first and i == 0)
                    some_next = not (last and i == TPB - 1)
                    pe.wait_ge(rot["done"], t + 1)
                    if i == 1:
                        pe.wait_ge(st["ready"], 3 * b + 1)
                    elif i > 1:
                        pe.wait_ge(st["masked"], 2 * b + i - 1)
                    elif some_before:
                        pe.wait_ge(act_out["ot_hi"], t - 1)
                        pe.wait_ge(out["ot_lo"], t - 1)
                    turn(misc_ps[0], qk_rot[odd][:, 0:HEADS, :].rearrange("p h d -> p (h d)"), ps["qt"])
                    if some_next:
                        pe.wait_ge(xt["hi"], t + 2)
                        pe.wait_ge(xt["lo"], t + 2)
                    else:
                        pe.wait_ge(out["inter_scaled"], 3 * b + i - 1)
                    turn(misc_ps[1], qk_rot[odd][:, HEADS:2 * HEADS, :].rearrange("p h d -> p (h d)"), ps["kt"])
                    if some_next:
                        q_proj(t + 1, other)
                    score(t, i)
                    if some_before:
                        o_turned(t - 1)
                    if i:
                        pe.wait_ge(st["ready"], 3 * b + i)
                        for g in range(KT):
                            last_mm = pe.matmul(misc_ps[1][:, g * P:(g + 1) * P], qt[:, g, :], state[:, g, :],
                                                start=True, stop=True)
                        last_mm.then_inc(ps["inter"], 1)
                    if some_next:
                        k_proj(t + 1, other)
                    if i < TPB - 1:
                        pe.wait_ge(rot["k_decayed"], t + 1)
                        if some_before:
                            pe.wait_ge(act_out["ot_hi"], t)
                            pe.wait_ge(out["ot_lo"], t)
                        for g in range(KT):
                            cols = slice(g * P, (g + 1) * P)
                            last_mm = pe.matmul(misc_ps[0][:, cols],
                                                k_dec[odd][:, :, :].rearrange("p h d -> p (h d)")[:, cols],
                                                v[odd][:, cols], start=True, stop=True)
                        last_mm.then_inc(ps["state"], 1)
                    if not (last and i >= TPB - 2):
                        if i:
                            pe.wait_ge(out["inter_scaled"], 3 * b + i)
                        x_turned(t + 2, odd)
                    if some_next:
                        v_proj(t + 1, other)
                    attend(t, odd)
                    if first and i == 1:
                        pe.wait_ge(w["split"], 5)
                    if some_before:
                        y_proj(t - 1)
                    if some_next:
                        gate_proj(t + 1)

            body(0, True, False)
            with pe.Fori(1, BATCHES - 1) as b:
                body(b, False, False)
            body(BATCHES - 1, False, True)
            o_turned(TILES - 1)
            pe.wait_ge(out["y_added"], TILES)
            y_proj(TILES - 1)

        @block.scalar
        def _(act):
            qk_flat = qk[:, :, :].rearrange("p h d -> p (h d)")

            def x_high(t, odd, stored=None):
                act.wait_ge(xt["ps"], t + 1)
                if stored is not None:
                    act.wait_ge(ps["low"], t - 1)
                    act.wait_ge(xt_stored[odd], stored)
                act.copy(xt_hi[odd][:, :, :], misc_ps[1][:, :].rearrange("p (k n) -> p k n", k=KT)).then_inc(xt["hi"], 1)

            def projected(t, odd, first=False, turned_next=False):
                act.wait_ge(ps["q"], t + 1)
                if not first:
                    act.wait_ge(rot["cos"], t)
                    act.wait_ge(rot["sin"], t)
                act.activation(qk_flat[:, 0:D], proj_ps[0][:, :], ACT.Silu).then_inc(act_out["q"], 1)
                act.wait_ge(ps["k"], t + 1)
                act.activation(qk_flat[:, D:2 * D], proj_ps[1][:, :], ACT.Silu).then_inc(act_out["k"], 1)
                if turned_next:
                    x_high(t + 1, 1 - odd, stored=16 * (t + 1 - (1 - odd)))
                act.wait_ge(ps["v"], t + 1)
                act.copy(v[odd][:, :], proj_ps[0][:, :]).then_inc(act_out["v"], 1)
                act.wait_ge(ps["low"], t + 1)
                act.copy(gate_low[:, :], proj_ps[1][0:HD, 0:P]).then_inc(act_out["low"], 1)

            def gated(t, odd):
                act.wait_ge(ps["gate"], t + 1)
                act.activation(gate[:, odd, :], proj_ps[1][:, :], ACT.Tanh, scale=0.5).then_inc(act_out["gate"], 1)

            def o_high(t):
                act.wait_ge(ps["ot"], t + 1)
                act.copy(ot_hi[:, :, :], misc_ps[0][:, :].rearrange("p (k n) -> p k n", k=KT)).then_inc(act_out["ot_hi"], 1)

            def w_high(n):
                act.wait_ge(w_loaded[n % 2], 16 * (n // 2 + 1))
                act.copy(w_hi[:, n, :, :], w_raw[:, n % 2, :, :]).then_inc(w["hi"], 1)

            x_high(0, 0)
            w_high(0)
            x_high(1, 1)
            w_high(1)
            w_high(2)
            act.wait_ge(loaded["const"], 16 * 10)
            act.copy(g1_hi[:, :, :], g1_raw[:, :, :]).then_inc(w["hi"], 1)
            projected(0, 0, first=True)
            gated(0, 0)
            act.wait_ge(w["normed"], KT)
            w_high(3)
            def body(b, first, last):
                for i in range(TPB):
                    t = b * TPB + i
                    odd, other = i % 2, (i + 1) % 2
                    act.wait_ge(ps["qt"], t + 1)
                    act.copy(qt[:, :, :], misc_ps[0][:, :].rearrange("p (k n) -> p k n", k=KT)).then_inc(act_out["qt"], 1)
                    act.wait_ge(ps["kt"], t + 1)
                    act.copy(kt_[:, :, :], misc_ps[1][:, :].rearrange("p (k n) -> p k n", k=KT)).then_inc(act_out["kt"], 1)
                    if not (first and i == 0):
                        o_high(t - 1)
                    if not (last and i == TPB - 1):
                        projected(t + 1, other, turned_next=not (last and i == TPB - 2))
                    act.wait_ge(out["gated"], t + 2)
                    act.activation(sq[:, :], x2[:, :], ACT.Square).then_inc(act_out["sq"], 1)
                    if not (last and i == TPB - 1):
                        gated(t + 1, other)

            body(0, True, False)
            with act.Fori(1, BATCHES - 1) as b:
                body(b, False, False)
            body(BATCHES - 1, False, True)
            o_high(TILES - 1)

        @block.gpsimd
        def _(pool):
            def ln_rstd(t, odd):
                pool.wait_ge(ln["stats"], t + 1)
                pool.tensor_tensor(ln_tmp[:, :], mean_var[:, odd, 1:2], eps_ln[:, :], ALU.add).then_inc(ln["rstd"], 1)
                pool.wait_ge(ln["rstd"], 2 * t + 1)
                pool.tensor_tensor(ln_rs[:, odd:odd + 1], ln_tmp[:, :], power[:, 0:1], ALU.pow).then_inc(ln["rstd"], 1)

            def swap(t, i, first=False):
                half = HD // 2
                pool.wait_ge(act_out["q"], t + 1)
                pool.wait_ge(act_out["k"], t + 1)
                if not first:
                    pool.wait_ge(rot["done"], t)
                for to, of in ((0, half), (half, 0)):
                    last = pool.tensor_tensor(qk_sin[:, :, to:to + half], qk[:, :, of:of + half],
                                              rope_sin[:, i:i + 1, to:to + half].to_broadcast([P, 2 * HEADS, half]), ALU.mult)
                last.then_inc(rot["sin"], 1)

            pool.memset(power[:, :], -0.5).then_inc(power_set, 1)
            pool.memset(eps_ln[:, :], 1e-5).then_inc(power_set, 1)
            pool.memset(eps_head[:, :], 4 * HD * 1e-6).then_inc(power_set, 1)
            pool.wait_ge(power_set, 3)
            ln_rstd(0, 0)
            ln_rstd(1, 1)
            pool.wait_ge(loaded["const"], 16 * 10)
            swap(0, 0, first=True)

            def body(b, first, last):
                for i in range(TPB):
                    t = b * TPB + i
                    if i in (1, 2):
                        pool.wait_ge(st["ready"], 3 * b + i)
                        pool.tensor_tensor(state_old[:, :, :], state[:, :, :], chunk_decay[:, :, :], ALU.mult).then_inc(st["old"], 1)
                    if not (last and i >= TPB - 2):
                        ln_rstd(t + 2, i % 2)
                    if not (last and i == TPB - 1):
                        swap(t + 1, (i + 1) % TPB)
                    pool.wait_ge(out["squares"], t + 1)
                    pool.tensor_tensor(ms[:, :], ss[:, :], eps_head[:, :], ALU.add).then_inc(out["rstd"], 1)
                    pool.wait_ge(out["rstd"], 2 * t + 1)
                    pool.tensor_tensor(rs[:, :], ms[:, :], power[:, :], ALU.pow).then_inc(out["rstd"], 1)

            body(0, True, False)
            with pool.Fori(1, BATCHES - 1) as b:
                body(b, False, False)
            body(BATCHES - 1, False, True)

        @block.vector
        def _(dve):
            def x_stats(t, odd, slot, count):
                dve.wait_ge(x_in[slot], 16 * count)
                dve.bn_stats(stats[:, :], x[:, slot, :]).then_inc(ln["stats_step"], 1)
                dve.wait_ge(ln["stats_step"], t + 1)
                dve.tensor_copy(stats_copy[:, :], stats[:, 0:1])
                dve.bn_aggr(mean_var[:, odd, :], stats[:, :]).then_inc(ln["stats"], 1)

            def x_normed(t, odd, slot, first=False):
                dve.wait_ge(ln["rstd"], 2 * t + 2)
                if not first:
                    dve.wait_ge(xt["ps"], t - 1)
                dve.tensor_scalar(xn[:, odd, :], x[:, slot, :], mean_var[:, odd, 0:1], ln_rs[:, odd:odd + 1],
                                  ALU.subtract, ALU.mult).then_inc(ln["normed"], 1)

            def x_low(t, odd):
                dve.wait_ge(xt["hi"], t + 1)
                dve.tensor_tensor(xt_lo[odd][:, :, :], misc_ps[1][:, :].rearrange("p (k n) -> p k n", k=KT),
                                  xt_hi[odd][:, :, :].bitcast(F32), ALU.subtract).then_inc(xt["lo"], 1)

            def rotate(t, i, odd):
                dve.wait_ge(act_out["q"], t + 1)
                dve.wait_ge(act_out["k"], t + 1)
                dve.tensor_tensor(qk_cos[:, :, :], qk[:, :, :], rope_cos[:, i:i + 1, :].to_broadcast([P, 2 * HEADS, HD]),
                                  ALU.mult).then_inc(rot["cos"], 1)
                dve.wait_ge(rot["cos"], t + 1)
                dve.wait_ge(rot["sin"], t + 1)
                dve.tensor_tensor(qk_rot[odd][:, :, :], qk_cos[:, :, :], qk_sin[:, :, :], ALU.add).then_inc(rot["done"], 1)
                dve.wait_ge(rot["done"], t + 1)
                dve.tensor_tensor(k_dec[odd][:, :, :], qk_rot[odd][:, HEADS:2 * HEADS, :],
                                  decay_k[:, :].unsqueeze(2).to_broadcast([P, HEADS, HD]), ALU.mult).then_inc(rot["k_decayed"], 1)

            def o_low(t):
                dve.wait_ge(act_out["ot_hi"], t + 1)
                dve.tensor_tensor(ot_lo[:, :, :], misc_ps[0][:, :].rearrange("p (k n) -> p k n", k=KT),
                                  ot_hi[:, :, :].bitcast(F32), ALU.subtract).then_inc(out["ot_lo"], 1)

            def add_y(t, slot):
                dve.wait_ge(ps["y"], t + 1)
                dve.tensor_tensor(x[:, slot, :], x[:, slot, :], y_ps[:, :], ALU.add).then_inc(out["y_added"], 1)

            def w_low(n, slot, count):
                dve.wait_ge(w["hi"], count)
                dve.tensor_tensor(w_lo[:, n, :, :], w_raw[:, slot, :, :], w_hi[:, n, :, :].bitcast(F32),
                                  ALU.subtract).then_inc(w["split"], 1)

            dve.sem_inc(out["gated"], 1)
            dve.sem_inc(out["y_added"], 1)
            x_stats(0, 0, 0, 1)
            x_normed(0, 0, 0, first=True)
            x_stats(1, 1, 1, 1)
            x_normed(1, 1, 1, first=True)
            x_low(0, 0)
            w_low(0, 0, 1)
            x_low(1, 1)
            w_low(1, 1, 2)
            w_low(2, 0, 3)
            dve.wait_ge(w["hi"], 4)
            dve.wait_ge(loaded["const"], 16 * 10)
            dve.tensor_tensor(g1_lo[:, :, :], g1_raw[:, :, :], g1_hi[:, :, :].bitcast(F32), ALU.subtract).then_inc(w["split"], 1)
            rotate(0, 0, 0)
            dve.wait_ge(w_loaded[1], 32)
            for k in range(KT):
                dve.tensor_scalar(w_raw[:, 1, k, :], w_raw[:, 1, k, :], norm_w[:, k:k + 1], 0.5 * (4 * HD) ** 0.5, ALU.mult, ALU.mult
                                  ).then_inc(w["normed"], 1)
            w_low(3, 1, 5)

            def body(b, first, last):
                for i in range(TPB):
                    t = b * TPB + i
                    odd, other = i % 2, (i + 1) % 2
                    ahead = (i + 2) % TPB
                    some_before = not (first and i == 0)
                    two_ahead = not (last and i >= TPB - 2)
                    if two_ahead:
                        x_stats(t + 2, odd, ahead, b + (i + 2) // TPB + 1)
                    for r in range(HPT):
                        dve.wait_ge(ps["scores"], HPT * t + r + 1)
                        dve.tensor_tensor(scores[:, r, :, :], score_ps[r][:, :].rearrange("p (g n) -> p g n", g=HPT),
                                          decay[:, r, :, :], ALU.mult).then_inc(masked, 1)
                    if some_before:
                        o_low(t - 1)
                    if i:
                        dve.wait_ge(ps["inter"], 3 * b + i)
                        dve.tensor_tensor(inter[:, :].rearrange("p (h d) -> p h d", h=HEADS),
                                          misc_ps[1][:, :].rearrange("p (h d) -> p h d", h=HEADS),
                                          decay_q[:, :].unsqueeze(2).to_broadcast([P, HEADS, HD]),
                                          ALU.mult).then_inc(out["inter_scaled"], 1)
                    if two_ahead:
                        x_normed(t + 2, odd, ahead)
                    if i < TPB - 1:
                        to, ready = (state, st["ready"]) if i == 0 else (state_new, st["masked"])
                        dve.wait_ge(ps["state"], 3 * b + i + 1)
                        dve.tensor_tensor(to[:, :, :], misc_ps[0][:, :].rearrange("p (k n) -> p k n", k=KT),
                                          same_head[:, :].unsqueeze(1).to_broadcast([P, KT, P]), ALU.mult).then_inc(ready, 1)
                        if i:
                            dve.wait_ge(st["masked"], 2 * b + i)
                            dve.wait_ge(st["old"], 2 * b + i)
                            dve.tensor_tensor(state[:, :, :], state_old[:, :, :], state_new[:, :, :],
                                              ALU.add).then_inc(st["ready"], 1)
                    if two_ahead:
                        x_low(t + 2, odd)
                    if not (last and i == TPB - 1):
                        rotate(t + 1, (i + 1) % TPB, other)
                    dve.wait_ge(ps["o"], t + 1)
                    dve.wait_ge(act_out["gate"], t + 1)
                    src = o_ps
                    if i:
                        dve.wait_ge(out["inter_scaled"], 3 * b + i)
                        dve.tensor_tensor(o_sum[:, :], o_ps[:, :], inter[:, :], ALU.add).then_inc(out["summed"], 1)
                        dve.wait_ge(out["summed"], 3 * b + i)
                        src = o_sum
                    dve.scalar_tensor_tensor(x2[:, :], gate[:, odd, :], 1.0, src[:, :], ALU.add, ALU.mult).then_inc(out["gated"], 1)
                    if some_before:
                        add_y(t - 1, (i - 1) % TPB)
                    dve.wait_ge(act_out["sq"], t + 1)
                    dve.tensor_reduce(ss[:, :], sq[:, :].rearrange("p (h d) -> p h d", h=HEADS), AX_X, ALU.add
                                      ).then_inc(out["squares"], 1)
                    dve.wait_ge(out["gated"], t + 2)
                    dve.wait_ge(out["rstd"], 2 * t + 2)
                    dve.tensor_tensor(o_norm[:, :].rearrange("p (h d) -> p h d", h=HEADS),
                                      x2[:, :].rearrange("p (h d) -> p h d", h=HEADS),
                                      rs[:, :].unsqueeze(2).to_broadcast([P, HEADS, HD]), ALU.mult).then_inc(out["normed"], 1)

            body(0, True, False)
            with dve.Fori(1, BATCHES - 1) as b:
                body(b, False, False)
            body(BATCHES - 1, False, True)
            o_low(TILES - 1)
            add_y(TILES - 1, TPB - 1)


def attention0_tables():
    import numpy as np

    f = np.float32
    half = HD // 2
    theta = f(10000.0) ** (f(-2.0) * np.arange(half, dtype=f) / f(HD))
    ang = np.arange(BT, dtype=f)[:, None] * theta[None, :].astype(f)
    cos, sin = np.cos(ang.astype(f)), np.sin(ang.astype(f))

    def tiled(a):
        return np.ascontiguousarray(a.reshape(TPB, P, HD).transpose(1, 0, 2).astype(f))

    log_lam = -(f(2.0) ** (f(-8.0) * (np.arange(HEADS, dtype=f) + f(1.0)) / f(HEADS))).astype(f)
    i = np.arange(P, dtype=f)
    diff = i[None, :] - i[:, None]
    d = np.exp(log_lam[:, None, None] * np.maximum(diff, 0)[None]) * (diff >= 0)[None]
    block = np.kron(np.eye(HPT), np.ones((HD, HD)))
    lam = np.exp(log_lam * f(P)).reshape(KT, HPT)
    chunk = np.stack([block * np.repeat(lam[g], HD)[:, None] for g in range(KT)], axis=1)
    return {
        "ident": np.eye(P, dtype=f),
        "cos": tiled(np.concatenate([cos, cos], axis=1)),
        "sin": tiled(np.concatenate([-sin, sin], axis=1)),
        "decay": np.ascontiguousarray(d.reshape(KT, HPT, P, P).transpose(2, 1, 0, 3).astype(f)),
        "decay_q": np.exp(log_lam[None, :] * (i[:, None] + f(1.0))).astype(f),
        "decay_k": np.exp(log_lam[None, :] * (f(P) - f(1.0) - i[:, None])).astype(f),
        "same_head": block.astype(f),
        "chunk_decay": np.ascontiguousarray(chunk.astype(f)),
    }


def swiglu_phase(nc, name, x_parts, up_src, down_src, groups, tiles_of_groups, routed, fp4, out_dram):
    chunks = 3 * JT
    SLOTS = 3
    T, L = tiles_of_groups
    assert max(T, L) == JT
    last_g = groups - 1
    mixed_g = last_g - MIXED_GROUPS
    steps_before_last = last_g * BATCHES

    semaphores = []
    with ExitStack() as ctx:
        ctx.callback(clear_semaphores, nc, semaphores)

        def sb(label, shape, dt=F32):
            return ctx.enter_context(nc.sbuf_tensor(f"{name}_{label}", shape, dt))

        def bank(label):
            return ctx.enter_context(nc.psum_tensor(f"{name}_{label}", [P, BANK], F32))

        def sem(label):
            semaphores.append(nc.alloc_semaphore(f"{name}_{label}"))
            return semaphores[-1]

        x_hi = sb("x_hi", [P, TILES, KT, P], F32R)
        x_lo = sb("x_lo", [P, TILES, KT, P], F32R)
        acc = sb("acc", [P, TILES, D])
        up_f32 = sb("up_f32", [P, JT, 2, KT, P])
        up_hi = sb("up_hi", [P, JT, 2, KT, P], F32R)
        up_lo = sb("up_lo", [P, JT, 2, KT, P], F32R)
        down_f32 = sb("down_f32", [P, JT, D])
        down_hi = sb("down_hi", [P, JT, D], F32R)
        down_lo = sb("down_lo", [P, JT, D], F32R)
        silu_g = sb("silu_g", [P, 2, BT])
        h_f32 = sb("h_f32", [P, 2, BT])
        h_hi = sb("h_hi", [P, JT, BT], F32R)
        h_lo = sb("h_lo", [P, JT, BT], F32R)
        gate_ps = [bank(f"gate{n}") for n in range(2)]
        up_ps = [bank(f"up{n}") for n in range(2)]
        y_ps = [bank(f"y{n}") for n in range(TPB)]

        x_loaded = [sem(f"x_loaded{b}") for b in range(BATCHES)]
        aux_loaded = sem("aux_loaded")
        weights_loaded = sem("weights_loaded")
        weights_hi = sem("weights_hi")
        weights_lo = sem("weights_lo")
        gu_ready = sem("gu_ready")
        silu_ready = sem("silu_ready")
        gu_free = sem("gu_free")
        hhi_ready = sem("hhi_ready")
        h_ready = sem("h_ready")
        y_ready = sem("y_ready")
        y_free = sem("y_free")
        stored = sem("stored")
        if fp4:
            words = sb("words", [P, SLOTS, D], I32)
            scales = sb("scales", [P, SLOTS, D], F16)
            magnitude = sb("magnitude", [P, 2, D], I32)
            sign_bit = sb("sign_bit", [P, 2, D], I32)
            above4 = sb("above4", [P, 2, D], BF16)
            above6 = sb("above6", [P, 2, D], BF16)
            half_sign = sb("half_sign", [P, 2, D], BF16)
            twice = sb("twice", [P, 2, D], BF16)
            value = sb("value", [P, 2, D], BF16)
            shift = sb("shift", [P, 1], I32)
            meansq = sb("meansq", [P, TILES])
            rstd = sb("rstd", [P, TILES])
            power = sb("power", [P, TILES])
            first_words = acc[:, 0:chunks, :].bitcast(I32)
            first_scales = acc[:, chunks:chunks + (chunks + 1) // 2, :].bitcast(F16)
            first_chunk = [sem(f"first_chunk{c}") for c in range(chunks)]
            chunk_loaded = [sem(f"chunk_loaded{n}") for n in range(SLOTS)]
            bits_ready = sem("bits_ready")
            lines_ready = sem("lines_ready")
            dq_step = sem("dq_step")
            value_ready = sem("value_ready")
            decoded = sem("decoded")
            power_set = sem("power_set")
            meansq_ready = sem("meansq_ready")
            rstd_step = sem("rstd_step")
            resid_loaded = [sem(f"resid_loaded{b}") for b in range(BATCHES)]
            final = sem("final")
            bias_m4 = sb("bias_m4", [P, 1])
            bias_m12 = sb("bias_m12", [P, 1])
            bias_half = sb("bias_half", [P, 1])
            bias_set = sem("bias_set")
        else:
            weight, start, weight_t = routed["weights"], routed["start"], routed["weights_turned"]
            ident = sb("ident", [P, P])
            comb_t = sb("comb_t", [routed["columns"], BATCHES, BT])
            row_weight = sb("row_weight", [P, 2, T, BT])
            ident_loaded = sem("ident_loaded")
            turned = sem("turned")
            turned_sb = sem("turned_sb")
            turned_stored = sem("turned_stored")
            row_weight_in = [sem(f"row_weight_in{n}") for n in range(2)]
            weighted = sem("weighted")
            first_loaded = [sem(f"first_loaded{n}") for n in range(JT + 1)]
            start_loaded = [sem(f"start_loaded{b}") for b in range(BATCHES)]
            comb = sb("comb", [P, TILES, routed["columns"]])

        def sums(pe, out, w_hi, w_lo, v_hi, v_lo, start, stop):
            pe.matmul(out, w_hi, v_hi, start=start, stop=False)
            pe.matmul(out, w_hi, v_lo, start=False, stop=False)
            return pe.matmul(out, w_lo, v_hi, start=False, stop=stop)

        def tiles_before(g, b):
            if isinstance(g, int) and g == last_g:
                return steps_before_last * T + b * L
            return (g * BATCHES + b) * T

        def pieces(g):
            return JT if fp4 or (isinstance(g, int) and g == last_g) else T

        def load_x(queue, b):
            for part, dst in ((0, x_hi), (1, x_lo)):
                queue.dma_start(dst[:, b * TPB:(b + 1) * TPB].bitcast(F32).rearrange("p t k n -> p t (k n)"),
                             x_parts[part, b * TPB:(b + 1) * TPB].rearrange("t p n -> p t n"),
                             ).then_inc(x_loaded[b], 16)

        def first_scales_at(c):
            return first_scales[:, c // 2, c % 2 * D:(c % 2 + 1) * D]

        block = ctx.enter_context(nc.Block())

        @block.sync
        def _(sp):
            def load_weights(g):
                n = pieces(g)
                sp.dma_start(up_f32[:, 0:n, :, :, :].rearrange("p j m k f -> p (j m k f)"),
                             up_src[bass.ds(g, 1), :, 0:n * 2 * D].rearrange("o p n -> (o p) n")).then_inc(weights_loaded, 16)
                sp.dma_start(down_f32[:, 0:n, :],
                             down_src[bass.ds(g, 1), 0:n * P].rearrange("o (j p) n -> p (o j) n", p=P)).then_inc(weights_loaded, 16)

            def load_chunk(g, c):
                sp.dma_start(words[:, c % SLOTS, :], up_src[bass.ds(g, 1), c].rearrange("o p n -> (o p) n")
                             ).then_inc(chunk_loaded[c % SLOTS], 16)
                sp.dma_start(scales[:, c % SLOTS, :], fp4["scales"][bass.ds(g, 1), c].rearrange("o n -> (o n)").partition_broadcast(P)
                             ).then_inc(chunk_loaded[c % SLOTS], 16)

            def store(b):
                sp.dma_start(out_dram[bass.ds(b * TPB, TPB)].rearrange("t p n -> p t n"),
                             acc[:, bass.ds(b * TPB, TPB), :]).then_inc(stored, 16)

            def load_row_weights(m, b):
                if BATCHES * m + b >= 2:
                    sp.wait_ge(weighted, T * (BATCHES * m + b - 1))
                for j in range(T):
                    for e, rows in rest_rows(m * T + j):
                        sp.dma_start(row_weight[rows, b % 2, j, :],
                                     weight_t[e, b * BT:(b + 1) * BT].partition_broadcast(rows.stop - rows.start)
                                     ).then_inc(row_weight_in[b % 2], 16)

            if fp4:
                sp.dma_start(shift[:, :], fp4["shift"]).then_inc(aux_loaded, 16)
                for c in range(chunks):
                    sp.dma_start(first_words[:, c, :], up_src[0, c]).then_inc(first_chunk[c], 16)
                    sp.dma_start(first_scales_at(c), fp4["scales"][0, c].partition_broadcast(P)).then_inc(first_chunk[c], 16)
                    if c == 3:
                        load_x(sp, 0)
                with sp.Fori(0, last_g) as g:
                    for c in range(chunks):
                        sp.wait_ge(decoded, chunks * (g + 1) + c - SLOTS + 1)
                        load_chunk(g + 1, c)
                for b in range(BATCHES):
                    sp.wait_ge(gu_ready, 2 * (steps_before_last * T + (b + 1) * L))
                    sp.dma_start(x_hi[:, b * TPB:(b + 1) * TPB].bitcast(F32).rearrange("p t k n -> p t (k n)"),
                                 fp4["resid"][b * TPB:(b + 1) * TPB].rearrange("t p n -> p t n")).then_inc(resid_loaded[b], 16)
                    if b:
                        sp.wait_ge(final, TPB * b)
                        store(b - 1)
                sp.wait_ge(final, TPB * BATCHES)
                store(BATCHES - 1)
                sp.wait_ge(stored, 16 * BATCHES)
            else:
                sp.dma_start(ident[:, :], routed["ident"]).then_inc(ident_loaded, 16)
                sp.dma_start(comb[:, :, :], weight).then_inc(aux_loaded, 16)
                for j in range(T):
                    sp.dma_start(up_f32[:, j, :, :, :].rearrange("p m k f -> p (m k f)"),
                                 up_src[0, :, j * 2 * D:(j + 1) * 2 * D]).then_inc(first_loaded[j], 16)
                    if j == 0:
                        load_x(sp, 0)
                sp.dma_start(down_f32[:, 0:T, :], down_src[0, 0:T * P].rearrange("(j p) n -> p j n", p=P)
                             ).then_inc(first_loaded[JT], 16)
                for b in range(BATCHES):
                    tiles = slice(b * TPB, (b + 1) * TPB)
                    sp.dma_start(acc[:, tiles, :], start[tiles].rearrange("t p n -> p t n")).then_inc(start_loaded[b], 16)
                    if b + 1 < BATCHES:
                        load_x(sp, b + 1)
                sp.wait_ge(turned_sb, BATCHES)
                sp.dma_start(weight_t, comb_t[:, :, :].rearrange("e b t -> e (b t)")).then_inc(turned_stored, 16)
                sp.wait_ge(turned_stored, 16)
                with sp.Fori(1, mixed_g) as g:
                    sp.wait_ge(weights_lo, 2 * T * g)
                    load_weights(g)
                for g in range(mixed_g, last_g + 1):
                    sp.wait_ge(weights_lo, 2 * T * g)
                    load_weights(g)
                    if g < last_g:
                        for b in range(BATCHES):
                            load_row_weights(g - mixed_g, b)
                with sp.Fori(0, BATCHES) as b:
                    sp.wait_ge(y_free, TPB * (steps_before_last + 1) + TPB * (b + 1))
                    store(b)
                sp.wait_ge(stored, 16 * BATCHES)

        @block.tensor
        def _(pe):
            def step(g, b, odd, tiles=T):
                n = g * BATCHES + b
                before = tiles_before(g, b)
                tokens = bass.ds(b * TPB, TPB)
                for j in range(tiles):
                    q = (odd * tiles + j) % 2
                    pe.wait_ge(gu_free, before + j + 1)
                    pe.wait_ge(weights_lo, 2 * pieces(0) * g + j + 1)
                    for m, ps in ((0, gate_ps[q]), (1, up_ps[q])):
                        for k in range(KT):
                            last = sums(pe, ps[:, :], up_hi[:, j, m, k, :], up_lo[:, j, m, k, :],
                                        x_hi[:, tokens, k, :], x_lo[:, tokens, k, :], k == 0, k == KT - 1)
                        last.then_inc(gu_ready, 1)
                for j in range(tiles):
                    pe.wait_ge(h_ready, before + j + 1)
                    pe.wait_ge(weights_lo, 2 * pieces(0) * g + pieces(g) + j + 1)
                    for t in range(TPB):
                        if j == 0:
                            pe.wait_ge(y_free, n * TPB + t + 1)
                        last = sums(pe, y_ps[t][:, :], h_hi[:, j, t * P:(t + 1) * P], h_lo[:, j, t * P:(t + 1) * P],
                                    down_hi[:, j, :], down_lo[:, j, :], j == 0, j == tiles - 1)
                        if j == tiles - 1:
                            last.then_inc(y_ready, 1)

            if not fp4:
                pe.wait_ge(ident_loaded, 16)
                pe.wait_ge(aux_loaded, 16)
                for t in range(TILES):
                    last = pe.transpose(y_ps[t // TPB][0:routed["columns"], t % TPB * P:(t % TPB + 1) * P], comb[:, t, :], ident[:, :])
                    if t % TPB == TPB - 1:
                        last.then_inc(turned, 1)
                pe.wait_ge(turned_sb, BATCHES)
            for b in range(BATCHES):
                pe.wait_ge(x_loaded[b], 32)
                step(0, b, b % 2)
            with pe.Fori(1, last_g) as g:
                if fp4:
                    for b in range(BATCHES):
                        step(g, b, b % 2)
                else:
                    with pe.Fori(0, BATCHES // 2) as pair:
                        step(g, 2 * pair, 0)
                        step(g, 2 * pair + 1, 1)
            for b in range(BATCHES):
                step(last_g, b, b % 2, L)

        @block.scalar
        def _(act):
            def high_parts(g, first=False):
                if not fp4 and not first:
                    act.wait_ge(weights_loaded, 32 * g)
                for j in range(pieces(g)):
                    if not fp4 and first:
                        act.wait_ge(first_loaded[j], 16)
                    if fp4:
                        act.wait_ge(decoded, chunks * g + 2 * j + 2)
                    if not first:
                        act.wait_ge(gu_ready, 2 * T * BATCHES * g - 2 * T + 2 * min(j, T - 1) + 2)
                    act.copy(up_hi[:, j], up_f32[:, j]).then_inc(weights_hi, 1)
                    if first and fp4:
                        if j == JT - 1:
                            load_x(act, 1)
                        for c in range(2 * j + 3, 2 * j + 5):
                            curve(c, c)
                if first and fp4:
                    for c in range(2 * JT + 3, chunks):
                        curve(c, c)
                if not first:
                    act.wait_ge(y_ready, TPB * BATCHES * g)
                elif not fp4:
                    act.wait_ge(first_loaded[JT], 16)
                for j in range(pieces(g)):
                    if fp4:
                        act.wait_ge(decoded, chunks * g + 2 * JT + j + 1)
                    act.copy(down_hi[:, j, :], down_f32[:, j, :]).then_inc(weights_hi, 1)

            def curve(c_all, c):
                h = c % 2
                act.wait_ge(bits_ready, c_all + 1)
                act.activation(above4[:, h, :], magnitude[:, h, :], ACT.Relu, bias=bias_m4[:, :], scale=1.0)
                act.activation(above6[:, h, :], magnitude[:, h, :], ACT.Relu, bias=bias_m12[:, :], scale=2.0)
                act.activation(half_sign[:, h, :], sign_bit[:, h, :], ACT.Identity, bias=bias_half[:, :],
                               scale=-0.125).then_inc(lines_ready, 1)

            def step(g, b, odd, tiles=T):
                for j in range(tiles):
                    q = (odd * tiles + j) % 2
                    k = tiles_before(g, b) + j
                    act.wait_ge(gu_ready, 2 * k + 1)
                    act.activation(silu_g[:, q, :], gate_ps[q][:, :], ACT.Silu).then_inc(silu_ready, 1)
                    act.wait_ge(gu_free, k + 3)
                    act.copy(h_hi[:, j, :], h_f32[:, q, :]).then_inc(hhi_ready, 1)
                    if fp4 and tiles == T:
                        c = b * JT + j
                        if c < chunks:
                            curve(chunks * (g + 1) + c, c)

            if not fp4:
                for b in range(BATCHES):
                    act.wait_ge(turned, b + 1)
                    act.copy(comb_t[:, b, :], y_ps[b][0:routed["columns"], :]).then_inc(turned_sb, 1)
            if fp4:
                act.wait_ge(bias_set, 3)
                for c in range(3):
                    curve(c, c)
            high_parts(0, first=True)
            if fp4:
                for b in range(BATCHES):
                    if b + 2 < BATCHES:
                        load_x(act, b + 2)
                    step(0, b, b % 2)
                high_parts(1)
                with act.Fori(1, last_g) as g:
                    for b in range(BATCHES):
                        step(g, b, b % 2)
                    high_parts(g + 1)
            else:
                with act.Fori(0, last_g - 1) as g:
                    with act.Fori(0, BATCHES // 2) as pair:
                        step(g, 2 * pair, 0)
                        step(g, 2 * pair + 1, 1)
                    high_parts(g + 1)
                for b in range(BATCHES):
                    step(last_g - 1, b, b % 2)
                high_parts(last_g)
            for b in range(BATCHES):
                step(last_g, b, b % 2, L)
            if fp4:
                for t in range(TILES - TPB, TILES):
                    act.wait_ge(y_free, TPB * (steps_before_last + 1) + t + 1)
                    act.activation(up_f32[:, (t % TPB) // 2, t % 2, :, :].rearrange("p k n -> p (k n)"), acc[:, t, :], ACT.Square, accum_out=meansq[:, t:t + 1]
                                   ).then_inc(meansq_ready, 1)

        @block.gpsimd
        def _(pool):
            def low_part(g, n):
                pool.wait_ge(weights_hi, 2 * pieces(0) * g + n + 1)
                j = n % pieces(g)
                whole, high, low = ((up_f32[:, j], up_hi[:, j], up_lo[:, j]) if n < pieces(g) else
                                    (down_f32[:, j, :], down_hi[:, j, :], down_lo[:, j, :]))
                pool.tensor_tensor(low, whole, high.bitcast(F32), ALU.subtract).then_inc(weights_lo, 1)

            def row_weights(m, b):
                here = sum(len(rest_rows(m * T + j)) for j in range(T))
                before = 2 * sum(len(rest_rows(n)) for n in range(m * T))
                pool.wait_ge(row_weight_in[b % 2], 16 * (before + here * (b // 2 + 1)))
                for j in range(T):
                    k = tiles_before(mixed_g + m, b) + j
                    pool.wait_ge(silu_ready, k + 1)
                    pool.tensor_tensor(silu_g[:, j, :], silu_g[:, j, :], row_weight[:, b % 2, j, :], ALU.mult).then_inc(weighted, 1)

            def scale_chunk(c_all, c, first=False):
                pool.wait_ge(value_ready, c_all + 1)
                to, shape = (up_f32[:, c // 2, c % 2], "p (k f) -> p k f") if c < 2 * JT else (down_f32[:, c - 2 * JT, :], None)
                values, by = value[:, c % 2, :], first_scales_at(c) if first else scales[:, c % SLOTS, :]
                if shape:
                    values, by = values.rearrange(shape, f=P), by.rearrange(shape, f=P)
                pool.tensor_tensor(to, values, by, ALU.mult).then_inc(decoded, 1)

            if fp4:
                pool.memset(power[:, :], -0.5).then_inc(power_set, 1)
                for c in range(chunks):
                    scale_chunk(c, c, first=True)
                    if c in (2, 4, 6):
                        low_part(0, (c - 2) // 2)
                for n in range(JT, 2 * JT):
                    low_part(0, n)
                with pool.Fori(0, last_g) as g:
                    pool.wait_ge(weights_lo, 2 * JT * (g + 1))
                    for c in range(chunks):
                        scale_chunk(chunks * (g + 1) + c, c)
                    for n in range(2 * JT):
                        low_part(g + 1, n)
                pool.wait_ge(power_set, 1)
                for b in range(BATCHES):
                    tiles = slice(b * TPB, (b + 1) * TPB)
                    pool.wait_ge(meansq_ready, TPB * (b + 1))
                    pool.tensor_scalar(meansq[:, tiles], meansq[:, tiles], 1.0 / D, 1e-6, ALU.mult, ALU.add).then_inc(rstd_step, 1)
                    pool.wait_ge(rstd_step, 2 * b + 1)
                    pool.tensor_tensor(rstd[:, tiles], meansq[:, tiles], power[:, tiles], ALU.pow).then_inc(rstd_step, 1)
            else:
                with pool.Fori(0, mixed_g) as g:
                    for n in range(2 * T):
                        low_part(g, n)
                for g in range(mixed_g, last_g):
                    for n in range(2 * T):
                        low_part(g, n)
                    for b in range(BATCHES):
                        row_weights(g - mixed_g, b)
                for n in range(2 * JT):
                    low_part(last_g, n)

        @block.vector
        def _(dve):
            def bits(g, c, first=False):
                if first:
                    dve.wait_ge(first_chunk[c], 32)
                else:
                    dve.wait_ge(chunk_loaded[c % SLOTS], 32 * (JT * (g - 1) + c // SLOTS + 1))
                packed = first_words[:, c, :] if first else words[:, c % SLOTS, :]
                for to, mask in ((magnitude, 7), (sign_bit, 8)):
                    last = dve.tensor_scalar(to[:, c % 2, :], packed, shift[:, :], mask,
                                             ALU.logical_shift_right, ALU.bitwise_and)
                last.then_inc(bits_ready, 1)

            def values(g, c, first=False):
                c_all = chunks * g + c
                h = c % 2
                dve.wait_ge(bits_ready, c_all + 1)
                dve.wait_ge(lines_ready, c_all + 1)
                dve.tensor_tensor(twice[:, h, :], magnitude[:, h, :], above4[:, h, :], ALU.add).then_inc(dq_step, 1)
                dve.wait_ge(dq_step, 2 * c_all + 1)
                dve.tensor_tensor(twice[:, h, :], twice[:, h, :], above6[:, h, :], ALU.add).then_inc(dq_step, 1)
                dve.wait_ge(dq_step, 2 * c_all + 2)
                if first:
                    if c >= 2:
                        dve.wait_ge(decoded, c - 1)
                else:
                    dve.wait_ge(decoded, c_all - (1 if c >= 1 else 0))
                dve.tensor_tensor(value[:, h, :], twice[:, h, :], half_sign[:, h, :], ALU.mult).then_inc(value_ready, 1)

            def step(g, b, odd, tiles=T, first=False, mixed=False):
                n = g * BATCHES + b
                for j in range(tiles):
                    q = (odd * tiles + j) % 2
                    k = tiles_before(g, b) + j
                    if mixed:
                        dve.wait_ge(weighted, k + 1 - tiles_before(mixed_g, 0))
                    else:
                        dve.wait_ge(silu_ready, k + 1)
                    dve.wait_ge(gu_ready, 2 * k + 2)
                    dve.tensor_tensor(h_f32[:, q, :], silu_g[:, q, :], up_ps[q][:, :], ALU.mult).then_inc(gu_free, 1)
                    dve.wait_ge(gu_free, k + 3)
                    dve.wait_ge(hhi_ready, k + 1)
                    dve.tensor_tensor(h_lo[:, j, :], h_f32[:, q, :], h_hi[:, j, :].bitcast(F32),
                                      ALU.subtract).then_inc(h_ready, 1)
                    if fp4 and tiles == L and j == 0 and b:
                        finish(b - 1)
                    if fp4 and tiles == T:
                        c = b * JT + j
                        if 1 <= c <= chunks:
                            values(g + 1, c - 1)
                        if c < chunks:
                            bits(g + 1, c)
                if first and not fp4:
                    dve.wait_ge(start_loaded[b], 16)
                for t in range(TPB):
                    tile = acc[:, bass.ds(b * TPB + t, 1), :].rearrange("p o n -> p (o n)")
                    dve.wait_ge(y_ready, n * TPB + t + 1)
                    dve.wait_ge(y_free, n * TPB + t + 1)
                    if first and fp4:
                        dve.tensor_copy(tile, y_ps[t][:, :]).then_inc(y_free, 1)
                    elif fp4 or mixed:
                        dve.tensor_tensor(tile, tile, y_ps[t][:, :], ALU.add).then_inc(y_free, 1)
                    else:
                        column = routed["columns"] - 1 if isinstance(g, int) and g == last_g else g
                        by = comb[:, bass.ds(b * TPB + t, 1), bass.ds(column, 1)].rearrange("p o n -> p (o n)")
                        dve.scalar_tensor_tensor(tile, y_ps[t][:, :], by, tile, ALU.mult, ALU.add).then_inc(y_free, 1)

            def squares(b):
                for i in range(TPB):
                    t = b * TPB + i
                    dve.wait_ge(y_free, TPB * (steps_before_last + 1) + t + 1)
                    if t:
                        dve.wait_ge(meansq_ready, t)
                    dve.tensor_tensor_reduce(magnitude[:, 0, :].bitcast(F32), acc[:, t, :], acc[:, t, :], 1.0, 0.0, ALU.mult, ALU.add,
                                             meansq[:, t:t + 1]).then_inc(meansq_ready, 1)

            def finish(b):
                dve.wait_ge(rstd_step, 2 * (b + 1))
                dve.wait_ge(resid_loaded[b], 16)
                for i in range(TPB):
                    t = b * TPB + i
                    dve.scalar_tensor_tensor(acc[:, t, :], acc[:, t, :], rstd[:, t:t + 1],
                                             x_hi[:, t, :, :].bitcast(F32).rearrange("p k n -> p (k n)"),
                                             ALU.mult, ALU.add).then_inc(final, 1)

            dve.sem_inc(gu_free, 2)
            dve.sem_inc(y_free, TPB)
            if fp4:
                dve.memset(bias_m4[:, :], -4.0).then_inc(bias_set, 1)
                dve.memset(bias_m12[:, :], -12.0).then_inc(bias_set, 1)
                dve.memset(bias_half[:, :], 0.5).then_inc(bias_set, 1)
                dve.wait_ge(aux_loaded, 16)
                bits(0, 0, first=True)
                for c in range(chunks):
                    if c + 1 < chunks:
                        bits(0, c + 1, first=True)
                    values(0, c, first=True)
                for b in range(BATCHES):
                    step(0, b, b % 2, first=True)
                with dve.Fori(1, last_g) as g:
                    for b in range(BATCHES):
                        step(g, b, b % 2)
                for b in range(BATCHES):
                    step(last_g, b, b % 2, L)
                    if b < BATCHES - 1:
                        squares(b)
                finish(BATCHES - 1)
            else:
                dve.wait_ge(aux_loaded, 16)
                for b in range(BATCHES):
                    step(0, b, b % 2, first=True)
                with dve.Fori(1, mixed_g) as g:
                    with dve.Fori(0, BATCHES // 2) as pair:
                        step(g, 2 * pair, 0)
                        step(g, 2 * pair + 1, 1)
                with dve.Fori(mixed_g, last_g) as g:
                    with dve.Fori(0, BATCHES // 2) as pair:
                        step(g, 2 * pair, 0, mixed=True)
                        step(g, 2 * pair + 1, 1, mixed=True)
                for b in range(BATCHES):
                    step(last_g, b, b % 2, L)


def rest_rows(n):
    return [(e, slice(max(e * REST - n * P, 0), min((e + 1) * REST - n * P, P)))
            for e in range(EXPERTS) if e * REST < (n + 1) * P and (e + 1) * REST > n * P]


SSM_HEADS = 16
SSM_P = 64
SSM_N = 64
E = SSM_HEADS * SSM_P
ET = E // P
TAPS = 4
CONV_TILES = ET + 1
SMALL = SSM_HEADS + EXPERTS + 2
HB = E // BANK
HPG = BANK // P
CONV_ORDER = (ET,) + tuple(range(ET))
ATANH = tuple(1.0 / (2 * n + 1) for n in range(1, 8))


def ssm_phase(nc, x_dram, wts, tables, x_parts, out_dram, comb_dram):
    name = "a1"
    semaphores = []
    with ExitStack() as ctx:
        ctx.callback(clear_semaphores, nc, semaphores)

        def sb(label, shape, dt=F32):
            return ctx.enter_context(nc.sbuf_tensor(f"{name}_{label}", shape, dt))

        def sem(label):
            semaphores.append(nc.alloc_semaphore(f"{name}_{label}"))
            return semaphores[-1]

        def sems(group, labels):
            return {label: sem(f"{group}_{label}") for label in labels.split()}

        z_hi = sb("z_hi", [P, KT, E], F32R)
        z_lo = sb("z_lo", [P, KT, E], F32R)
        c_hi = sb("c_hi", [P, KT, E + 2 * SSM_N], F32R)
        c_lo = sb("c_lo", [P, KT, E + 2 * SSM_N], F32R)
        small_raw = sb("small_raw", [P, KT, SMALL])
        small_hi = sb("small_hi", [P, KT, SMALL], F32R)
        small_lo = sb("small_lo", [P, KT, SMALL], F32R)
        w_raw = sb("w_raw", [P, 2, KT, P])
        w_out = sb("w_out", [P, ET, D])
        norm_w = sb("norm_w", [P, ET])
        conv_w = sb("conv_w", [P, CONV_TILES, TAPS])
        conv_b = sb("conv_b", [P, CONV_TILES])
        dt_bias = sb("dt_bias", [P, SSM_HEADS])
        a_neg = sb("a_neg", [P, SSM_HEADS])
        skip_d = sb("skip_d", [P, SSM_HEADS])
        ident = sb("ident", [P, P])
        upto = sb("upto", [P, P])
        after = sb("after", [P, P])
        ones = sb("ones", [P, P])
        earlier = sb("earlier", [P, EXPERTS, EXPERTS])
        power = sb("power", [P, 1])
        eps_ln = sb("eps_ln", [P, 1])
        eps_rms = sb("eps_rms", [P, 1])

        x = sb("x", [P, TPB, D])
        x_last = sb("x_last", [P, D])
        y_out = w_raw[:, :, :, :].rearrange("p o k n -> p o (k n)")
        small_t = sb("small_t", [SMALL, BT])
        stats = sb("stats", [P, TPB, 6])
        mean_var = sb("mean_var", [P, TPB, 2])
        ln_tmp = sb("ln_tmp", [P, TPB])
        ln_rs = sb("ln_rs", [P, TPB])
        ln_tmp2 = sb("ln_tmp2", [P, 1])
        xn = sb("xn", [P, 2, D])
        xt_hi = sb("xt_hi", [P, TPB, KT, P], F32R)
        xt_lo = sb("xt_lo", [P, TPB, KT, P], F32R)
        tph = [P, TPB, SSM_HEADS]
        dt_raw, dt_abs, dt_exp, dt_den, dt_z, dt_z2, dt_q, dt_pos, dt, a = (
            sb(label, tph) for label in
            ("dt_raw", "dt_abs", "dt_exp", "dt_den", "dt_z", "dt_z2", "dt_q", "dt_pos", "dt", "a"))
        decays = sb("decays", [P, 3, TPB, SSM_HEADS])
        logits = sb("logits", [P, TPB, EXPERTS + 1])
        top = sb("top", [P, TPB])
        probs = sb("probs", [P, TPB, EXPERTS])
        total = sb("total", [P, TPB])
        greater = sb("greater", [P, TPB, EXPERTS, EXPERTS])
        equal = sb("equal", [P, TPB, EXPERTS, EXPERTS])
        rank = sb("rank", [P, TPB, EXPERTS])
        shared = sb("shared", [P, TPB])
        comb = sb("comb", [P, TPB, EXPERTS + 4])

        conv_acc = sb("conv_acc", [P, 2, BT])
        conv = sb("conv", [P, ET + 2, BT])
        b_tok = sb("b_tok", [P, TPB, SSM_N])
        g_mask = sb("g_mask", [P, TPB, P])
        a_mask = sb("a_mask", [P, SSM_HEADS, P])
        l_exp = sb("l_exp", [P, 2, HPG, P])
        m_t = sb("m_t", [P, SSM_HEADS, P])
        h_tok = sb("h_tok", [P, SSM_HEADS, SSM_P])
        h_dt = sb("h_dt", [P, SSM_HEADS, SSM_P])
        h_dec = sb("h_dec", [P, SSM_HEADS, SSM_P])
        z_silu = sb("z_silu", [P, E])
        y = sb("y", [P, SSM_HEADS, SSM_P])
        sq_out = sb("sq_out", [P, E], BF16)
        ss = sb("ss", [P, 1])
        ms = sb("ms", [P, 1])
        y_rs = sb("y_rs", [P, 1])
        yt = sb("yt", [P, ET, P])
        state = sb("state", [SSM_N, SSM_HEADS, SSM_P])

        def banks(label):
            return ctx.enter_context(nc.psum_tensor(f"{name}_{label}", [P, 2, BANK], F32))

        seg_ps, y_ps, off_ps, proj_ps = banks("seg_ps"), banks("y_ps"), banks("off_ps"), banks("proj_ps")

        loaded = sems("loaded", "ident const")
        w = sems("w", "hi small_hi z_hi split z_split small normed a consts")
        ln = sems("ln", "stats_step stats rstd normed")
        xt = sems("xt", "ps hi lo")
        sm = sems("sm", "sums sums_sb ps dt_raw logits abs exp step dt a")
        rt = sems("rt", "step exp tanh rank ready")
        cv = sems("cv", "ps init step done silu")
        bc = sems("bc", "g_ps g_masked b_ps b_tok cum_ps decays")
        sg = sems("sg", "a_mask ps exp m")
        zz = sems("zz", "ps tanh silu")
        hh = sems("hh", "ps tok dt dec skip")
        yy = sems("yy", "diag_ps off_ps off_scaled diag_added skip_added gated ss ms rs t_ps t_sb out_ps x_added")
        st = sems("st", "ps scaled ready")
        x_in = [sem(f"x_in{n}") for n in range(TPB)]
        last_in = sem("last_in")
        y_stored = [sem(f"y_stored{n}") for n in range(TPB)]
        xt_stored = sem("xt_stored")
        comb_stored = sem("comb_stored")
        w_loaded = [sem(f"w_loaded{n}") for n in range(2)]
        z_loaded = [sem(f"z_loaded{n}") for n in range(2)]
        out_loaded = sem("out_loaded")

        Z_PIECES, C_PIECES = E // P, E // P + 1
        z_raw = (m_t, a_mask)
        N_CONST = 11

        def c_piece(m):
            return Z_PIECES + (m - 1) % C_PIECES

        def c_columns(m):
            return slice(((m - 1) % C_PIECES) * P, ((m - 1) % C_PIECES + 1) * P)

        def z_whole(n):
            return z_raw[n // (Z_PIECES // 2)][:, n % (Z_PIECES // 2) * KT:(n % (Z_PIECES // 2) + 1) * KT, :]

        def heads(ap, n_inner):
            return ap.unsqueeze(2).to_broadcast([ap.shape[0], SSM_HEADS, n_inner])

        block = ctx.enter_context(nc.Block())

        def whole(bank_pair):
            return bank_pair[:, :, :].rearrange("p b n -> p (b n)").rearrange("p (h d) -> p h d", h=SSM_HEADS)

        @block.sync
        def _(sp):
            def load_x(batch, i):
                sp.dma_start(x[:, i, :], x_dram[bass.ds(batch * TPB + i, 1)].rearrange("o p n -> (o p) n")
                             ).then_inc(x_in[i], 16)

            def load_last(batch):
                sp.dma_start(x_last[:, :], x_dram[bass.ds(batch * TPB + TPB - 1, 1)].rearrange("o p n -> (o p) n")
                             ).then_inc(last_in, 16)

            def store_batch_parts(b):
                sp.wait_ge(xt["hi"], TPB * b + TPB)
                sp.wait_ge(xt["lo"], TPB * b + TPB)
                for part, buf in ((0, xt_hi), (1, xt_lo)):
                    sp.dma_start(x_parts[part, bass.ds(b * TPB, TPB)].rearrange("t p n -> p t n"),
                                 buf[:, :, :, :].bitcast(F32).rearrange("p t k n -> p t (k n)")).then_inc(xt_stored, 16)

            def store_y(b, i):
                sp.wait_ge(yy["x_added"], b * TPB + i + 1)
                sp.dma_start(out_dram[bass.ds(b * TPB + i, 1)].rearrange("o p n -> (o p) n"), y_out[:, i % 2, :]
                             ).then_inc(y_stored[i], 16)

            def store_comb(b):
                sp.wait_ge(rt["ready"], b + 1)
                sp.dma_start(comb_dram[:, bass.ds(b * TPB, TPB), :], comb[:, :, :]).then_inc(comb_stored, 16)

            load_x(0, 0)
            sp.dma_start(ident[:, :], tables["ident"]).then_inc(loaded["ident"], 16)
            for i in range(1, TPB):
                load_x(0, i)
            consts = ((small_raw, wts["small"]), (conv_w, wts["conv_w"]), (conv_b, wts["conv_b"]),
                      (dt_bias, wts["dt_bias"].partition_broadcast(P)), (a_neg, wts["a_log"].partition_broadcast(P)),
                      (skip_d, wts["skip_d"].partition_broadcast(P)), (norm_w, wts["norm_w"]),
                      (upto, tables["upto"]), (after, tables["after"]), (ones, tables["ones"]),
                      (earlier, tables["earlier"].partition_broadcast(P)))
            assert len(consts) == N_CONST
            for dst, src in consts:
                sp.dma_start(dst[:], src).then_inc(loaded["const"], 16)
            load_last(0)
            for m in range(C_PIECES):
                if m >= 2:
                    sp.wait_ge(w["split"], m - 1)
                sp.dma_start(w_raw[:, m % 2, :, :], wts["in_proj"][c_piece(m)]).then_inc(w_loaded[m % 2], 16)
                if m in (3, 5):
                    n = (m - 3) // 2
                    sp.dma_start(z_raw[n][:, :, :].rearrange("p (n k) f -> p n (k f)", k=KT),
                                 wts["in_proj"][n * Z_PIECES // 2:(n + 1) * Z_PIECES // 2].rearrange("n p k f -> p n (k f)")
                                 ).then_inc(z_loaded[n], 16)
            sp.dma_start(w_out[:, :, :], wts["out_proj"]).then_inc(out_loaded, 16)
            store_batch_parts(0)
            sp.wait_ge(ln["normed"], TPB)
            load_x(1, 3)

            def body(b, last):
                store_comb(b)
                for i in range(TPB - 1):
                    store_y(b, i)
                    if not last:
                        load_x(b + 1, i)
                if not last:
                    store_batch_parts(b + 1)
                    sp.wait_ge(ln["normed"], TPB * (b + 2))
                    load_x((b + 2) % BATCHES, 3)
                store_y(b, TPB - 1)
                if not last:
                    load_last(b + 1)

            with sp.Fori(0, BATCHES - 1) as b:
                body(b, False)
            body(BATCHES - 1, True)
            sp.wait_ge(comb_stored, 16 * BATCHES)
            sp.wait_ge(xt_stored, 32 * BATCHES)
            for i in range(TPB):
                sp.wait_ge(y_stored[i], 16 * BATCHES)
            sp.wait_ge(x_in[3], 16 * (BATCHES + 1))

        @block.tensor
        def _(pe):
            def sums(to, l_hi, l_lo, r_hi, r_lo, k):
                pe.matmul(to, l_hi, r_hi, start=k == 0, stop=False)
                pe.matmul(to, l_hi, r_lo, start=False, stop=False)
                return pe.matmul(to, l_lo, r_hi, start=False, stop=k == KT - 1)

            def x_turned(b, tiles, first=False):
                for i in tiles:
                    pe.wait_ge(ln["normed"], TPB * b + i + 1)
                    if i >= 2:
                        pe.wait_ge(xt["hi"], TPB * b + i - 1)
                        pe.wait_ge(xt["lo"], TPB * b + i - 1)
                    elif not first:
                        pe.wait_ge(sg["exp"], HPG * TPB * b)
                    for k in range(KT):
                        last = pe.transpose(seg_ps[:, i % 2, k * P:(k + 1) * P], xn[:, i % 2, k * P:(k + 1) * P], ident[:, :])
                    last.then_inc(xt["ps"], 1)

            def small_proj(b):
                for k in range(KT):
                    last = sums(seg_ps[0:SMALL, 1, :], small_hi[:, k, :], small_lo[:, k, :], xt_hi[:, :, k, :], xt_lo[:, :, k, :], k)
                last.then_inc(sm["sums"], 1)

            def small_turned(b):
                for i in range(TPB):
                    last = pe.transpose(seg_ps[:, 0, i * SMALL:(i + 1) * SMALL], small_t[:, i * P:(i + 1) * P],
                                        ident[0:SMALL, 0:SMALL])
                last.then_inc(sm["ps"], 1)

            def conv_proj(b, q, first):
                f = CONV_ORDER[q]
                cols = slice(f * P, (f + 1) * P)
                if first:
                    pe.wait_ge(w["split"], q + 1)
                if q >= 2:
                    pe.wait_ge(cv["done"], CONV_TILES * b + q - 1)
                elif not first:
                    pe.wait_ge(zz["silu"], HB * TPB * b)
                for k in range(KT):
                    last = sums(proj_ps[:, q % 2, :], c_hi[:, k, cols], c_lo[:, k, cols], xt_hi[:, :, k, :], xt_lo[:, :, k, :], k)
                last.then_inc(cv["ps"], 1)

            def grams(b):
                pe.wait_ge(cv["silu"], CONV_TILES * b + 1)
                pe.wait_ge(sm["logits"], b + 1)
                for i in range(TPB):
                    cols = slice(i * P, (i + 1) * P)
                    last = pe.matmul(seg_ps[:, 1, cols], conv[0:SSM_N, ET, cols], conv[0:SSM_N, ET + 1, cols], start=True, stop=True)
                last.then_inc(bc["g_ps"], 1)
                for i in range(TPB):
                    last = pe.transpose(seg_ps[:, 0, i * SSM_N:(i + 1) * SSM_N], conv[0:SSM_N, ET, i * P:(i + 1) * P],
                                        ident[0:SSM_N, 0:SSM_N])
                last.then_inc(bc["b_ps"], 1)

            def cumulate(b):
                pe.wait_ge(sm["a"], b + 1)
                pe.wait_ge(bc["b_tok"], b + 1)
                n = TPB * SSM_HEADS
                for m, mask in enumerate((after, upto, ones)):
                    last = pe.matmul(seg_ps[:, 0, m * n:(m + 1) * n], mask[:, :], a[:, :, :].rearrange("p t h -> p (t h)"),
                                     start=True, stop=True)
                last.then_inc(bc["cum_ps"], 1)

            def segments(t, i, b):
                pe.wait_ge(sg["a_mask"], t + 1)
                for g in range(HPG):
                    if g >= 2:
                        pe.wait_ge(sg["exp"], HPG * t + g - 1)
                    elif i:
                        pe.wait_ge(sg["exp"], HPG * t - 1 + g)
                    elif g == 0:
                        pe.wait_ge(bc["decays"], b + 1)
                    else:
                        pe.wait_ge(bc["g_masked"], b + 1)
                    pe.matmul(seg_ps[:, g % 2, :], after[:, :], a_mask[:, g * HPG:(g + 1) * HPG, :],
                              start=True, stop=True).then_inc(sg["ps"], 1)

            def z_proj(t, i, b, half):
                if isinstance(t, int) and half == 0:
                    pe.wait_ge(w["z_split"], Z_PIECES)
                pe.wait_ge(hh["tok"], HB * t + half + 1)
                for k in range(KT):
                    cols = slice(half * BANK, (half + 1) * BANK)
                    last = sums(proj_ps[:, half, :], xt_hi[:, i, k, :], xt_lo[:, i, k, :], z_hi[:, k, cols], z_lo[:, k, cols], k)
                last.then_inc(zz["ps"], 1)

            def h_turned(t, i, b, half):
                if i == 0:
                    pe.wait_ge(cv["silu"], CONV_TILES * (b + 1))
                else:
                    pe.wait_ge(zz["silu"], HB * t - 1 + half)
                for f in range(ET // HB):
                    last = pe.transpose(proj_ps[:, half, f * P:(f + 1) * P],
                                        conv[:, half * (ET // HB) + f, i * P:(i + 1) * P], ident[:, :])
                last.then_inc(hh["ps"], 1)

            def y_turned(t):
                pe.wait_ge(yy["gated"], t + 1)
                for f in range(ET):
                    last = pe.transpose(y_ps[:, f // HPG, (f % HPG) * P:(f % HPG + 1) * P],
                                        y[:, 2 * f:2 * f + 2, :].rearrange("p h d -> p (h d)"), ident[:, :])
                last.then_inc(yy["t_ps"], 1)

            def out_proj(t):
                pe.wait_ge(yy["t_sb"], t + 1)
                for f in range(ET):
                    last = pe.matmul(off_ps[:, 0, :], yt[:, f, :], w_out[:, f, :], start=f == 0, stop=f == ET - 1)
                last.then_inc(yy["out_ps"], 1)

            def project_batch(b, before):
                first = before is None
                x_turned(b, range(TPB) if first else range(2, TPB), first)
                pe.wait_ge(xt["hi"], TPB * (b + 1))
                pe.wait_ge(xt["lo"], TPB * (b + 1))
                if first:
                    pe.wait_ge(w["small"], 1)
                small_proj(b)
                for q in range(CONV_TILES):
                    if q == 1:
                        pe.wait_ge(sm["sums_sb"], b + 1)
                    conv_proj(b, q, first)
                    if q == 1:
                        small_turned(b)
                    if q == 4:
                        grams(b)
                    if q == 6 and not first:
                        y_turned(before)
                cumulate(b)
                if not first:
                    out_proj(before)

            def ahead(t, i, b):
                for half in range(HB):
                    h_turned(t, i, b, half)
                segments(t, i, b)
                for half in range(HB):
                    z_proj(t, i, b, half)

            pe.wait_ge(loaded["ident"], 16)
            project_batch(0, None)
            ahead(0, 0, 0)

            def body(b, last):
                for i in range(TPB):
                    t = b * TPB + i
                    if i == TPB - 1 and not last:
                        x_turned(b + 1, (0, 1))
                    if i:
                        pe.wait_ge(st["ready"], 3 * b + i)
                        for half in (1, 0):
                            if half == 0:
                                pe.wait_ge(yy["x_added"], t)
                            mm = pe.matmul(off_ps[:, half, :], conv[0:SSM_N, ET + 1, i * P:(i + 1) * P],
                                           state[:, half * 8:(half + 1) * 8, :], start=True, stop=True)
                        mm.then_inc(yy["off_ps"], 1)
                    pe.wait_ge(sg["m"], HPG * (t + 1))
                    pe.wait_ge(hh["dt"], t + 1)
                    if not (isinstance(b, int) and b == 0 and i == 0) and i:
                        pe.wait_ge(yy["t_sb"], t)
                    for h in range(SSM_HEADS):
                        mm = pe.matmul(y_ps[:, h // 8, (h % 8) * SSM_P:(h % 8 + 1) * SSM_P], m_t[:, h, :], h_dt[:, h, :],
                                       start=True, stop=True)
                    mm.then_inc(yy["diag_ps"], 1)
                    if i < TPB - 1:
                        segments(t + 1, i + 1, b)
                        pe.wait_ge(hh["dec"], t + 1)
                        if i:
                            pe.wait_ge(yy["off_scaled"], 3 * b + i)
                        for half in range(HB):
                            mm = pe.matmul(off_ps[0:SSM_N, half, :], b_tok[:, i, :], h_dec[:, half * 8:(half + 1) * 8, :],
                                           start=True, stop=True)
                        mm.then_inc(st["ps"], 1)
                        for half in range(HB):
                            h_turned(t + 1, i + 1, b, half)
                        y_turned(t)
                        for half in range(HB):
                            z_proj(t + 1, i + 1, b, half)
                        pe.wait_ge(st["ready"], 3 * b + i + 1)
                        out_proj(t)
                    elif last:
                        y_turned(t)
                        out_proj(t)
                    else:
                        project_batch(b + 1, t)
                        ahead(t + 1, 0, b + 1)

            with pe.Fori(0, BATCHES - 1) as b:
                body(b, False)
            body(BATCHES - 1, True)

        @block.scalar
        def _(act):
            def project_batch(b, before):
                first = before is None
                for i in range(TPB) if first else range(2, TPB):
                    x_high(b, i)
                    if i == 1:
                        if first:
                            w_small_high()
                            w_high(0)
                            w_high(1)
                act.wait_ge(sm["sums"], b + 1)
                act.copy(small_t[:, :], seg_ps[0:SMALL, 1, :]).then_inc(sm["sums_sb"], 1)
                if not first:
                    square(before)
                for q in range(CONV_TILES + 1):
                    if first:
                        if q + 2 < C_PIECES:
                            w_high(q + 2)
                        if 0 <= q - 2 < Z_PIECES:
                            z_high(q - 2)
                    if q < CONV_TILES:
                        f = CONV_ORDER[q]
                        act.wait_ge(cv["ps"], CONV_TILES * b + q + 1)
                        if q >= 2:
                            act.wait_ge(cv["silu"], CONV_TILES * b + q - 1)
                        act.activation(conv_acc[:, q % 2, :], proj_ps[:, q % 2, :], ACT.Identity,
                                       bias=conv_b[:, f:f + 1], scale=conv_w[:, f, TAPS - 1:TAPS]).then_inc(cv["init"], 1)
                    if q:
                        f = CONV_ORDER[q - 1]
                        act.wait_ge(cv["done"], CONV_TILES * b + q)
                        if f < ET:
                            last = act.activation(conv[:, f, :], conv_acc[:, (q - 1) % 2, :], ACT.Silu)
                        else:
                            for n in range(2):
                                last = act.activation(conv[0:SSM_N, ET + n, :],
                                                      conv_acc[n * SSM_N:(n + 1) * SSM_N, (q - 1) % 2, :], ACT.Silu)
                        last.then_inc(cv["silu"], 1)
                    if q == 2:
                        act.wait_ge(sm["dt_raw"], b + 1)
                        act.activation(dt_abs[:, :, :], dt_raw[:, :, :], ACT.Abs).then_inc(sm["abs"], 1)
                        act.wait_ge(sm["abs"], b + 1)
                        act.activation(dt_exp[:, :, :], dt_abs[:, :, :], ACT.Exp, scale=-1.0).then_inc(sm["exp"], 1)
                        act.wait_ge(rt["step"], 7 * b + 2)
                        act.activation(probs[:, :, :], logits[:, :, 0:EXPERTS], ACT.Exp).then_inc(rt["exp"], 1)
                        act.activation(shared[:, :], logits[:, :, EXPERTS], ACT.Tanh, scale=0.5).then_inc(rt["tanh"], 1)
                    if q == 5:
                        act.wait_ge(bc["b_ps"], b + 1)
                        act.copy(b_tok[:, :, :], seg_ps[:, 0, 0:TPB * SSM_N].rearrange("p (t n) -> p t n", t=TPB)
                                 ).then_inc(bc["b_tok"], 1)
                    if q == 7 and not first:
                        y_out_copy(before)
                act.wait_ge(bc["cum_ps"], b + 1)
                act.activation(decays[:, :, :, :].rearrange("p m t h -> p (m t h)"), seg_ps[:, 0, 0:3 * TPB * SSM_HEADS],
                               ACT.Exp).then_inc(bc["decays"], 1)

            def x_high(b, i):
                if not (isinstance(b, int) and b == 0):
                    if i in (0, 2):
                        act.wait_ge(zz["ps"], HB * (TPB * b - (0 if i else 2)))
                        act.wait_ge(xt_stored, 32 * b)
                act.wait_ge(xt["ps"], TPB * b + i + 1)
                act.copy(xt_hi[:, i, :, :], seg_ps[:, i % 2, :].rearrange("p (k n) -> p k n", k=KT)).then_inc(xt["hi"], 1)

            def w_small_high():
                act.wait_ge(loaded["const"], 16 * N_CONST)
                act.copy(small_hi[:, :, :], small_raw[:, :, :]).then_inc(w["small_hi"], 1)
                act.activation(a_neg[:, :], a_neg[:, :], ACT.Exp).then_inc(w["a"], 1)

            def w_high(m):
                act.wait_ge(w_loaded[m % 2], 16 * (m // 2 + 1))
                act.copy(c_hi[:, :, c_columns(m)], w_raw[:, m % 2, :, :]).then_inc(w["hi"], 1)

            def z_high(n):
                act.wait_ge(z_loaded[n // (Z_PIECES // 2)], 16)
                act.copy(z_hi[:, :, n * P:(n + 1) * P], z_whole(n)).then_inc(w["z_hi"], 1)

            def segments(t):
                for g in range(HPG):
                    act.wait_ge(sg["ps"], HPG * t + g + 1)
                    if not (isinstance(t, int) and t == 0 and g < 2):
                        act.wait_ge(sg["m"], HPG * t + g - 1)
                    act.activation(l_exp[:, g % 2, :, :], seg_ps[:, g % 2, :].rearrange("p (h l) -> p h l", h=HPG),
                                   ACT.Exp).then_inc(sg["exp"], 1)

            def z_tanh(t, half):
                if half == 0 and not (isinstance(t, int) and t == 0):
                    act.wait_ge(yy["gated"], t)
                act.wait_ge(zz["ps"], HB * t + half + 1)
                act.activation(z_silu[:, half * BANK:(half + 1) * BANK], proj_ps[:, half, :], ACT.Tanh, scale=0.5
                               ).then_inc(zz["tanh"], 1)

            def h_copied(t):
                if not (isinstance(t, int) and t == 0):
                    act.wait_ge(yy["skip_added"], t)
                    act.wait_ge(hh["dec"], t)
                for half in range(HB):
                    act.wait_ge(hh["ps"], HB * t + half + 1)
                    act.copy(h_tok[:, half * 8:(half + 1) * 8, :], proj_ps[:, half, :].rearrange("p (h d) -> p h d", d=SSM_P)
                             ).then_inc(hh["tok"], 1)

            def ahead(t):
                h_copied(t)
                segments(t)
                z_tanh(t, 0)
                z_tanh(t, 1)

            def square(t):
                act.wait_ge(yy["gated"], t + 1)
                if not (isinstance(t, int) and t == 0):
                    act.wait_ge(yy["ms"], t)
                act.activation(sq_out[:, :], y[:, :, :].rearrange("p h d -> p (h d)"), ACT.Square,
                               accum_out=ss[:, :]).then_inc(yy["ss"], 1)

            def y_out_copy(t):
                act.wait_ge(yy["t_ps"], t + 1)
                act.copy(yt[:, :, :], y_ps[:, :, :].rearrange("p b (f n) -> p (b f) n", n=P)).then_inc(yy["t_sb"], 1)

            act.wait_ge(w["consts"], 3)
            project_batch(0, None)
            ahead(0)

            def body(b, last):
                for i in range(TPB):
                    t = b * TPB + i
                    if i < TPB - 1:
                        segments(t + 1)
                        h_copied(t + 1)
                        y_out_copy(t)
                        z_tanh(t + 1, 0)
                        z_tanh(t + 1, 1)
                        square(t)
                    elif last:
                        square(t)
                        y_out_copy(t)
                    else:
                        x_high(b + 1, 0)
                        x_high(b + 1, 1)
                        project_batch(b + 1, t)
                        ahead(t + 1)

            with act.Fori(0, BATCHES - 1) as b:
                body(b, False)
            body(BATCHES - 1, True)

        @block.gpsimd
        def _(pool):
            def rstd_pair(b, pair):
                tiles = slice(2 * pair, 2 * pair + 2)
                pool.wait_ge(ln["stats"], TPB * b + 2 * pair + 2)
                pool.tensor_tensor(ln_tmp[:, tiles], mean_var[:, tiles, 1], eps_ln[:, :].to_broadcast([P, 2]), ALU.add
                                   ).then_inc(ln["rstd"], 1)
                pool.wait_ge(ln["rstd"], 4 * b + 2 * pair + 1)
                pool.tensor_tensor(ln_rs[:, tiles], ln_tmp[:, tiles], power[:, :].to_broadcast([P, 2]), ALU.pow).then_inc(ln["rstd"], 1)

            def mask_a(t, i, b):
                if i == 0:
                    pool.wait_ge(sm["a"], b + 1)
                if not (isinstance(t, int) and t == 0):
                    pool.wait_ge(sg["ps"], HPG * t)
                pool.tensor_tensor(a_mask[:, :, :], heads(a[:, i, :], P), upto[:, :].unsqueeze(1).to_broadcast([P, SSM_HEADS, P]),
                                   ALU.mult).then_inc(sg["a_mask"], 1)

            def h_products(t, i, b):
                pool.wait_ge(hh["tok"], HB * (t + 1))
                if not (isinstance(t, int) and t == 0):
                    pool.wait_ge(yy["diag_ps"], t)
                pool.tensor_tensor(h_dt[:, :, :], h_tok[:, :, :], heads(dt[:, i, :], SSM_P), ALU.mult).then_inc(hh["dt"], 1)
                pool.wait_ge(hh["dt"], t + 1)
                if i == 0:
                    pool.wait_ge(bc["decays"], b + 1)
                if i:
                    pool.wait_ge(st["ps"], 3 * b + i)
                pool.tensor_tensor(h_dec[:, :, :], h_dt[:, :, :], heads(decays[:, 0, i, :], SSM_P), ALU.mult).then_inc(hh["dec"], 1)
                pool.tensor_tensor(h_tok[:, :, :], h_tok[:, :, :], heads(skip_d[:, :], SSM_P), ALU.mult).then_inc(hh["skip"], 1)

            def rms(t):
                pool.wait_ge(yy["ss"], t + 1)
                pool.tensor_tensor(ms[:, :], ss[:, :], eps_rms[:, :], ALU.add).then_inc(yy["ms"], 1)
                pool.wait_ge(yy["ms"], t + 1)
                if not (isinstance(t, int) and t == 0):
                    pool.wait_ge(yy["x_added"], t)
                pool.tensor_tensor(y_rs[:, :], ms[:, :], power[:, :], ALU.pow).then_inc(yy["rs"], 1)

            pool.memset(power[:, :], -0.5).then_inc(w["consts"], 1)
            pool.memset(eps_ln[:, :], 1e-5).then_inc(w["consts"], 1)
            pool.memset(eps_rms[:, :], 4 * E * 1e-6).then_inc(w["consts"], 1)
            pool.wait_ge(w["consts"], 3)
            rstd_pair(0, 0)
            rstd_pair(0, 1)
            for n in range(Z_PIECES):
                cols = slice(n * P, (n + 1) * P)
                pool.wait_ge(w["z_hi"], n + 1)
                pool.tensor_tensor(z_lo[:, :, cols], z_whole(n), z_hi[:, :, cols].bitcast(F32), ALU.subtract
                                   ).then_inc(w["z_split"], 1)
            pool.wait_ge(loaded["const"], 16 * N_CONST)
            pool.wait_ge(w["z_split"], Z_PIECES)
            mask_a(0, 0, 0)
            h_products(0, 0, 0)
            mask_a(1, 1, 0)

            def body(b, last):
                for i in range(TPB):
                    t = b * TPB + i
                    if i in (1, 2):
                        pool.wait_ge(yy["off_ps"], 3 * b + i)
                        pool.tensor_tensor(state[:, :, :], state[:, :, :], heads(decays[0:SSM_N, 2, i, :], SSM_P),
                                           ALU.mult).then_inc(st["scaled"], 1)
                    if i >= TPB - 2 and not last:
                        rstd_pair(b + 1, i - (TPB - 2))
                    rms(t)
                    if i < TPB - 1:
                        h_products(t + 1, i + 1, b)
                        if i < TPB - 2:
                            mask_a(t + 2, i + 2, b)
                    elif not last:
                        mask_a(t + 1, 0, b + 1)
                        h_products(t + 1, 0, b + 1)
                        mask_a(t + 2, 1, b + 1)

            with pool.Fori(0, BATCHES - 1) as b:
                body(b, False)
            body(BATCHES - 1, True)

        @block.vector
        def _(dve):
            def small_parts(b):
                dve.wait_ge(sm["ps"], b + 1)
                small = seg_ps[:, 0, 0:TPB * SMALL].rearrange("p (t c) -> p t c", t=TPB)
                dve.tensor_tensor(dt_raw[:, :, :], small[:, :, 0:SSM_HEADS], dt_bias[:, :].unsqueeze(1).to_broadcast(tph),
                                  ALU.add).then_inc(sm["dt_raw"], 1)
                dve.tensor_copy(logits[:, :, :], small[:, :, SSM_HEADS:SSM_HEADS + EXPERTS + 1]).then_inc(sm["logits"], 1)
                dve.wait_ge(sm["dt_raw"], b + 1)
                dve.tensor_scalar(dt_pos[:, :, :], dt_raw[:, :, :], 0.0, None, ALU.max)
                softmax_max(b)

            def softplus(b, second_half):
                STEPS = 5 + len(ATANH)
                n = [STEPS * b + (5 if second_half else 0)]

                def step(ins):
                    ins.then_inc(sm["step"], 1)
                    n[0] = n[0] + 1
                    dve.wait_ge(sm["step"], n[0])

                if not second_half:
                    dve.wait_ge(sm["exp"], b + 1)
                    step(dve.tensor_scalar(dt_den[:, :, :], dt_exp[:, :, :], 2.0, None, ALU.add))
                    step(dve.reciprocal(dt_den[:, :, :], dt_den[:, :, :]))
                    step(dve.tensor_tensor(dt_z[:, :, :], dt_exp[:, :, :], dt_den[:, :, :], ALU.mult))
                    step(dve.tensor_tensor(dt_z2[:, :, :], dt_z[:, :, :], dt_z[:, :, :], ALU.mult))
                    step(dve.tensor_scalar(dt_q[:, :, :], dt_z2[:, :, :], ATANH[-1], None, ALU.mult))
                    return
                for c in ATANH[-2::-1]:
                    step(dve.scalar_tensor_tensor(dt_q[:, :, :], dt_q[:, :, :], c, dt_z2[:, :, :], ALU.add, ALU.mult))
                step(dve.scalar_tensor_tensor(dt_q[:, :, :], dt_q[:, :, :], 1.0, dt_z[:, :, :], ALU.add, ALU.mult))
                dve.scalar_tensor_tensor(dt[:, :, :], dt_q[:, :, :], 2.0, dt_pos[:, :, :], ALU.mult, ALU.add).then_inc(sm["dt"], 1)
                dve.wait_ge(sm["dt"], b + 1)
                dve.scalar_tensor_tensor(a[:, :, :], dt[:, :, :], -1.0, a_neg[:, :].unsqueeze(1).to_broadcast(tph),
                                         ALU.mult, ALU.mult).then_inc(sm["a"], 1)

            def softmax_max(b):
                dve.wait_ge(sm["logits"], b + 1)
                dve.tensor_reduce(top[:, :], logits[:, :, 0:EXPERTS], AX_X, ALU.max).then_inc(rt["step"], 1)
                dve.wait_ge(rt["step"], 7 * b + 1)
                dve.tensor_tensor(logits[:, :, 0:EXPERTS], logits[:, :, 0:EXPERTS],
                                  top[:, :].unsqueeze(2).to_broadcast([P, TPB, EXPERTS]), ALU.subtract).then_inc(rt["step"], 1)

            def route(b):
                pairs = [P, TPB, EXPERTS, EXPERTS]
                dve.wait_ge(rt["exp"], b + 1)
                dve.tensor_reduce(total[:, :], probs[:, :, :], AX_X, ALU.add).then_inc(rt["step"], 1)
                dve.wait_ge(rt["step"], 7 * b + 3)
                dve.reciprocal(total[:, :], total[:, :]).then_inc(rt["step"], 1)
                dve.wait_ge(rt["step"], 7 * b + 4)
                dve.tensor_tensor(probs[:, :, :], probs[:, :, :], total[:, :].unsqueeze(2).to_broadcast([P, TPB, EXPERTS]),
                                  ALU.mult).then_inc(rt["step"], 1)
                dve.wait_ge(rt["step"], 7 * b + 5)
                other = probs[:, :, :].unsqueeze(2).to_broadcast(pairs)
                own = probs[:, :, :].unsqueeze(3).to_broadcast(pairs)
                dve.tensor_tensor(greater[:, :, :, :], other, own, ALU.is_gt)
                dve.tensor_tensor(equal[:, :, :, :], other, own, ALU.is_equal).then_inc(rt["step"], 1)
                dve.wait_ge(rt["step"], 7 * b + 6)
                dve.tensor_tensor(equal[:, :, :, :], equal[:, :, :, :], earlier[:, :, :].unsqueeze(1).to_broadcast(pairs),
                                  ALU.mult).then_inc(rt["step"], 1)
                dve.wait_ge(rt["step"], 7 * b + 7)
                dve.tensor_tensor(greater[:, :, :, :], greater[:, :, :, :], equal[:, :, :, :], ALU.add).then_inc(rt["rank"], 1)
                dve.wait_ge(rt["rank"], 2 * b + 1)
                dve.tensor_reduce(rank[:, :, :], greater[:, :, :, :], AX_X, ALU.add).then_inc(rt["rank"], 1)
                dve.wait_ge(rt["rank"], 2 * b + 2)
                if not (isinstance(b, int) and b == 0):
                    dve.wait_ge(comb_stored, 16 * b)
                dve.scalar_tensor_tensor(comb[:, :, 0:EXPERTS], rank[:, :, :], 2.0, probs[:, :, :], ALU.is_lt, ALU.mult)
                dve.wait_ge(rt["tanh"], b + 1)
                dve.tensor_scalar(comb[:, :, EXPERTS:EXPERTS + 4], shared[:, :].unsqueeze(2).to_broadcast([P, TPB, 4]), 0.5, 0.5,
                                  ALU.mult, ALU.add).then_inc(rt["ready"], 1)

            def project_batch(b, before):
                first = before is None
                if first:
                    pair_stats(b, 0)
                    pair_normed(b, 0, 0)
                    pair_normed(b, 0, 1)
                    pair_stats(b, 1)
                    low_part(b, 0)
                    low_part(b, 1)
                pair_normed(b, 1, 0)
                pair_normed(b, 1, 1)
                if first:
                    w_small_low()
                low_part(b, 2)
                low_part(b, 3)
                if first:
                    w_low(0)
                    w_low(1)
                if not first:
                    y_gated(before, TPB - 1, b - 1)
                for q in range(CONV_TILES):
                    f = CONV_ORDER[q]
                    for tap in range(1, TAPS):
                        if tap == 1:
                            dve.wait_ge(cv["init"], CONV_TILES * b + q + 1)
                        else:
                            dve.wait_ge(cv["step"], (TAPS - 2) * (CONV_TILES * b + q) + tap - 1)
                        acc = conv_acc[:, q % 2, tap:BT]
                        last = dve.scalar_tensor_tensor(acc, proj_ps[:, q % 2, 0:BT - tap],
                                                        conv_w[:, f, TAPS - 1 - tap:TAPS - tap], acc, ALU.mult, ALU.add)
                        last.then_inc(cv["done"] if tap == TAPS - 1 else cv["step"], 1)
                    if q == 6:
                        dve.wait_ge(bc["g_ps"], b + 1)
                        dve.tensor_tensor(g_mask[:, :, :], seg_ps[:, 1, :].rearrange("p (t l) -> p t l", t=TPB),
                                          upto[:, :].unsqueeze(1).to_broadcast([P, TPB, P]), ALU.mult).then_inc(bc["g_masked"], 1)
                    if q == 1:
                        small_parts(b)
                    if q in (3, 4):
                        softplus(b, q == 4)
                    if first and q + 2 < C_PIECES:
                        w_low(q + 2)
                if not first:
                    add_out(before, TPB - 1, b - 1)
                route(b)

            def pair_stats(b, pair):
                for i in (2 * pair, 2 * pair + 1):
                    dve.wait_ge(x_in[i], 16 * b + 16)
                    last = dve.bn_stats(stats[:, i, :], x[:, i, :])
                last.then_inc(ln["stats_step"], 1)
                dve.wait_ge(ln["stats_step"], 2 * b + pair + 1)
                dve.tensor_copy(ln_tmp2[:, :], stats[:, 2 * pair + 1, 0:1])
                for i in (2 * pair, 2 * pair + 1):
                    dve.bn_aggr(mean_var[:, i, :], stats[:, i, :]).then_inc(ln["stats"], 1)

            def pair_normed(b, pair, n):
                i = 2 * pair + n
                dve.wait_ge(ln["rstd"], 4 * b + 2 * pair + 2)
                if pair:
                    dve.wait_ge(xt["ps"], TPB * b + i - 1)
                dve.tensor_scalar(xn[:, i % 2, :], x[:, i, :], mean_var[:, i, 0:1], ln_rs[:, i:i + 1],
                                  ALU.subtract, ALU.mult).then_inc(ln["normed"], 1)

            def low_part(b, i):
                dve.wait_ge(xt["hi"], TPB * b + i + 1)
                dve.tensor_tensor(xt_lo[:, i, :, :], seg_ps[:, i % 2, :].rearrange("p (k n) -> p k n", k=KT),
                                  xt_hi[:, i, :, :].bitcast(F32), ALU.subtract).then_inc(xt["lo"], 1)

            def w_small_low():
                dve.wait_ge(w["small_hi"], 1)
                dve.wait_ge(loaded["const"], 16 * N_CONST)
                dve.tensor_tensor(small_lo[:, :, :], small_raw[:, :, :], small_hi[:, :, :].bitcast(F32), ALU.subtract
                                  ).then_inc(w["small"], 1)
                dve.wait_ge(w["a"], 1)

            def w_low(m):
                dve.wait_ge(w["hi"], m + 1)
                dve.tensor_tensor(c_lo[:, :, c_columns(m)], w_raw[:, m % 2, :, :], c_hi[:, :, c_columns(m)].bitcast(F32),
                                  ALU.subtract).then_inc(w["split"], 1)

            def z_gated(t, half):
                dve.wait_ge(zz["tanh"], HB * t + half + 1)
                cols = slice(half * BANK, (half + 1) * BANK)
                dve.scalar_tensor_tensor(z_silu[:, cols], z_silu[:, cols], 1.0, proj_ps[:, half, :], ALU.add, ALU.mult
                                         ).then_inc(zz["silu"], 1)

            def m_products(t, i):
                for g in range(HPG):
                    dve.wait_ge(sg["exp"], HPG * t + g + 1)
                    dve.tensor_tensor(m_t[:, g * HPG:(g + 1) * HPG, :], l_exp[:, g % 2, :, :],
                                      g_mask[:, i:i + 1, :].to_broadcast([P, HPG, P]), ALU.mult).then_inc(sg["m"], 1)

            def add_out(t, i, b):
                dve.wait_ge(yy["out_ps"], t + 1)
                dve.wait_ge(yy["rs"], t + 1)
                if i == TPB - 1:
                    dve.wait_ge(last_in, 16 * b + 16)
                if i >= 2:
                    dve.wait_ge(y_stored[i - 2], 16 * b + 16)
                elif not (isinstance(b, int) and b == 0):
                    dve.wait_ge(y_stored[i + 2], 16 * b)
                residual = x_last[:, :] if i == TPB - 1 else x[:, i, :]
                dve.scalar_tensor_tensor(y_out[:, i % 2, :], off_ps[:, 0, :], y_rs[:, :], residual, ALU.mult, ALU.add
                                         ).then_inc(yy["x_added"], 1)

            project_batch(0, None)
            dve.wait_ge(out_loaded, 16)
            for f in range(ET):
                dve.tensor_scalar(w_out[:, f, :], w_out[:, f, :], norm_w[:, f:f + 1], float(E) ** 0.5, ALU.mult, ALU.mult
                                  ).then_inc(w["normed"], 1)
            dve.wait_ge(w["z_split"], Z_PIECES)
            m_products(0, 0)
            for half in range(HB):
                z_gated(0, half)

            def off_scaled(t, i, b):
                dve.wait_ge(yy["off_ps"], 3 * b + i)
                dve.tensor_tensor(y[:, :, :], whole(off_ps), heads(decays[:, 1, i, :], SSM_P), ALU.mult).then_inc(yy["off_scaled"], 1)

            def y_gated(t, i, b):
                if i:
                    dve.wait_ge(yy["off_scaled"], 3 * b + i)
                    dve.wait_ge(yy["diag_ps"], t + 1)
                    dve.tensor_tensor(y[:, :, :], y[:, :, :], whole(y_ps), ALU.add).then_inc(yy["diag_added"], 1)
                    dve.wait_ge(yy["diag_added"], 3 * b + i)
                    dve.wait_ge(hh["skip"], t + 1)
                    dve.tensor_tensor(y[:, :, :], y[:, :, :], h_tok[:, :, :], ALU.add).then_inc(yy["skip_added"], 1)
                else:
                    dve.wait_ge(yy["diag_ps"], t + 1)
                    dve.wait_ge(hh["skip"], t + 1)
                    dve.tensor_tensor(y[:, :, :], h_tok[:, :, :], whole(y_ps), ALU.add).then_inc(yy["skip_added"], 1)
                dve.wait_ge(yy["skip_added"], t + 1)
                dve.wait_ge(zz["silu"], HB * (t + 1))
                dve.tensor_tensor(y[:, :, :], y[:, :, :], z_silu[:, :].rearrange("p (h d) -> p h d", d=SSM_P),
                                  ALU.mult).then_inc(yy["gated"], 1)

            def body(b, last):
                for i in range(TPB):
                    t = b * TPB + i
                    if i < TPB - 1 or last:
                        if i:
                            off_scaled(t, i, b)
                        y_gated(t, i, b)
                    else:
                        off_scaled(t, i, b)
                        low_part(b + 1, 0)
                        low_part(b + 1, 1)
                        pair_stats(b + 1, 1)
                    if i < TPB - 1:
                        m_products(t + 1, i + 1)
                        dve.wait_ge(st["ps"], 3 * b + i + 1)
                        src = off_ps[0:SSM_N, :, :].rearrange("p b n -> p (b n)").rearrange("p (h d) -> p h d", d=SSM_P)
                        if i == 0:
                            dve.tensor_copy(state[:, :, :], src).then_inc(st["ready"], 1)
                        else:
                            dve.wait_ge(st["scaled"], 2 * b + i)
                            dve.tensor_tensor(state[:, :, :], state[:, :, :], src, ALU.add).then_inc(st["ready"], 1)
                        if i == TPB - 2 and not last:
                            pair_stats(b + 1, 0)
                        for half in range(HB):
                            z_gated(t + 1, half)
                        if i == TPB - 2 and not last:
                            pair_normed(b + 1, 0, 0)
                            pair_normed(b + 1, 0, 1)
                        add_out(t, i, b)
                    elif last:
                        add_out(t, i, b)
                    else:
                        project_batch(b + 1, t)
                        m_products(t + 1, 0)
                        for half in range(HB):
                            z_gated(t + 1, half)

            with dve.Fori(0, BATCHES - 1) as b:
                body(b, False)
            body(BATCHES - 1, True)


def ssm_tables():
    import numpy as np

    i = np.arange(P)
    e = np.arange(EXPERTS)
    f = np.float32
    return {
        "ident": np.eye(P, dtype=f),
        "upto": (i[:, None] <= i[None, :]).astype(f),
        "after": (i[:, None] > i[None, :]).astype(f),
        "ones": np.ones((P, P), f),
        "earlier": (e[None, :] < e[:, None]).astype(f),
    }


def model_kernel(nc, ins, out):
    x_parts = nc.dram_tensor("x_parts", (2, TILES + 2, P, D), F32, kind="Internal").ap()
    after_attention0 = nc.dram_tensor("after_attention0", (TILES, P, D), F32, kind="Internal").ap()
    after_layer0 = nc.dram_tensor("after_layer0", (TILES, P, D), F32, kind="Internal").ap()
    after_attention1 = nc.dram_tensor("after_attention1", (TILES, P, D), F32, kind="Internal").ap()
    expert_weights = nc.dram_tensor("expert_weights", (P, TILES, EXPERTS + SHARED_GROUPS), F32, kind="Internal").ap()

    def named(prefix, labels):
        return {label: ins[f"{prefix}_{label}"] for label in labels.split()}

    linear_attention_phase(nc, ins["x"], named("a0", "qkvo g1 g2 norm_w"),
                           named("t0", "ident cos sin decay decay_q decay_k same_head chunk_decay"),
                           x_parts, after_attention0)
    fp4 = named("f0", "scales shift")
    fp4["resid"] = after_attention0
    swiglu_phase(nc, "f0", x_parts, ins["f0_words"], None, FP4_GROUPS, (3, 2), None, fp4, after_layer0)
    ssm_phase(nc, after_layer0, named("a1", "in_proj small conv_w conv_b dt_bias a_log skip_d norm_w out_proj"),
              named("t1", "ident upto after ones earlier"), x_parts, after_attention1, expert_weights)
    routed = {"weights": expert_weights, "columns": EXPERTS + SHARED_GROUPS, "start": after_attention1,
              "weights_turned": nc.dram_tensor("weights_turned", (EXPERTS + SHARED_GROUPS, TILES * P), F32, kind="Internal").ap(),
              "ident": ins["t1_ident"]}
    swiglu_phase(nc, "f1", x_parts, ins["f1_up"], ins["f1_down"], MOE_GROUPS, (2, 3), routed, None, out)


def rows_on_partitions(w):
    return w.reshape(-1, P, w.shape[-1]).transpose(1, 0, 2)


def lay_attention0(wq, wk, wv, wo, wg1, wg2, norm_weight):
    import numpy as np

    return {
        "a0_qkvo": np.stack([rows_on_partitions(w).reshape(P, KT * D) for w in (wq, wk, wv, wo)]),
        "a0_g1": rows_on_partitions(wg1),
        "a0_g2": wg2,
        "a0_norm_w": norm_weight.reshape(KT, P).T,
    }


def in_groups(w):
    import numpy as np

    pad = np.zeros((FP4_GROUPS * GF - w.shape[0],) + w.shape[1:], w.dtype)
    return np.concatenate([w, pad]).reshape((FP4_GROUPS, GF) + w.shape[1:])


def lay_fp4(up_packed, up_scales, down_packed, down_scales):
    import numpy as np

    inter = up_packed.shape[0] // 2
    gate_up = np.stack([in_groups(w) for w in up_packed.reshape(2, inter, -1)])
    words = gate_up.reshape(2, FP4_GROUPS, JT, P, KT, P // 8).transpose(1, 2, 0, 5, 4, 3)
    words = np.repeat(words, 8, axis=3).reshape(FP4_GROUPS, 2 * JT, P, D)
    down = in_groups(np.repeat(down_packed.T, 8, axis=0)).reshape(FP4_GROUPS, JT, P, D)
    up_by = np.stack([in_groups(w) for w in up_scales.T.reshape(2, inter, KT)])
    up_by = up_by.reshape(2, FP4_GROUPS, JT, P, KT).transpose(1, 2, 0, 4, 3).reshape(FP4_GROUPS, 2 * JT, D)
    down_by = np.concatenate([down_scales, np.zeros((FP4_GROUPS * JT - len(down_scales), D), down_scales.dtype)])
    return {
        "f0_words": np.concatenate([words, down], 1),
        "f0_scales": np.concatenate([up_by, down_by.reshape(FP4_GROUPS, JT, D)], 1),
        "f0_shift": (4 * (np.arange(P, dtype=np.int32) % 8)).reshape(P, 1),
    }


def lay_attention1(in_proj_w, conv_w, conv_b, dt_bias, a_log, skip_d, norm_w, out_proj_w, gate_w, shared_gate_w):
    import numpy as np

    w = in_proj_w.T
    wide = rows_on_partitions(w[:, :2 * E + 2 * SSM_N])
    zero = np.zeros((D, 1), np.float32)

    def by_feature_tile(a):
        return a.reshape(CONV_TILES, P, -1).transpose(1, 0, 2)

    return {
        "a1_in_proj": wide.reshape(P, KT, -1, P).transpose(2, 0, 1, 3),
        "a1_small": rows_on_partitions(np.concatenate([w[:, 2 * E + 2 * SSM_N:], gate_w.T, shared_gate_w.T, zero], 1)),
        "a1_conv_w": by_feature_tile(conv_w),
        "a1_conv_b": by_feature_tile(conv_b[:, None])[:, :, 0],
        "a1_dt_bias": dt_bias,
        "a1_a_log": a_log,
        "a1_skip_d": skip_d,
        "a1_norm_w": norm_w.reshape(ET, P).T,
        "a1_out_proj": rows_on_partitions(out_proj_w.T),
    }


def lay_experts(fc1, fc2, proj, shared_fc1, shared_fc2, shared_proj):
    import numpy as np

    whole, pair = EXPERT_FEATURES - REST, 2 * P

    def grouped(expert, shared):
        pairs = [expert[:, :whole].reshape(-1, pair, D), shared[:SHARED_GROUPS * pair].reshape(-1, pair, D),
                 expert[:, whole:].reshape(-1, pair, D)]
        pairs = np.concatenate(pairs)
        pairs = np.concatenate([pairs, np.zeros((len(pairs), GF - pair, D), np.float32)], 1)
        return np.concatenate([pairs, shared[None, SHARED_GROUPS * pair:]])

    up = np.stack([grouped(fc1, shared_fc1), grouped(fc2, shared_fc2)], 1).reshape(-1, 2, JT, P, KT, P)
    return {
        "f1_up": up.transpose(0, 5, 2, 1, 4, 3).reshape(-1, P, JT * 2 * KT * P),
        "f1_down": grouped(proj.transpose(0, 2, 1), shared_proj.T),
    }


def kernel(**inputs):
    import concourse.bacc as bacc
    import numpy as np
    from concourse.bass_utils import run_bass_kernel_spmd

    given = {name: np.asarray(a) for name, a in inputs.items()}

    def take(prefix, labels):
        return [given[f"{prefix}_{label}"] for label in labels.split()]

    x = given["L0_attn_x"]
    arrays = {"x": x.reshape(TILES, P, D)}
    arrays.update(lay_attention0(*take("L0_attn", "Wq Wk Wv Wo Wg1 Wg2 norm_weight")))
    arrays.update(lay_fp4(*take("L0_ffn", "gate_up_packed gate_up_scales down_packed down_scales")))
    arrays.update(lay_attention1(*take("L1_attn", "in_proj_w conv_w conv_b dt_bias A_log D norm_w out_proj_w"),
                                 *take("L1_ffn", "gate_w shared_gate_w")))
    arrays.update(lay_experts(*take("L1_ffn", "expert_fc1 expert_fc2 expert_proj shared_fc1 shared_fc2 shared_proj")))
    arrays.update({f"t0_{label}": table for label, table in attention0_tables().items()})
    arrays.update({f"t1_{label}": table for label, table in ssm_tables().items()})

    nc = bacc.Bacc("TRN2", target_bir_lowering=False, num_devices=1)
    arrays = {name: np.ascontiguousarray(a) for name, a in arrays.items()}
    ins = {name: nc.dram_tensor(f"in_{name}", a.shape, mybir.dt.from_np(a.dtype), kind="ExternalInput").ap()
           for name, a in arrays.items()}
    out = nc.dram_tensor("out", (TILES, P, D), F32, kind="ExternalOutput").ap()
    model_kernel(nc, ins, out)
    result = run_bass_kernel_spmd(nc, [{f"in_{name}": a for name, a in arrays.items()}], core_ids=[0])
    return result.results[0]["out"].reshape(x.shape)
```
